# Optimizing a Trainium2 kernel written in Bass

```python
import numpy as np
import jax
import jax.numpy as jnp

def _softmax(x, axis=-1):
    return jax.nn.softmax(x, axis=axis)

def _gelu(x):
    return jax.nn.gelu(x, approximate=True)

def _silu(x):
    return jax.nn.silu(x)

def _sigmoid(x):
    return jax.nn.sigmoid(x)

def _layernorm(x, axis=-1, eps=1e-05):
    m = jnp.mean(x, axis=axis, keepdims=True)
    v = jnp.var(x, axis=axis, keepdims=True)
    return (x - m) / jnp.sqrt(v + eps)

def _scatter_add(tgt, idx, src, axis=0):
    return tgt.at[idx].add(src)

def _segment_sum(src, seg, n):
    return jax.ops.segment_sum(src, seg, n)
kernel_name = 'mk_gnn_resnorm_d4_gnn_r8_9a860b'

def setup_inputs(seed: int=0):
    np.random.seed(seed)
    _w = jnp.asarray

    def _rec_inputs():
        import jax
        import jax.numpy as jnp
        _gk = jax.random.key(seed)
        x = -0.0003713 + 1 * jax.random.normal(jax.random.fold_in(_gk, 1), (6250, 128), jnp.float32)
        _s = jax.random.randint(jax.random.fold_in(_gk, 2), (50000,), 0, 6250, jnp.int32)
        _d = jax.random.randint(jax.random.fold_in(_gk, 3), (50000,), 0, 6250, jnp.int32)
        _loop = jnp.arange(6250, dtype=jnp.int32)
        src = jnp.concatenate([_s, _d, _loop])
        dst = jnp.concatenate([_d, _s, _loop])
        _o = jnp.argsort(dst, stable=True)
        src = src[_o]
        dst = dst[_o]
        edge_attr_128 = 5.93493e-05 + 1.00006 * jax.random.normal(jax.random.fold_in(_gk, 12), (106250, 128), jnp.float32)
        return (x, src, dst, edge_attr_128)
    x, src, dst, edge_attr_128 = _rec_inputs()

    def _L0_gnn_setup():
        import jax, jax.numpy as jnp
        import numpy as np
        N_NODES = 12500
        N_EDGES = 75000
        H = 128
        key = jax.random.key(seed)
        ks = jax.random.split(key, 8)
        x = jax.random.normal(ks[0], (N_NODES, H), dtype=jnp.float32)
        edge_index = jax.random.randint(ks[1], (2, N_EDGES), 0, N_NODES, dtype=jnp.int64)
        edge_attr = jax.random.normal(ks[2], (N_EDGES, H), dtype=jnp.float32)
        W1 = jax.random.normal(ks[3], (2 * H, 2 * H), dtype=jnp.float32) / np.sqrt(2 * H)
        b1 = jnp.zeros((2 * H,), dtype=jnp.float32)
        gamma = jnp.ones((2 * H,), dtype=jnp.float32)
        beta = jnp.zeros((2 * H,), dtype=jnp.float32)
        prelu_a = jnp.full((1,), 0.25, dtype=jnp.float32)
        W2 = jax.random.normal(ks[4], (2 * H, H), dtype=jnp.float32) / np.sqrt(2 * H)
        b2 = jnp.zeros((H,), dtype=jnp.float32)
        return {'x': x, 'edge_index': edge_index, 'edge_attr': edge_attr, 'W1': W1, 'b1': b1, 'gamma': gamma, 'beta': beta, 'prelu_a': prelu_a, 'W2': W2, 'b2': b2}
    _L0_gnn_all = _L0_gnn_setup()
    _L0_gnn_in = {k: v for k, v in _L0_gnn_all.items() if k in ('W1', 'b1', 'gamma', 'beta', 'prelu_a', 'W2', 'b2')}
    del _L0_gnn_all

    def _L1_gnn_setup():
        import jax, jax.numpy as jnp
        import numpy as np
        K = 3
        ALPHA = 0.5
        key = jax.random.key(seed)
        k1, k2, k3, k4 = jax.random.split(key, 4)
        N, E, D_IN, D_OUT = (6250, 80000, 128, 128)
        h = jax.random.normal(k1, (N, D_IN), dtype=jnp.float32)
        W = jax.random.normal(k2, (D_OUT, D_IN), dtype=jnp.float32) * (1.0 / np.sqrt(D_IN))
        src = jax.random.randint(k3, (E,), 0, N, dtype=jnp.int64)
        dst = jax.random.randint(k4, (E,), 0, N, dtype=jnp.int64)
        return {'h': h, 'W': W, 'src': src, 'dst': dst}
    _L1_gnn_all = _L1_gnn_setup()
    _L1_gnn_in = {k: v for k, v in _L1_gnn_all.items() if k in ('W',)}
    del _L1_gnn_all

    def _L2_gnn_setup():
        import jax, jax.numpy as jnp
        import numpy as np
        N, E, D, H = (6250, 100000, 128, 8)
        HD = D // H
        key = jax.random.key(seed)
        ks = jax.random.split(key, 9)
        x = jax.random.normal(ks[0], (N, D), dtype=jnp.float32)
        edge_index = jax.random.randint(ks[1], (2, E), 0, N, dtype=jnp.int64)
        s = 0.05
        Wq = jax.random.normal(ks[2], (D, D), dtype=jnp.float32) * s
        bq = jax.random.normal(ks[3], (D,), dtype=jnp.float32) * s
        Wk = jax.random.normal(ks[4], (D, D), dtype=jnp.float32) * s
        bk = jax.random.normal(ks[5], (D,), dtype=jnp.float32) * s
        Wv = jax.random.normal(ks[6], (D, D), dtype=jnp.float32) * s
        bv = jax.random.normal(ks[7], (D,), dtype=jnp.float32) * s
        return {'x': x, 'Wq': Wq, 'bq': bq, 'Wk': Wk, 'bk': bk, 'Wv': Wv, 'bv': bv, 'edge_index': edge_index}
    _L2_gnn_all = _L2_gnn_setup()
    _L2_gnn_in = {k: v for k, v in _L2_gnn_all.items() if k in ('Wq', 'bq', 'Wk', 'bk', 'Wv', 'bv')}
    del _L2_gnn_all

    def _L3_gnn_setup():
        import jax, jax.numpy as jnp
        import numpy as np
        N, E = (1250, 80000)
        IN_DIM, EDGE_DIM, OUT_DIM = (128, 128, 128)
        key = jax.random.key(seed)
        ks = jax.random.split(key, 9)
        s = 0.02
        return {'x': jax.random.normal(ks[0], (N, IN_DIM), dtype=jnp.float32), 'edge_index': jax.random.randint(ks[1], (2, E), 0, N, dtype=jnp.int64), 'edge_attr': jax.random.normal(ks[2], (E, EDGE_DIM), dtype=jnp.float32), 'We': jax.random.normal(ks[3], (EDGE_DIM, IN_DIM), dtype=jnp.float32) * s, 'be': jnp.zeros((IN_DIM,), dtype=jnp.float32), 'W1': jax.random.normal(ks[4], (2 * IN_DIM, OUT_DIM), dtype=jnp.float32) * s, 'b1': jnp.zeros((OUT_DIM,), dtype=jnp.float32), 'W2': jax.random.normal(ks[5], (OUT_DIM, OUT_DIM), dtype=jnp.float32) * s, 'b2': jnp.zeros((OUT_DIM,), dtype=jnp.float32)}
    _L3_gnn_all = _L3_gnn_setup()
    _L3_gnn_in = {k: v for k, v in _L3_gnn_all.items() if k in ('We', 'be', 'W1', 'b1', 'W2', 'b2')}
    del _L3_gnn_all
    return {'x': x, 'src': src, 'dst': dst, 'edge_attr_128': edge_attr_128, 'L0_gnn_W1': _L0_gnn_in['W1'], 'L0_gnn_b1': _L0_gnn_in['b1'], 'L0_gnn_gamma': _L0_gnn_in['gamma'], 'L0_gnn_beta': _L0_gnn_in['beta'], 'L0_gnn_prelu_a': _L0_gnn_in['prelu_a'], 'L0_gnn_W2': _L0_gnn_in['W2'], 'L0_gnn_b2': _L0_gnn_in['b2'], 'L1_gnn_W': _L1_gnn_in['W'], 'L2_gnn_Wq': _L2_gnn_in['Wq'], 'L2_gnn_bq': _L2_gnn_in['bq'], 'L2_gnn_Wk': _L2_gnn_in['Wk'], 'L2_gnn_bk': _L2_gnn_in['bk'], 'L2_gnn_Wv': _L2_gnn_in['Wv'], 'L2_gnn_bv': _L2_gnn_in['bv'], 'L3_gnn_We': _L3_gnn_in['We'], 'L3_gnn_be': _L3_gnn_in['be'], 'L3_gnn_W1': _L3_gnn_in['W1'], 'L3_gnn_b1': _L3_gnn_in['b1'], 'L3_gnn_W2': _L3_gnn_in['W2'], 'L3_gnn_b2': _L3_gnn_in['b2']}

def reference(x, src, dst, edge_attr_128, L0_gnn_W1, L0_gnn_b1, L0_gnn_gamma, L0_gnn_beta, L0_gnn_prelu_a, L0_gnn_W2, L0_gnn_b2, L1_gnn_W, L2_gnn_Wq, L2_gnn_bq, L2_gnn_Wk, L2_gnn_bk, L2_gnn_Wv, L2_gnn_bv, L3_gnn_We, L3_gnn_be, L3_gnn_W1, L3_gnn_b1, L3_gnn_W2, L3_gnn_b2):
    import jax
    import jax.numpy as jnp

    def _L0_gnn_ref(x, edge_index, edge_attr, W1, b1, gamma, beta, prelu_a, W2, b2):
        import jax, jax.numpy as jnp
        import numpy as np
        N_NODES = 12500
        N_EDGES = 75000
        H = 128
        n = x.shape[0]
        col = edge_index[1]
        summed = jax.ops.segment_sum(edge_attr, col, num_segments=n)
        cnt = jax.ops.segment_sum(jnp.ones((edge_attr.shape[0],), edge_attr.dtype), col, num_segments=n)
        agg = summed / jnp.maximum(cnt, 1.0)[:, None]
        h = jnp.concatenate([x, agg], axis=1)
        h = h @ W1 + b1
        mu = jnp.mean(h, axis=-1, keepdims=True)
        var = jnp.mean(jnp.square(h - mu), axis=-1, keepdims=True)
        h = (h - mu) * jax.lax.rsqrt(var + 1e-05) * gamma + beta
        h = jnp.where(h >= 0, h, prelu_a[0] * h)
        return h @ W2 + b2

    def _L1_gnn_ref(h, W, src, dst):
        import jax, jax.numpy as jnp
        import numpy as np
        K = 3
        ALPHA = 0.5
        N = h.shape[0]
        ones = jnp.ones(src.shape[0], dtype=h.dtype)
        out_deg = jax.ops.segment_sum(ones, src, num_segments=N)
        in_deg = jax.ops.segment_sum(ones, dst, num_segments=N)
        norm_out = jnp.clip(out_deg, 1.0, None) ** (-0.5)
        norm_in = jnp.clip(in_deg, 1.0, None) ** (-0.5)
        h0 = h
        x = h
        for _ in range(K):
            msg = (x * norm_out[:, None])[src]
            agg = jax.ops.segment_sum(msg, dst, num_segments=N)
            x = (1.0 - ALPHA) * (agg * norm_in[:, None]) + ALPHA * h0
        return x @ W.T

    def _L2_gnn_ref(x, Wq, bq, Wk, bk, Wv, bv, edge_index):
        import jax, jax.numpy as jnp
        import numpy as np
        N, E, D, H = (6250, 100000, 128, 8)
        HD = D // H
        n = x.shape[0]
        Q = (x @ Wq.T + bq).reshape(n, H, HD)
        K = (x @ Wk.T + bk).reshape(n, H, HD)
        V = (x @ Wv.T + bv).reshape(n, H, HD)
        src, dst = (edge_index[0], edge_index[1])
        score = jnp.sum(K[src] * Q[dst], axis=-1, keepdims=True) / np.sqrt(HD)
        score = jnp.exp(jnp.clip(score, -5.0, 5.0))
        msg = V[src] * score
        wV = jax.ops.segment_sum(msg, dst, num_segments=n)
        Z = jax.ops.segment_sum(score, dst, num_segments=n)
        h_out = wV / (Z + 1e-06)
        return h_out.reshape(n, H * HD)

    def _L3_gnn_ref(x, edge_index, edge_attr, We, be, W1, b1, W2, b2):
        import jax, jax.numpy as jnp
        import numpy as np
        N, E = (1250, 80000)
        IN_DIM, EDGE_DIM, OUT_DIM = (128, 128, 128)
        src, dst = (edge_index[0], edge_index[1])
        num_nodes = x.shape[0]
        edge_emb = edge_attr @ We + be
        edge_agg = jax.ops.segment_sum(edge_emb, dst, num_segments=num_nodes)
        x_comb = jnp.concatenate([x, edge_agg], axis=-1)
        neigh = jax.ops.segment_sum(x_comb[src], dst, num_segments=num_nodes)
        h = x_comb + neigh
        return jax.nn.relu(h @ W1 + b1) @ W2 + b2
    edge_index = jnp.stack([src, dst])
    x = _layernorm(x + _L0_gnn_ref(x, edge_index, edge_attr_128, L0_gnn_W1, L0_gnn_b1, L0_gnn_gamma, L0_gnn_beta, L0_gnn_prelu_a, L0_gnn_W2, L0_gnn_b2), axis=-1)
    x = _layernorm(x + _L1_gnn_ref(x, L1_gnn_W, src, dst), axis=-1)
    x = _layernorm(x + _L2_gnn_ref(x, L2_gnn_Wq, L2_gnn_bq, L2_gnn_Wk, L2_gnn_bk, L2_gnn_Wv, L2_gnn_bv, edge_index), axis=-1)
    x = _layernorm(x + _L3_gnn_ref(x, edge_index, edge_attr_128, L3_gnn_We, L3_gnn_be, L3_gnn_W1, L3_gnn_b1, L3_gnn_W2, L3_gnn_b2), axis=-1)
    return x

_drawn_inputs = setup_inputs


def setup_inputs(seed=0):
    import zlib

    import numpy as np

    out = dict(_drawn_inputs(seed))
    spreads = {'L0_gnn_b1': (0.0, 0.1),
     'L0_gnn_gamma': (1.0, 0.2),
     'L0_gnn_beta': (0.0, 0.1),
     'L0_gnn_b2': (0.0, 0.1),
     'L3_gnn_be': (0.0, 0.1),
     'L3_gnn_b1': (0.0, 0.576),
     'L3_gnn_b2': (0.0, 0.1)}
    factors = {'L2_gnn_bq': 8.0, 'L2_gnn_bk': 8.0}
    for name, (base, spread) in spreads.items():
        noise = np.random.default_rng([zlib.crc32(name.encode()), seed]).standard_normal(out[name].shape)
        drawn = base * np.exp(spread * noise) if base else spread * noise
        out[name] = jnp.asarray(drawn.astype(out[name].dtype))
    for name, factor in factors.items():
        out[name] = (out[name] * factor).astype(out[name].dtype)
    return out
```

```python
import concourse.bass as bass
from concourse import mybir
from contextlib import ExitStack

N, E, D = 6250, 106250, 128
P = 128
NW = -(-N // P)
NPAD = NW * P
LAST = N - (NW - 1) * P
K = 19
CHUNK = K * P
H = 8
HD = D // H
D2 = 2 * D
EP, EJ = 125, 850
HJ = 34
HSTEPS = EJ // HJ
GROUPS = [(a, min(a + 4, K)) for a in range(0, K, 4)]
NG = len(GROUPS)
CREDIT = 2
L1_STEPS = 3

F32, I32 = mybir.dt.float32, mybir.dt.int32
ALU = mybir.AluOpType
ACT = mybir.ActivationFunctionType
AXX = mybir.AxisListType.X


class Chain:

    def __init__(self, eng, sem, n, spare=None):
        self.eng, self.sem, self.n, self.base, self.j = eng, sem, n, 0, 0
        self.spare = spare

    def start(self, window):
        self.base, self.j = window * self.n, 0

    def __call__(self, ins):
        self.j += 1
        ins.then_inc(self.sem, 1)
        self.eng.wait_ge(self.sem, self.base + self.j)

    def held(self, ins):
        self(ins)
        self.eng.sem_inc(self.spare, 1)

    def end(self):
        assert self.j == self.n, (self.j, self.n)


def windows(eng, phase, body):
    g0 = phase * NW
    with eng.Fori(0, NW // 2) as i:
        for h in range(2):
            body(i * 2 + h, i * 2 + (g0 + h), (g0 + h) % 2, i + (g0 + h) // 2)
    w = NW - 1
    body(w, g0 + w, (g0 + w) % 2, (g0 + w) // 2)


def build(nc, A, out):
    ctx = ExitStack()
    with ctx:
        def sb(name, shape, dt=F32):
            return ctx.enter_context(nc.sbuf_tensor(name, shape, dt))

        def sem(name):
            return ctx.enter_context(nc.semaphore(name))

        def dram(name, shape):
            return nc.dram_tensor(name, shape, F32).ap()

        ctx.enter_context(nc.allow_non_contiguous_dma(reason="small columns of biases, once"))

        z_tab = [dram(f"z_tab{j}", (NPAD, D)) for j in range(L1_STEPS)]
        kv_tab = dram("kv_tab", (NPAD, D2))
        y_tab = dram("y_tab", (NPAD, D))
        tables = [*z_tab, kv_tab, y_tab]

        X = sb("X", [P, NW, D])
        Q = sb("Q", [P, NW, D])
        ST = sb("ST", [P, NW, P])
        src_all = sb("src_all", [P, NW, K], I32)
        dst_all = sb("dst_all", [P, NW, K], I32)
        dloc = sb("dloc", [P, NW, K])
        idx_cur = sb("idx_cur", [P, 2, K], I32)
        rows = sb("rows", [P, 2, K * D2])
        oh = sb("oh", [P, 2, K, P])
        ohT = sb("ohT", [P, 2, 4, P])
        store = sb("store", [P, 2, D2])
        iota_f = sb("iota_f", [P, P])
        ident = sb("ident", [P, P])
        wbase = sb("wbase", [P, NW + 1])
        ones = sb("ones", [P, P])
        indeg = sb("indeg", [P, NW])
        inv_cnt = sb("inv_cnt", [P, NW])
        nin_half = sb("nin_half", [P, NW])
        nout = sb("nout", [P, NW])
        outdeg = sb("outdeg", [P, NW])
        first_i = sb("first_i", [P, NW + 1], I32)
        first_f = sb("first_f", [P, NW + 1])
        below = sb("below", [P, NW + 1])
        eps_t = sb("eps_t", [P, 1])
        dst_flat = sb("dst_flat", [EP, EJ], I32)
        src_flat = sb("src_flat", [EP, EJ], I32)
        src_hi = sb("src_hi", [EP, EJ], I32)
        src_lo_f = sb("src_lo_f", [EP, EJ])
        src_hi_f = sb("src_hi_f", [EP, EJ])
        w1a = sb("w1a", [P, D2]); w1b = sb("w1b", [P, D2])
        w2a = sb("w2a", [P, D]); w2b = sb("w2b", [P, D])
        b1 = sb("b1", [P, D2]); gamma = sb("gamma", [P, D2]); beta = sb("beta", [P, D2])
        alpha = sb("alpha", [P, 1]); b2 = sb("b2", [P, D])
        wraw = sb("wraw", [P, 5, D])
        wT = sb("wT", [P, 5, D])
        bqkv = sb("bqkv", [P, 3 * D])
        l3_w1a = sb("l3_w1a", [P, D]); l3_w1b = sb("l3_w1b", [P, D]); l3_w2 = sb("l3_w2", [P, D])
        be_col = sb("be_col", [P, 1]); be_bc = sb("be_bc", [P, P])
        l3_b1 = sb("l3_b1", [P, D]); l3_b2 = sb("l3_b2", [P, D])
        l3_m = sb("l3_m", [P, D]); l3_v = sb("l3_v", [P, D])
        xs = sb("xs", [P, D])
        xT = sb("xT", [P, P]); sT = sb("sT", [P, P])
        hbuf = sb("hbuf", [P, D2]); hneg = sb("hneg", [P, D2]); hT = sb("hT", [P, 2, P])
        stats = sb("stats", [P, 6]); mv = sb("mv", [P, 2]); std = sb("std", [P, 1]); rstd = sb("rstd", [P, 1])
        yb = sb("yb", [P, D]); zr = sb("zr", [P, H])
        sc = sb("sc", [P, K, H])
        hlo = rows[:, 0, 0:HJ * P].rearrange("p (j n) -> p j n", n=P)
        hhi = rows[:, 1, 0:HJ * NW].rearrange("p (j n) -> p j n", n=NW)

        def pb(name, shape):
            return ctx.enter_context(nc.psum_tensor(name, shape, F32))
        acc = [pb(f"acc{i}", [P, 512]) for i in range(2)]
        psT = [pb(f"psT{i}", [P, 512]) for i in range(2)]
        psQ = [pb(f"psQ{i}", [P, 512]) for i in range(2)]
        psA = pb("psA", [P, 512]); psB = pb("psB", [P, 512])

        s_const = sem("const_ready"); s_in = sem("inputs_loaded"); s_edges = sem("edges_loaded")
        s_wT = sem("weights_transposed"); s_wc = sem("weights_copied"); s_fold = sem("l3_folded"); s_foldc = sem("l3_fold_copied")
        s_off = sem("offsets_summed"); s_offc = sem("offsets_ready"); s_below = sem("below_counted")
        s_hoh = sem("hist_onehots"); s_hmm = sem("hist_products"); s_deg = sem("outdeg_ready")
        s_win = sem("window_indices_loaded"); s_winr = sem("window_indices_ready")
        s_ea = [sem(f"edge_rows_loaded{i}") for i in range(2)]
        s_setup = sem("dve_setup"); s_spare = sem("carries_a_wait"); s_dve = sem("dve_step"); s_nodes = sem("node_weights_ready"); s_sqrt = sem("sqrt_ready")
        s_idx = sem("gather_indices_ready"); s_gat = [sem(f"rows_gathered{i}") for i in range(2)]
        s_oh = sem("onehot_ready"); s_agg = sem("aggregated"); s_accr = sem("acc_read")
        s_store = sem("rows_to_store"); s_stored = sem("rows_stored"); s_free = sem("store_buffer_free")
        s_l0x = sem("l0_x_copied"); s_tp = sem("pe_transposed"); s_tc = sem("transposes_copied")
        s_mm = sem("pe_product_ready"); s_var = sem("variance_ready"); s_std = sem("std_ready")
        s_h = sem("layer_hidden_ready"); s_xn = sem("x_new_ready")
        s_qT = sem("onehots_transposed"); s_qTc = sem("onehotT_copied"); s_qe = sem("queries_expanded")
        s_qer = sem("queries_read"); s_sc = sem("scores_ready"); s_exp = sem("exp_ready"); s_msg = sem("messages_ready")

        def bc_row(v, n):
            return v.rearrange("(a n) -> a n", a=1).to_broadcast([P, n])

        LOADS = [(w1a[:, :], A["L0_gnn_W1"][0:P, :]), (w1b[:, :], A["L0_gnn_W1"][P:2 * P, :]),
                 (w2a[:, :], A["L0_gnn_W2"][0:P, :]), (w2b[:, :], A["L0_gnn_W2"][P:2 * P, :]),
                 (b1[:, :], bc_row(A["L0_gnn_b1"], D2)), (gamma[:, :], bc_row(A["L0_gnn_gamma"], D2)),
                 (beta[:, :], bc_row(A["L0_gnn_beta"], D2)), (alpha[:, :], bc_row(A["L0_gnn_prelu_a"], 1)),
                 (b2[:, :], bc_row(A["L0_gnn_b2"], D)),
                 (wraw[:, 0, :], A["L1_gnn_W"]), (wraw[:, 1, :], A["L2_gnn_Wq"]), (wraw[:, 2, :], A["L2_gnn_Wk"]),
                 (wraw[:, 3, :], A["L2_gnn_Wv"]), (wraw[:, 4, :], A["L3_gnn_We"]),
                 (bqkv[:, 0:D], bc_row(A["L2_gnn_bq"], D)), (bqkv[:, D:2 * D], bc_row(A["L2_gnn_bk"], D)),
                 (bqkv[:, 2 * D:3 * D], bc_row(A["L2_gnn_bv"], D)),
                 (l3_w1a[:, :], A["L3_gnn_W1"][0:P, :]), (l3_w1b[:, :], A["L3_gnn_W1"][P:2 * P, :]),
                 (l3_w2[:, :], A["L3_gnn_W2"]), (be_col[:, :], A["L3_gnn_be"].rearrange("(p a) -> p a", a=1)),
                 (l3_b1[:, :], bc_row(A["L3_gnn_b1"], D)), (l3_b2[:, :], bc_row(A["L3_gnn_b2"], D)),
                 *[(X[:, w:w + 6, :], A["x"][w * P:(w + 6) * P, :].rearrange("(w p) d -> p w d", p=P))
                   for w in range(0, NW - 1, 6)],
                 (X[0:LAST, NW - 1, :], A["x"][(NW - 1) * P:N, :])]

        block = ctx.enter_context(nc.Block())

        @block.sync
        def _(sp):
            sp.sem_inc(s_free, CREDIT)
            sp.dma_start(dst_flat[:, :], A["dst"].rearrange("(p j) -> p j", p=EP)).then_inc(s_edges, 16)
            sp.dma_start(src_flat[:, :], A["src"].rearrange("(p j) -> p j", p=EP)).then_inc(s_edges, 16)
            sp.wait_ge(s_const, 4)
            for dst_ap, src_ap in LOADS:
                sp.dma_start(dst_ap, src_ap).then_inc(s_in, 16)
            sp.wait_ge(s_offc, 1)

            def load_window(w, G, par, use):
                first = sp.value_load(first_i[0:1, bass.ds(w, 1)], min_val=0, max_val=E - CHUNK)
                for dst_ap, name in ((src_all, "src"), (dst_all, "dst")):
                    sp.dma_start(dst_ap[:, bass.ds(w, 1), :].rearrange("p a k -> p (a k)"),
                                 A[name][bass.ds(first, CHUNK)].rearrange("(p k) -> p k", p=P)).then_inc(s_win, 16)
                sp.wait_ge(s_win, (w + 1) * 32)
                sp.sem_inc(s_winr, 1)
            windows(sp, 0, load_window)

            def storing(phase, table, width):
                def store_window(w, G, par, use):
                    sp.wait_ge(s_store, G + 1)
                    sp.dma_start(table[bass.ds(w * P, P), :], store[:, par, 0:width]).then_inc(s_stored, 16)
                    sp.wait_ge(s_stored, (G + 1) * 16)
                    sp.sem_inc(s_free, 1)
                windows(sp, phase, store_window)
            for j in range(L1_STEPS):
                storing(j, z_tab[j], D)
            storing(3, kv_tab, D2)
            storing(4, y_tab, D)

            def store_out(w, G, par, use):
                last = isinstance(w, int) and w == NW - 1
                n = LAST if last else P
                dst_ap = out[w * P:w * P + n, :] if last else out[bass.ds(w * P, P), :]
                sp.wait_ge(s_store, G + 1)
                sp.dma_start(dst_ap, store[0:n, par, 0:D]).then_inc(s_stored, 16)
                sp.wait_ge(s_stored, (G + 1) * 16)
                sp.sem_inc(s_free, 1)
            windows(sp, 5, store_out)

        @block.gpsimd
        def _(pool):
            nc.gpsimd.memset(X[:, NW - 1, :], 0.0).then_inc(s_const, 1)
            nc.gpsimd.memset(ident[:, :], 0.0).then_inc(s_const, 1)
            nc.gpsimd.iota(iota_f[:, :], pattern=[[1, P]], base=0, channel_multiplier=0,
                           allow_small_or_imprecise_dtypes=True).then_inc(s_const, 1)
            nc.gpsimd.iota(wbase[:, :], pattern=[[P, NW + 1]], base=0, channel_multiplier=0,
                           allow_small_or_imprecise_dtypes=True).then_inc(s_const, 1)
            pool.wait_ge(s_const, 4)
            nc.gpsimd.affine_select(out=ident[:, :], in_=ident[:, :], compare_op=ALU.not_equal, fill=1.0,
                                    base=0, pattern=[[-1, P]], channel_multiplier=1).then_inc(s_const, 1)

            def gathering(phase, table, width):
                pool.wait_ge(s_free, (phase + 1) * NW + CREDIT)

                def gather_window(w, G, par, use):
                    pool.wait_ge(s_idx, G + 1)
                    pool.sem_inc(s_const, 1)
                    for k in range(K):
                        pool.indirect_dma_start(rows[:, par, k * width:(k + 1) * width], None, table,
                                                bass.IndirectOffsetOnAxis(ap=idx_cur[:, par, k:k + 1], axis=0)
                                                ).then_inc(s_gat[par], 16)
                windows(pool, phase, gather_window)
            for phase, table in enumerate(tables):
                gathering(phase, table, D2 if phase == 3 else D)

        @block.scalar
        def _(act):
            act.wait_ge(s_wT, 1)
            nc.scalar.copy(wT[:, 0:4, :].rearrange("p a d -> p (a d)"), psT[0][:, :]).then_inc(s_wc, 1)
            nc.scalar.copy(wT[:, 4, :], psT[1][:, 0:D]).then_inc(s_wc, 1)
            act.wait_ge(s_deg, 1)
            nc.scalar.activation(nout[:, :], outdeg[:, :], ACT.Sqrt).then_inc(s_sqrt, 1)
            act.wait_ge(s_fold, 1)
            nc.scalar.copy(l3_m[:, :], psA[:, 0:D]).then_inc(s_foldc, 1)
            nc.scalar.copy(l3_v[:, :], psA[:, D:2 * D]).then_inc(s_foldc, 1)

            act.wait_ge(s_offc, 1)
            act.wait_ge(s_hmm, HSTEPS)

            def edge_load(w, G, par, use):
                act.wait_ge(s_agg, w + 1)
                first = act.value_load(first_i[0:1, bass.ds(w, 1)], min_val=0, max_val=E - CHUNK)
                act.dma_start(rows[:, par, 0:K * D],
                              A["edge_attr_128"][bass.ds(first, CHUNK), :].rearrange("(p k) d -> p (k d)", p=P)
                              ).then_inc(s_ea[par], 16)

            TP0, TC0, MM0, VAR0 = 3 * NW, 4 * NW, 2 * NW, 2 * NW

            def std_of(n):
                act.wait_ge(s_var, n)
                nc.scalar.activation(std[:, :], mv[:, 1:2], ACT.Sqrt, bias=eps_t[:, :]).then_inc(s_std, 1)

            def l0_steps(w, G, par, use):
                edge_load(w, G, par, use)
                nc.scalar.copy(xs[:, :], X[:, bass.ds(w, 1), :].rearrange("p a d -> p (a d)")).then_inc(s_l0x, 1)
                act.wait_ge(s_tp, 3 * w + 1)
                nc.scalar.copy(xT[:, :], psT[0][:, 0:P]).then_inc(s_tc, 1)
                act.wait_ge(s_agg, w + 1 + CREDIT)
                nc.scalar.copy(sT[:, :], acc[par][:, 0:P]).then_inc(s_tc, 1)
                nc.scalar.copy(ST[:, bass.ds(w, 1), :].rearrange("p a d -> p (a d)"), acc[par][:, 0:P]).then_inc(s_tc, 1)
                std_of(2 * w + 1)
                act.wait_ge(s_tp, 3 * w + 3)
                nc.scalar.copy(hT[:, :, :].rearrange("p a d -> p (a d)"), psT[1][:, 0:D2]).then_inc(s_tc, 1)
                std_of(2 * w + 2)
            act.wait_ge(s_in, 16 * len(LOADS))
            windows(act, 0, l0_steps)
            act.wait_ge(s_nodes, 1)
            nc.scalar.activation(nin_half[:, :], inv_cnt[:, :], ACT.Sqrt).then_inc(s_sqrt, 1)

            def indices(w, G, par):
                act.wait_ge(s_agg, G + NW + 1)
                nc.scalar.copy(idx_cur[:, par, :], src_all[:, bass.ds(w, 1), :].rearrange("p a k -> p (a k)")
                               ).then_inc(s_idx, 1)

            def ahead(phase, body):
                indices(0, phase * NW, (phase * NW) % 2)

                def step(w, G, par, use):
                    if not (isinstance(w, int) and w == NW - 1):
                        indices(w + 1, G + 1, 1 - par)
                    if body is not None:
                        body(w, G, par, use)
                windows(act, phase, step)
            ahead(0, None)
            ahead(1, None)

            def l1_last(w, G, par, use):
                act.wait_ge(s_tp, TP0 + 2 * w + 1)
                nc.scalar.copy(xT[:, :], psT[0][:, 0:P]).then_inc(s_tc, 1)
                std_of(VAR0 + w + 1)
                act.wait_ge(s_tp, TP0 + 2 * w + 2)
                nc.scalar.copy(xT[:, :], psT[0][:, 0:P]).then_inc(s_tc, 1)
            ahead(2, l1_last)
            TP1, TC1, VAR1 = TP0 + 2 * NW, TC0 + 2 * NW, VAR0 + NW

            def l2(w, G, par, use):
                for g, (a, b) in enumerate(GROUPS):
                    act.wait_ge(s_qT, w * NG + g + 1)
                    if g >= 2:
                        act.wait_ge(s_qe, w * NG + g - 1)
                    nc.scalar.copy(ohT[:, g % 2, 0:b - a, :].rearrange("p k n -> p (k n)"),
                                   psT[g % 2][:, 0:(b - a) * P]).then_inc(s_qTc, 1)
                act.wait_ge(s_sc, w + 1)
                s_at = rows[:, par, :].rearrange("p (k n) -> p k n", n=D2)[:, :, D - H:D]
                nc.scalar.activation(s_at, sc[:, :, :], ACT.Exp, scale=1.0 / HD ** 0.5).then_inc(s_exp, 1)
                std_of(VAR1 + w + 1)
                act.wait_ge(s_tp, TP1 + w + 1)
                nc.scalar.copy(xT[:, :], psA[:, 0:P]).then_inc(s_tc, 1)
                nc.scalar.copy(sT[:, :], ST[:, bass.ds(w, 1), :].rearrange("p a d -> p (a d)")).then_inc(s_tc, 1)
            ahead(3, l2)
            TP2, VAR2 = TP1 + NW, VAR1 + NW

            def l3(w, G, par, use):
                act.wait_ge(s_tp, TP2 + w + 1)
                nc.scalar.copy(xT[:, :], psT[0][:, 0:P]).then_inc(s_tc, 1)
                std_of(VAR2 + w + 1)
            ahead(4, l3)

        TC0, TC1, TC2 = 4 * NW, 6 * NW, 8 * NW
        MM0, MM1, MM2 = 2 * NW, 4 * NW, 5 * NW
        VAR0, VAR1, VAR2 = 2 * NW, 3 * NW, 4 * NW
        TP0, TP1, TP2 = 3 * NW, 5 * NW, 6 * NW

        @block.vector
        def _(dve):
            setup = Chain(dve, s_setup, 0)

            def flat(t, w):
                return t[:, bass.ds(w, 1), :].rearrange("p a d -> p (a d)")

            def onehot(w, par):
                return nc.vector.tensor_tensor(
                    oh[:, par, :, :], flat(dloc, w).unsqueeze(2).to_broadcast([P, K, P]),
                    iota_f[:, :].unsqueeze(1).to_broadcast([P, K, P]), ALU.is_equal)

            setup(nc.vector.memset(ones[:, :], 1.0))
            setup(nc.vector.memset(eps_t[:, :], 1e-5))
            setup(nc.vector.memset(below[:, :], 0.0))
            dve.wait_ge(s_const, 5)
            dve.wait_ge(s_edges, 32)
            scratch = rows[0:EP, 0, 0:EJ]
            for w in range(1, NW):
                setup(nc.vector.tensor_scalar(scratch, dst_flat[:, :], float(P * w), None, ALU.is_lt, ALU.add,
                                        accum_out=below[0:EP, w:w + 1]))
            nc.vector.tensor_scalar(src_hi[:, :], src_flat[:, :], 7, None, ALU.arith_shift_right).then_inc(s_below, 1)
            dve.wait_ge(s_off, 1)
            setup(nc.vector.tensor_scalar(first_f[:, :], psB[:, 0:NW + 1], float(E - CHUNK), None, ALU.min))
            nc.vector.tensor_copy(first_i[:, :], first_f[:, :]).then_inc(s_offc, 1)
            dve.wait_ge(s_below, 1)
            setup(nc.vector.tensor_copy(src_hi_f[:, :], src_hi[:, :]))
            setup(nc.vector.tensor_scalar(src_hi[:, :], src_flat[:, :], P - 1, None, ALU.bitwise_and))
            setup(nc.vector.tensor_copy(src_lo_f[:, :], src_hi[:, :]))
            iota_w = iota_f[0:EP, 0:NW]

            def hist_onehots(col):
                lo = src_lo_f[:, col].unsqueeze(2).to_broadcast([EP, HJ, P])
                hi = src_hi_f[:, col].unsqueeze(2).to_broadcast([EP, HJ, NW])
                nc.vector.tensor_tensor(hlo[0:EP, :, :], lo, iota_f[0:EP, :].unsqueeze(1).to_broadcast([EP, HJ, P]), ALU.is_equal).then_inc(s_hoh, 1)
                nc.vector.tensor_tensor(hhi[0:EP, :, :], hi, iota_w.unsqueeze(1).to_broadcast([EP, HJ, NW]), ALU.is_equal).then_inc(s_hoh, 1)
            hist_onehots(slice(0, HJ))
            with dve.Fori(1, HSTEPS) as i:
                dve.wait_ge(s_hmm, i)
                hist_onehots(bass.ds(i * HJ, HJ))
            dve.wait_ge(s_hmm, HSTEPS)
            nc.vector.tensor_scalar(outdeg[:, :], psA[:, 2 * D:2 * D + NW], 1.0, None, ALU.max).then_inc(s_deg, 1)
            dve.wait_ge(s_sqrt, 1)
            setup(nc.vector.reciprocal(nout[:, :], nout[:, :]))
            dve.wait_ge(s_in, 16 * len(LOADS))
            setup(nc.vector.tensor_copy(be_bc[:, :], be_col[:, :].to_broadcast([P, P])))
            nc.vector.tensor_copy(be_bc[:, :], be_bc[:, :]).then_inc(s_h, 1)

            base = [0]

            def layernorm(link, src, n_var, dst_ap, width=D):
                link.held(nc.vector.bn_stats(stats[:, :], src))
                nc.vector.bn_aggr(mv[:, :], stats[:, :]).then_inc(s_var, 1)
                dve.wait_ge(s_std, n_var)
                link(nc.vector.reciprocal(rstd[:, :], std[:, :]))
                link(nc.vector.tensor_scalar(dst_ap, src, mv[:, 0:1], rstd[:, :], ALU.subtract, ALU.mult))

            link = Chain(dve, s_dve, 18, s_spare)

            def l0(w, G, par, use):
                link.start(w)
                dve.wait_ge(s_winr, w + 1)
                link(nc.vector.tensor_scalar(flat(dloc, w), flat(dst_all, w), wbase[:, bass.ds(w, 1)], None, ALU.subtract))
                dve.wait_ge(s_agg, w + 1)
                onehot(w, par).then_inc(s_oh, 1)
                dve.wait_ge(s_mm, 2 * w + 1)
                link(nc.vector.tensor_scalar(indeg[:, bass.ds(w, 1)], psB[:, 0:1], 0.0, None, ALU.max))
                link(nc.vector.tensor_scalar(zr[:, 0:1], psB[:, 0:1], 1.0, None, ALU.max))
                link(nc.vector.reciprocal(zr[:, 1:2], zr[:, 0:1]))
                link(nc.vector.tensor_scalar(hneg[:, :], psQ[0][:, 0:D2], zr[:, 1:2], None, ALU.mult))
                link(nc.vector.tensor_tensor(hneg[:, :], hneg[:, :], b1[:, :], ALU.add))
                link(nc.vector.tensor_tensor(hbuf[:, :], hneg[:, :], psQ[1][:, 0:D2], ALU.add))
                layernorm(link, hbuf[:, :], 2 * w + 1, hbuf[:, :])
                link(nc.vector.tensor_tensor(hbuf[:, :], hbuf[:, :], gamma[:, :], ALU.mult))
                link(nc.vector.tensor_tensor(hbuf[:, :], hbuf[:, :], beta[:, :], ALU.add))
                link(nc.vector.tensor_scalar(hneg[:, :], hbuf[:, :], 0.0, alpha[:, :], ALU.min, ALU.mult))
                nc.vector.scalar_tensor_tensor(hbuf[:, :], hbuf[:, :], 0.0, hneg[:, :], ALU.max, ALU.add).then_inc(s_h, 1)
                dve.wait_ge(s_mm, 2 * w + 2)
                link(nc.vector.tensor_tensor(yb[:, :], psA[:, 0:D], b2[:, :], ALU.add))
                link(nc.vector.tensor_tensor(yb[:, :], yb[:, :], xs[:, :], ALU.add))
                link.held(nc.vector.bn_stats(stats[:, :], yb[:, :]))
                nc.vector.bn_aggr(mv[:, :], stats[:, :]).then_inc(s_var, 1)
                dve.wait_ge(s_std, 2 * w + 2)
                link(nc.vector.reciprocal(rstd[:, :], std[:, :]))
                link(nc.vector.tensor_scalar(flat(X, w), yb[:, :], mv[:, 0:1], rstd[:, :], ALU.subtract, ALU.mult))
                dve.wait_ge(s_free, G + 1)
                nc.vector.tensor_scalar(store[:, par, 0:D], flat(X, w), nout[:, bass.ds(w, 1)], None, ALU.mult).then_inc(s_store, 1)
                link.end()
            windows(dve, 0, l0)
            s0 = 18 * NW

            link = Chain(dve, s_dve, 0)
            link.base = s0
            link(nc.vector.tensor_scalar(zr[:, 0:1], zr[:, 0:1], 0.0, None, ALU.add))
            link(nc.vector.tensor_scalar(below[:, 0:NW], indeg[:, :], 1.0, None, ALU.max))
            nc.vector.tensor_copy(inv_cnt[:, :], below[:, 0:NW]).then_inc(s_nodes, 1)
            dve.wait_ge(s_sqrt, 2)
            link(nc.vector.reciprocal(inv_cnt[:, :], nin_half[:, :]))
            link(nc.vector.tensor_scalar(nin_half[:, :], inv_cnt[:, :], 0.5, None, ALU.mult))
            s0 += link.j

            def ready(w, G, par):
                dve.wait_ge(s_agg, G + NW + 1)
                onehot(w, par).then_inc(s_oh, 1)

            def store_free(G):
                dve.wait_ge(s_free, G + NW + 1)

            for step in range(L1_STEPS):
                last = step == L1_STEPS - 1
                n = 8 if last else 2
                link = Chain(dve, s_dve, n, s_spare)

                def l1(w, G, par, use, link=link, last=last, s0=s0):
                    link.start(w)
                    link.base = link.base + s0
                    ready(w, G, par)
                    dve.wait_ge(s_agg, G + NW + 1 + CREDIT)
                    link(nc.vector.tensor_scalar(yb[:, :], acc[par][:, 0:D], nin_half[:, bass.ds(w, 1)], None, ALU.mult))
                    nc.vector.sem_inc(s_accr, 1)
                    if not last:
                        link(nc.vector.scalar_tensor_tensor(xs[:, :], flat(X, w), 0.5, yb[:, :], ALU.mult, ALU.add))
                        store_free(G)
                        nc.vector.tensor_scalar(store[:, 1 - par, 0:D], xs[:, :], nout[:, bass.ds(w, 1)], None, ALU.mult).then_inc(s_store, 1)
                        link.end()
                        return
                    nc.vector.scalar_tensor_tensor(xs[:, :], flat(X, w), 0.5, yb[:, :], ALU.mult, ALU.add).then_inc(s_h, 1)
                    dve.wait_ge(s_mm, MM0 + 2 * w + 1)
                    link(nc.vector.tensor_tensor(yb[:, :], psA[:, 0:D], flat(X, w), ALU.add))
                    link.held(nc.vector.bn_stats(stats[:, :], yb[:, :]))
                    nc.vector.bn_aggr(mv[:, :], stats[:, :]).then_inc(s_var, 1)
                    dve.wait_ge(s_std, VAR0 + w + 1)
                    link(nc.vector.reciprocal(rstd[:, :], std[:, :]))
                    nc.vector.tensor_scalar(xs[:, :], yb[:, :], mv[:, 0:1], rstd[:, :], ALU.subtract, ALU.mult).then_inc(s_h, 1)
                    link(nc.vector.tensor_scalar(flat(X, w), yb[:, :], mv[:, 0:1], rstd[:, :], ALU.subtract, ALU.mult))
                    dve.wait_ge(s_mm, MM0 + 2 * w + 2)
                    link(nc.vector.tensor_tensor(flat(Q, w), psB[:, 0:D], bqkv[:, 0:D], ALU.add))
                    store_free(G)
                    link(nc.vector.tensor_copy(zr[:, 0:1], rstd[:, :]))
                    link(nc.vector.tensor_copy(zr[:, 1:2], rstd[:, :]))
                    nc.vector.tensor_tensor(store[:, 1 - par, :], psB[:, D:3 * D], bqkv[:, D:3 * D], ALU.add).then_inc(s_store, 1)
                    link.end()
                windows(dve, step, l1)
                s0 += n * NW

            n2 = 10
            link = Chain(dve, s_dve, n2, s_spare)

            def l2(w, G, par, use, s0=s0):
                link.start(w)
                link.base = link.base + s0
                ready(w, G, par)
                kv = rows[:, par, :].rearrange("p (k n) -> p k n", n=D2)
                dve.wait_ge(s_gat[par], (use + 1) * 16 * K)
                for g, (a, b) in enumerate(GROUPS):
                    q = psQ[g % 2][:, 0:(b - a) * D].rearrange("p (k n) -> p k n", n=D)
                    dve.wait_ge(s_qe, w * NG + g + 1)
                    nc.vector.tensor_tensor(kv[:, a:b, 0:D], kv[:, a:b, 0:D], q, ALU.mult).then_inc(s_qer, 1)
                dve.wait_ge(s_qer, (w + 1) * NG)
                link(nc.vector.tensor_reduce(sc[:, :, :], kv[:, :, 0:D].rearrange("p k (h d) -> p k h d", d=HD), AXX, ALU.add))
                lim = 5.0 * HD ** 0.5
                nc.vector.tensor_scalar(sc[:, :, :], sc[:, :, :], lim, -lim, ALU.min, ALU.max).then_inc(s_sc, 1)
                dve.wait_ge(s_exp, w + 1)
                for g, (a, b) in enumerate(GROUPS):
                    v = kv[:, a:b, D:D2].rearrange("p k (h d) -> p k h d", d=HD)
                    s = kv[:, a:b, D - H:D].unsqueeze(3).to_broadcast([P, b - a, H, HD])
                    nc.vector.tensor_tensor(v, v, s, ALU.mult).then_inc(s_msg, 1)
                dve.wait_ge(s_agg, G + NW + 1 + CREDIT)
                link(nc.vector.tensor_scalar(zr[:, :], acc[par][:, 0:H], 1e-6, None, ALU.add))
                link(nc.vector.reciprocal(zr[:, :], zr[:, :]))
                link(nc.vector.tensor_tensor(yb[:, :].rearrange("p (h d) -> p h d", d=HD),
                                             acc[par][:, H:H + D].rearrange("p (h d) -> p h d", d=HD),
                                             zr[:, :].unsqueeze(2).to_broadcast([P, H, HD]), ALU.mult))
                nc.vector.sem_inc(s_accr, 1)
                link(nc.vector.tensor_tensor(yb[:, :], yb[:, :], flat(X, w), ALU.add))
                link.held(nc.vector.bn_stats(stats[:, :], yb[:, :]))
                nc.vector.bn_aggr(mv[:, :], stats[:, :]).then_inc(s_var, 1)
                dve.wait_ge(s_std, VAR1 + w + 1)
                link(nc.vector.reciprocal(rstd[:, :], std[:, :]))
                nc.vector.tensor_scalar(xs[:, :], yb[:, :], mv[:, 0:1], rstd[:, :], ALU.subtract, ALU.mult).then_inc(s_h, 1)
                link(nc.vector.tensor_scalar(flat(X, w), yb[:, :], mv[:, 0:1], rstd[:, :], ALU.subtract, ALU.mult))
                dve.wait_ge(s_mm, MM1 + w + 1)
                link(nc.vector.tensor_scalar(yb[:, :], l3_v[:, :], indeg[:, bass.ds(w, 1)], None, ALU.mult))
                link(nc.vector.tensor_tensor(flat(Q, w), psB[:, 0:D], yb[:, :], ALU.add))
                store_free(G)
                nc.vector.tensor_tensor(store[:, 1 - par, 0:D], psB[:, 0:D], yb[:, :], ALU.add).then_inc(s_store, 1)
                link.end()
            windows(dve, 3, l2)
            s0 += link.n * NW

            link = Chain(dve, s_dve, 6, s_spare)

            def l3(w, G, par, use, s0=s0):
                link.start(w)
                link.base = link.base + s0
                ready(w, G, par)
                dve.wait_ge(s_agg, G + NW + 1 + CREDIT)
                link(nc.vector.tensor_tensor(yb[:, :], acc[par][:, 0:D], flat(Q, w), ALU.add))
                nc.vector.sem_inc(s_accr, 1)
                link(nc.vector.tensor_tensor(yb[:, :], yb[:, :], l3_b1[:, :], ALU.add))
                nc.vector.tensor_scalar(xs[:, :], yb[:, :], 0.0, None, ALU.max).then_inc(s_h, 1)
                dve.wait_ge(s_mm, MM2 + w + 1)
                link(nc.vector.tensor_tensor(yb[:, :], psA[:, 0:D], l3_b2[:, :], ALU.add))
                link(nc.vector.tensor_tensor(yb[:, :], yb[:, :], flat(X, w), ALU.add))
                link.held(nc.vector.bn_stats(stats[:, :], yb[:, :]))
                nc.vector.bn_aggr(mv[:, :], stats[:, :]).then_inc(s_var, 1)
                dve.wait_ge(s_std, VAR2 + w + 1)
                link(nc.vector.reciprocal(rstd[:, :], std[:, :]))
                store_free(G)
                nc.vector.tensor_scalar(store[:, 1 - par, 0:D], yb[:, :], mv[:, 0:1], rstd[:, :], ALU.subtract, ALU.mult).then_inc(s_store, 1)
                link.end()
            windows(dve, 4, l3)

        @block.tensor
        def _(pe):
            mm = nc.tensor.matmul
            pe.sem_inc(s_agg, CREDIT)
            pe.wait_ge(s_const, 5)
            pe.wait_ge(s_in, 16 * len(LOADS))
            for j in range(4):
                nc.tensor.transpose(psT[0][:, j * P:(j + 1) * P], wraw[:, j, :], ident[:, :])
            nc.tensor.transpose(psT[1][:, 0:P], wraw[:, 4, :], ident[:, :]).then_inc(s_wT, 1)
            pe.wait_ge(s_below, 1)
            mm(psB[:, 0:NW + 1], ones[:, :], below[:, :], start=True, stop=True).then_inc(s_off, 1)
            for step in range(1):
                pe.wait_ge(s_hoh, 2)
                for j in range(HJ):
                    m = mm(psA[:, 2 * D:2 * D + NW], hlo[0:EP, j, :], hhi[0:EP, j, :], start=(j == 0), stop=False, skip_group_check=True)
                m.then_inc(s_hmm, 1)
            with pe.Fori(1, HSTEPS) as i:
                pe.wait_ge(s_hoh, i * 2 + 2)
                for j in range(HJ):
                    m = mm(psA[:, 2 * D:2 * D + NW], hlo[0:EP, j, :], hhi[0:EP, j, :], start=False, stop=(j == HJ - 1), skip_group_check=True)
                m.then_inc(s_hmm, 1)
            pe.wait_ge(s_h, 1)
            pe.wait_ge(s_wc, 2)
            mm(psA[:, 0:D], wT[:, 4, :], l3_w1b[:, :], start=True, stop=True)
            mm(psA[:, D:2 * D], be_bc[:, :], l3_w1b[:, :], start=True, stop=True).then_inc(s_fold, 1)
            pe.wait_ge(s_foldc, 2)

            def l0(w, G, par, use):
                pe.wait_ge(s_l0x, w + 1)
                nc.tensor.transpose(psT[0][:, 0:P], xs[:, :], ident[:, :]).then_inc(s_tp, 1)
                pe.wait_ge(s_oh, w + 1)
                pe.wait_ge(s_ea[par], (use + 1) * 16)
                for k in range(K):
                    ea = rows[:, par, k * D:(k + 1) * D]
                    m = mm(acc[par][:, 0:P], ea, oh[:, par, k, :], start=(k == 0), stop=(k == K - 1))
                for k in range(K):
                    m = mm(psB[:, 0:1], oh[:, par, k, :], ones[:, 0:1], start=(k == 0), stop=(k == K - 1))
                m.then_inc(s_agg, 1)
                pe.wait_ge(s_tc, 4 * w + 3)
                mm(psQ[1][:, 0:D2], xT[:, :], w1a[:, :], start=True, stop=True)
                mm(psQ[0][:, 0:D2], sT[:, :], w1b[:, :], start=True, stop=True).then_inc(s_mm, 1)
                pe.wait_ge(s_h, w + 2)
                nc.tensor.transpose(psT[1][:, 0:P], hbuf[:, 0:P], ident[:, :]).then_inc(s_tp, 1)
                nc.tensor.transpose(psT[1][:, P:2 * P], hbuf[:, P:2 * P], ident[:, :]).then_inc(s_tp, 1)
                pe.wait_ge(s_tc, 4 * w + 4)
                mm(psA[:, 0:D], hT[:, 0, :], w2a[:, :], start=True, stop=False)
                mm(psA[:, 0:D], hT[:, 1, :], w2b[:, :], start=False, stop=True).then_inc(s_mm, 1)
            windows(pe, 0, l0)

            def aggregate(G, par, use, width=D, offset=0, row=D):
                pe.wait_ge(s_oh, G + NW + 1)
                pe.wait_ge(s_gat[par], (use + 1) * 16 * K)
                for k in range(K):
                    r = rows[:, par, k * row + offset:k * row + offset + width]
                    m = mm(acc[par][:, 0:width], oh[:, par, k, :], r, start=(k == 0), stop=(k == K - 1))
                m.then_inc(s_agg, 1)

            def acc_free(G):
                pe.wait_ge(s_accr, G + 1)
            pe.sem_inc(s_accr, CREDIT)

            for step in range(L1_STEPS):
                def l1(w, G, par, use, step=step):
                    acc_free(G)
                    aggregate(G, par, use)
                    if step < L1_STEPS - 1:
                        return
                    pe.wait_ge(s_h, NW + 1 + 2 * w + 1)
                    nc.tensor.transpose(psT[0][:, 0:P], xs[:, :], ident[:, :]).then_inc(s_tp, 1)
                    pe.wait_ge(s_tc, TC0 + 2 * w + 1)
                    mm(psA[:, 0:D], xT[:, :], wT[:, 0, :], start=True, stop=True).then_inc(s_mm, 1)
                    pe.wait_ge(s_h, NW + 1 + 2 * w + 2)
                    nc.tensor.transpose(psT[0][:, 0:P], xs[:, :], ident[:, :]).then_inc(s_tp, 1)
                    pe.wait_ge(s_tc, TC0 + 2 * w + 2)
                    mm(psB[:, 0:3 * D], xT[:, :], wT[:, 1:4, :].rearrange("p a d -> p (a d)"), start=True, stop=True).then_inc(s_mm, 1)
                windows(pe, step, l1)

            def l2(w, G, par, use):
                acc_free(G)
                pe.wait_ge(s_oh, G + NW + 1)
                q_w = Q[:, bass.ds(w, 1), :].rearrange("p a d -> p (a d)")

                def turn(g):
                    a, b = GROUPS[g]
                    for k in range(a, b):
                        m = nc.tensor.transpose(psT[g % 2][:, (k - a) * P:(k - a + 1) * P], oh[:, par, k, :], ident[:, :])
                    m.then_inc(s_qT, 1)

                turn(0)
                for g, (a, b) in enumerate(GROUPS):
                    if g + 1 < NG:
                        turn(g + 1)
                    pe.wait_ge(s_qTc, w * NG + g + 1)
                    if g >= 2:
                        pe.wait_ge(s_qer, w * NG + g - 1)
                    for k in range(a, b):
                        m = mm(psQ[g % 2][:, (k - a) * D:(k - a + 1) * D], ohT[:, g % 2, k - a, :], q_w, start=True, stop=True)
                    m.then_inc(s_qe, 1)
                pe.wait_ge(s_msg, (w + 1) * NG)
                aggregate(G, par, use, D + H, D - H, D2)
                pe.wait_ge(s_h, 3 * NW + 1 + w + 1)
                nc.tensor.transpose(psA[:, 0:P], xs[:, :], ident[:, :]).then_inc(s_tp, 1)
                pe.wait_ge(s_tc, TC1 + 2 * w + 2)
                mm(psB[:, 0:D], xT[:, :], l3_w1a[:, :], start=True, stop=False)
                mm(psB[:, 0:D], sT[:, :], l3_m[:, :], start=False, stop=True).then_inc(s_mm, 1)
            windows(pe, 3, l2)

            def l3(w, G, par, use):
                acc_free(G)
                aggregate(G, par, use)
                pe.wait_ge(s_h, 4 * NW + 1 + w + 1)
                nc.tensor.transpose(psT[0][:, 0:P], xs[:, :], ident[:, :]).then_inc(s_tp, 1)
                pe.wait_ge(s_tc, TC2 + w + 1)
                mm(psA[:, 0:D], xT[:, :], l3_w2[:, :], start=True, stop=True).then_inc(s_mm, 1)
            windows(pe, 4, l3)


_INS = ['x', 'src', 'dst', 'edge_attr_128', 'L0_gnn_W1', 'L0_gnn_b1', 'L0_gnn_gamma', 'L0_gnn_beta', 'L0_gnn_prelu_a',
        'L0_gnn_W2', 'L0_gnn_b2', 'L1_gnn_W', 'L2_gnn_Wq', 'L2_gnn_bq', 'L2_gnn_Wk', 'L2_gnn_bk', 'L2_gnn_Wv', 'L2_gnn_bv',
        'L3_gnn_We', 'L3_gnn_be', 'L3_gnn_W1', 'L3_gnn_b1', 'L3_gnn_W2', 'L3_gnn_b2']


def kernel(**inputs):
    import numpy as _np
    import concourse.bacc as _bacc
    from concourse import mybir as _mybir
    from concourse.bass_utils import run_bass_kernel_spmd as _run

    nc = _bacc.Bacc("TRN2", target_bir_lowering=False, num_devices=1)
    arrays, args = {}, {}
    for name in _INS:
        a = _np.ascontiguousarray(inputs[name])
        arrays[f"in_{name}"] = a
        args[name] = nc.dram_tensor(f"in_{name}", a.shape, _mybir.dt.from_np(a.dtype), kind="ExternalInput").ap()
    out = nc.dram_tensor("out_0", (N, D), _mybir.dt.float32, kind="ExternalOutput").ap()
    build(nc, args, out)
    return _run(nc, [arrays], core_ids=[0]).results[0]["out_0"]
```

```python
import concourse.bass as bass
from concourse import mybir
from contextlib import ExitStack

N, E, D = 6250, 106250, 128
P = 128
NW = -(-N // P)
NPAD = NW * P
LAST = N - (NW - 1) * P
K = 19
CHUNK = K * P
H = 8
HD = D // H
D2 = 2 * D
EP, EJ = 125, 850
HJ = 34
HSTEPS = EJ // HJ
GROUPS = [(a, min(a + 4, K)) for a in range(0, K, 4)]
NG = len(GROUPS)
CREDIT = 2
L1_STEPS = 3

BN, BT = 8, 2
WB = P // BN
NB = NW * WB
BW = NW * BN
ROW = 32
BR = BT * P // ROW
ER = -(-E // ROW) + BR
CW = 7
NCH = NW // CW
CB = CW * WB
RING = 4
ZS = 64.0
FAR = 1024.0

F32, I32 = mybir.dt.float32, mybir.dt.int32
F16, BF16 = mybir.dt.float16, mybir.dt.bfloat16
ALU = mybir.AluOpType
ACT = mybir.ActivationFunctionType
AXX = mybir.AxisListType.X


class Chain:

    def __init__(self, eng, sem, n, spare=None, base=0):
        self.eng, self.sem, self.n, self.spare, self.first, self.base, self.j = eng, sem, n, spare, base, base, 0

    def start(self, window):
        self.base, self.j = window * self.n + self.first, 0

    def __call__(self, ins):
        self.j += 1
        ins.then_inc(self.sem, 1)
        self.eng.wait_ge(self.sem, self.base + self.j)

    def held(self, ins):
        self(ins)
        self.eng.sem_inc(self.spare, 1)

    def end(self):
        assert self.j == self.n, (self.j, self.n)


class W:

    def __init__(self, i, rest, unroll):
        self.i, self.rest, self.unroll = i, rest, unroll
        self.v = i * unroll + rest if unroll else rest

    def mod(self, m):
        assert self.unroll % m == 0
        return self.rest % m

    def div(self, m):
        return self.i * (self.unroll // m) + self.rest // m if self.unroll else self.rest // m

    def plus(self, c):
        return W(self.i, self.rest + c, self.unroll)


def windows(eng, phase, body, unroll=2):
    with eng.Fori(0, (NW - 1) // unroll) as i:
        for h in range(unroll):
            body(W(i, h, unroll), W(i, phase * NW + h, unroll))
    last = W(0, NW - 1, 0)
    body(last, last.plus(phase * NW))


def skewed(eng, body, unroll):
    body(W(0, 0, 0), None)
    with eng.Fori(0, (NW - 1) // unroll) as i:
        for h in range(unroll):
            body(W(i, h + 1, unroll), W(i, h, unroll))
    body(None, W(0, NW - 1, 0))


REP_FREE = 8 + 2 + 9 + 1 + NCH * 8 + 3 + 1


def build(nc, A, out):
    ctx = ExitStack()
    with ctx:
        def sb(name, shape, dt=F32):
            return ctx.enter_context(nc.sbuf_tensor(name, shape, dt))

        def sem(name):
            return ctx.enter_context(nc.semaphore(name))

        def dram(name, shape, dt=F32):
            return nc.dram_tensor(name, shape, dt).ap()

        ctx.enter_context(nc.allow_non_contiguous_dma(reason="small columns and tables, once"))

        kv_tab = dram("kv_tab", (NPAD, D2))
        edge_tab = dram("edge_tab", (ER, 2, ROW), I32)
        off_tab = dram("off_tab", (NB,), I32)
        adj = dram("adj", (NW, P, NW, P), BF16)

        def carve(region, at, shape, dt=F32, parts=P):
            n = 1
            for x in shape:
                n *= x
            words = n * (2 if dt in (F16, BF16) else 4) // 4
            v = region[0:parts, at:at + words]
            if dt != F32:
                v = v.bitcast(dt)
            if len(shape) > 1:
                names = " ".join(f"d{i}" for i in range(len(shape)))
                v = v.rearrange(f"p ({names}) -> p {names}", **{f"d{i}": x for i, x in enumerate(shape)})
            return v, at + words

        X = sb("X", [P, NW, D])
        r_st = sb("r_st", [P, NW * P])
        r_zq = sb("r_zq", [P, 2 * NW * D])
        r_rows = sb("r_rows", [P, 2 * K * D2])
        r_oh = sb("r_oh", [P, 2 * K * P])
        r_tab = sb("r_tab", [P, NB * BT * 3 // 2])
        r_l0 = sb("r_l0", [P, K * P + D])
        rep, at = carve(r_st, 0, (P, HJ), BF16)
        pack, at = carve(r_st, at, (NCH, BR, 2 * ROW), I32, CB)
        lo_f, at = carve(r_zq, 0, (NCH, BT * P), F32, CB)
        comb_f, at = carve(r_zq, at, (NCH, BT * P), F32, CB)
        t_int, at = carve(r_zq, at, (BT * P,), I32, CB)
        t_a, at = carve(r_zq, at, (BT * P,), F32, CB)
        t_b, at = carve(r_zq, at, (BT * P,), F32, CB)
        hlo, at = carve(r_rows, 0, (2, P, HJ), BF16)
        hhi, at = carve(r_rows, at, (2, NW, HJ), BF16)
        dst_all, at = carve(r_rows, at, (NW, K), I32)
        flat_d, at = carve(r_oh, 0, (EJ,), I32)
        flat_s, at = carve(r_oh, at, (EJ,), I32)
        flat_i, at = carve(r_oh, at, (EJ,), I32)
        lo16, at = carve(r_oh, at, (2, EJ), BF16)
        hi16, at = carve(r_oh, at, (2, EJ), BF16)
        ST = r_st[:, :].rearrange("p (w n) -> p w n", n=P)
        ea, at = carve(r_rows, 0, (2, K, D))
        loh, at = carve(r_rows, at, (2, P, 8 * BT), BF16)
        rep_a, at = carve(r_rows, at, (P, 8 * BT), BF16)
        coh, at = carve(r_rows, at, (RING, BT, BW), BF16)
        assert at <= 2 * K * D2
        abuf, _ = carve(r_zq, NW * D, (2, NW, P), BF16)
        comb_t, at = carve(r_tab, 0, (NB * BT,))
        lo_t, at = carve(r_tab, at, (NB * BT,), BF16)
        zp = [carve(r_zq, b * NW * D, (NW, D2), F16)[0] for b in range(2)]
        Q, _ = carve(r_zq, NW * D, (NW, D))
        yp, _ = carve(r_zq, 0, (NW, 3 * D), BF16)
        aslot, at = carve(r_rows, 0, (3, NW, P), BF16)
        assert at <= 2 * K * D2
        rows = r_rows[:, :].rearrange("p (b n) -> p b n", b=2)
        oh = r_oh[:, :].rearrange("p (b k n) -> p b k n", b=2, n=P)
        ohT, _ = carve(r_tab, 0, (2, 4, P))
        qe = r_l0[:, 0:K * P].rearrange("p (k n) -> p k n", n=D)
        at = 0
        w1a, w1b, b1, gamma, beta, hbuf, hneg = (r_l0[:, D2 * i:D2 * i + D2] for i in range(7))
        w2a, w2b, b2 = (r_l0[:, 7 * D2 + D * i:7 * D2 + D * i + D] for i in range(3))
        hT = r_l0[:, 7 * D2 + 3 * D:7 * D2 + 5 * D].rearrange("p (a n) -> p a n", n=P)

        src_all = sb("src_all", [P, NW, K], I32)
        dloc = sb("dloc", [P, NW, K])
        idx_cur = sb("idx_cur", [P, 2, K], I32)
        comb_cur = sb("comb_cur", [P, 2, WB * BT])
        store = sb("store", [P, 2, D2])
        iota_f = sb("iota_f", [P, P])
        iota_b = sb("iota_b", [P, BW], F16)
        ident = sb("ident", [P, P])
        ident16 = sb("ident16", [P, P], BF16)
        wbase = sb("wbase", [P, NW])
        bbase = sb("bbase", [CB, NCH])
        ones = sb("ones", [P, WB])
        tri = sb("tri", [P, WB])
        upper = sb("upper", [NW, NW])
        indeg = sb("indeg", [P, NW])
        nin = sb("nin", [P, NW])
        inv_cnt = sb("inv_cnt", [P, NW])
        nout = sb("nout", [P, NW])
        clip = sb("clip", [P, 2, NW])
        tot = sb("tot", [NW, WB])
        off_i = sb("off_i", [WB, NW], I32)
        first_i = sb("first_i", [1, NW], I32)
        blk_off = sb("blk_off", [CB, NCH], I32)
        blk_row = sb("blk_row", [CB, NCH], I32)
        row_i = sb("row_i", [CB, NCH, BR], I32)
        eps_t = sb("eps_t", [P, 1])
        alpha = sb("alpha", [P, 1])
        wraw = sb("wraw", [P, 5, D])
        wT = sb("wT", [P, 5, D])
        bqkv = sb("bqkv", [P, 3 * D])
        l3_w1a = sb("l3_w1a", [P, D])
        l3_w1b = sb("l3_w1b", [P, D])
        l3_w2 = sb("l3_w2", [P, D])
        be_col = sb("be_col", [P, 1])
        be_bc = sb("be_bc", [P, P])
        l3_b1 = sb("l3_b1", [P, D])
        l3_b2 = sb("l3_b2", [P, D])
        l3_m = sb("l3_m", [P, D])
        l3_v = sb("l3_v", [P, D])
        xs = sb("xs", [P, D])
        xT = sb("xT", [P, P])
        sT = sb("sT", [P, P])
        stats = sb("stats", [P, 6])
        mv = sb("mv", [P, 2])
        std = sb("std", [P, 1])
        rstd = sb("rstd", [P, 1])
        yb = sb("yb", [P, D])
        yc = sb("yc", [P, D])
        zr = sb("zr", [P, H])
        sc = sb("sc", [P, K, H])
        empty = sb("empty", [BR + 1, 2 * ROW], I32)

        def pb(name, banks):
            return ctx.enter_context(nc.psum_tensor(name, [P, banks, 512], F32))
        acc = pb("acc", 2)
        pair = [pb("pair0", 2), pb("pair1", 2)]
        psA = pb("psA", 1)[:, 0, :]
        psB = pb("psB", 1)[:, 0, :]

        s_const = sem("constants_ready"); s_in = sem("weights_loaded"); s_edges = sem("edges_loaded")
        s_tab = sem("edge_table_written"); s_empty = sem("empty_rows_written")
        s_wT = sem("weights_transposed"); s_wc = sem("weights_copied")
        s_be = sem("be_spread"); s_fold = sem("l3_folded"); s_foldc = sem("l3_fold_copied")
        s_hoh = sem("hist_onehots"); s_hmm = sem("hist_products"); s_ind = sem("indegree_copied")
        s_tot = sem("window_totals"); s_totc = sem("window_totals_copied"); s_off = sem("offsets_summed")
        s_first = sem("first_edges_ready"); s_offw = sem("offsets_written"); s_offr = sem("block_offsets_loaded")
        s_rowi = sem("block_rows_ready"); s_pack = sem("block_edges_gathered")
        s_comb = sem("block_tables_ready"); s_ct = sem("block_tables_transposed"); s_ctc = sem("block_tables_copied")
        s_rep = sem("repeated_iota_ready"); s_win = sem("window_indices_loaded"); s_histd = sem("histograms_read")
        s_clip = sem("degrees_clipped"); s_sqrt = sem("degree_roots_ready"); s_setup = sem("dve_setup_step")
        s_ea = [sem(f"edge_rows_loaded{i}") for i in range(2)]
        s_oh0 = sem("l0_onehot_ready"); s_edge = sem("edge_features_summed"); s_coh = sem("block_onehots_ready")
        s_blk = sem("blocks_counted"); s_evac = sem("block_pairs_copied"); s_ab = sem("adjacency_stored")
        s_abf = sem("adjacency_buffer_free"); s_spare = sem("carries_a_wait"); s_dve = sem("dve_step")
        s_xs = sem("l0_x_copied"); s_tp = sem("pe_transposed"); s_tc = sem("transposes_copied")
        s_mm = sem("pe_product_ready"); s_var = sem("variance_ready"); s_std = sem("std_ready")
        s_h = sem("hidden_ready"); s_h2 = sem("be_term_ready"); s_yp = sem("y_part_step"); s_spare0 = sem("block_columns_ready"); s_z = sem("propagated_row_ready")
        s_a = [sem(f"adjacency_loaded{i}") for i in range(3)]
        s_fagg = sem("propagated"); s_facc = sem("propagated_read")
        s_idx = sem("gather_indices_ready"); s_gat = [sem(f"rows_gathered{i}") for i in range(2)]
        s_oh = sem("l2_onehot_ready"); s_agg = sem("l2_aggregated"); s_qT = sem("onehots_transposed")
        s_qTc = sem("onehotT_copied"); s_qe = sem("queries_expanded"); s_qec = sem("queries_copied")
        s_prod = sem("qk_products_ready"); s_sc = sem("scores_ready"); s_exp = sem("exp_ready"); s_msg = sem("messages_ready")
        s_store = sem("rows_to_store"); s_stored = sem("rows_stored"); s_free = sem("store_buffer_free")

        def bc_row(v, n):
            return v.rearrange("(a n) -> a n", a=1).to_broadcast([P, n])

        LOADS = [(w1a, A["L0_gnn_W1"][0:P, :]), (w1b, A["L0_gnn_W1"][P:2 * P, :]),
                 (w2a, A["L0_gnn_W2"][0:P, :]), (w2b, A["L0_gnn_W2"][P:2 * P, :]),
                 (b1, bc_row(A["L0_gnn_b1"], D2)), (gamma, bc_row(A["L0_gnn_gamma"], D2)),
                 (beta, bc_row(A["L0_gnn_beta"], D2)), (alpha[:, :], bc_row(A["L0_gnn_prelu_a"], 1)),
                 (b2, bc_row(A["L0_gnn_b2"], D)),
                 (wraw[:, 0, :], A["L1_gnn_W"]), (wraw[:, 1, :], A["L2_gnn_Wq"]), (wraw[:, 2, :], A["L2_gnn_Wk"]),
                 (wraw[:, 3, :], A["L2_gnn_Wv"]), (wraw[:, 4, :], A["L3_gnn_We"]),
                 (bqkv[:, 0:D], bc_row(A["L2_gnn_bq"], D)), (bqkv[:, D:2 * D], bc_row(A["L2_gnn_bk"], D)),
                 (bqkv[:, 2 * D:3 * D], bc_row(A["L2_gnn_bv"], D)),
                 (l3_w1a[:, :], A["L3_gnn_W1"][0:P, :]), (l3_w1b[:, :], A["L3_gnn_W1"][P:2 * P, :]),
                 (l3_w2[:, :], A["L3_gnn_W2"]), (be_col[:, :], A["L3_gnn_be"].rearrange("(p a) -> p a", a=1)),
                 (l3_b1[:, :], bc_row(A["L3_gnn_b1"], D)), (l3_b2[:, :], bc_row(A["L3_gnn_b2"], D)),
                 *[(X[:, w:w + 6, :], A["x"][w * P:(w + 6) * P, :].rearrange("(w p) d -> p w d", p=P))
                   for w in range(0, NW - 1, 6)],
                 (X[0:LAST, NW - 1, :], A["x"][(NW - 1) * P:N, :])]
        N_CONST = 11
        TP1, TC1, MM1, VAR1, H1 = 3 * NW, 4 * NW, 2 * NW, 2 * NW, NW
        TP2, TC2, MM2, VAR2, H2 = 5 * NW, 6 * NW, 4 * NW, 3 * NW, 3 * NW
        TP3, TC3, MM3, VAR3, H3 = 6 * NW, 8 * NW, 5 * NW, 4 * NW, 4 * NW

        def at_window(t, w):
            return t[:, bass.ds(w.v, 1), :].rearrange("p a d -> p (a d)")

        def column(t, w):
            return t[:, bass.ds(w.v, 1)]

        block = ctx.enter_context(nc.Block())

        @block.sync
        def _(sp):
            sp.sem_inc(s_abf, CREDIT)
            sp.dma_start(flat_d[0:EP, :], A["dst"].rearrange("(p j) -> p j", p=EP)).then_inc(s_edges, 16)
            sp.wait_ge(s_edges, 16)
            sp.sem_inc(s_spare, 1)
            sp.dma_start(flat_s[0:EP, :], A["src"].rearrange("(p j) -> p j", p=EP)).then_inc(s_edges, 16)
            full = E // ROW
            sp.wait_ge(s_const, N_CONST)
            sp.dma_start(edge_tab[full:ER, :, :].rearrange("r a n -> r (a n)"), empty[0:ER - full, :]).then_inc(s_empty, 16)
            for i, name in enumerate(("src", "dst")):
                sp.dma_start(edge_tab[0:full, i, :], A[name][0:full * ROW].rearrange("(r n) -> r n", n=ROW)).then_inc(s_tab, 16)
            sp.wait_ge(s_empty, 16)
            for i, name in enumerate(("src", "dst")):
                sp.dma_start(edge_tab[full:full + 1, i, 0:E - full * ROW],
                             A[name][full * ROW:E].rearrange("(r n) -> r n", r=1)).then_inc(s_tab, 16)
            for dst_ap, src_ap in LOADS:
                sp.dma_start(dst_ap, src_ap).then_inc(s_in, 16)
            sp.wait_ge(s_first, 2)
            sp.dma_start(off_tab.rearrange("(w m) -> m w", m=WB), off_i[:, :]).then_inc(s_offw, 16)
            sp.wait_ge(s_offw, 16)
            sp.dma_start(blk_off[:, :], off_tab.rearrange("(c p) -> p c", p=CB)).then_inc(s_offr, 16)

            sp.wait_ge(s_histd, 2)

            def load_window(w, G):
                first = sp.value_load(first_i[0:1, bass.ds(w.v, 1)], min_val=0, max_val=E - CHUNK)
                for dst_ap, name in ((src_all, "src"), (dst_all, "dst")):
                    sp.dma_start(at_window(dst_ap, w),
                                 A[name][bass.ds(first, CHUNK)].rearrange("(p k) -> p k", p=P)).then_inc(s_win, 16)
            windows(sp, 0, load_window)

            def store_adjacency(w, G):
                sp.wait_ge(s_evac, (w.v + 1) * (WB // 2) + CREDIT)
                sp.dma_start(adj[bass.ds(w.v, 1), :, :, :].rearrange("a p w n -> p (a w n)"),
                             abuf[:, w.mod(2), :, :].rearrange("p w n -> p (w n)")).then_inc(s_ab, 16)
                sp.wait_ge(s_ab, (w.v + 1) * 16)
                sp.sem_inc(s_abf, 1)
            windows(sp, 0, store_adjacency)

            def load_adjacency(w, G):
                sp.wait_ge(s_fagg, G.v + 1)
                sp.dma_start(aslot[:, G.mod(3), :, :].rearrange("p w n -> p (w n)"),
                             adj[bass.ds(w.v, 1), :, :, :].rearrange("a p w n -> p (a w n)")).then_inc(s_a[G.mod(3)], 16)
            sp.wait_ge(s_edge, NW + CREDIT)
            for phase in range(L1_STEPS):
                windows(sp, phase, load_adjacency, 6)
            sp.wait_ge(s_agg, NW + CREDIT)
            windows(sp, L1_STEPS, load_adjacency, 6)

        @block.gpsimd
        def _(pool):
            pool.sem_inc(s_free, CREDIT)
            small = dict(channel_multiplier=0, allow_small_or_imprecise_dtypes=True)
            nc.gpsimd.iota(rep[:, :, :], pattern=[[1, P], [0, HJ]], base=0, **small).then_inc(s_const, 1)
            nc.gpsimd.memset(X[:, NW - 1, :], 0.0).then_inc(s_const, 1)
            nc.gpsimd.memset(ident[:, :], 0.0).then_inc(s_const, 1)
            nc.gpsimd.memset(tri[:, :], 1.0).then_inc(s_const, 1)
            nc.gpsimd.memset(upper[:, :], 1.0).then_inc(s_const, 1)
            nc.gpsimd.memset(empty[:, :], -1).then_inc(s_const, 1)
            pool.wait_ge(s_const, 6)
            nc.gpsimd.affine_select(out=ident[:, :], in_=ident[:, :], compare_op=ALU.not_equal, fill=1.0,
                                    base=0, pattern=[[-1, P]], channel_multiplier=1).then_inc(s_const, 1)
            nc.gpsimd.affine_select(out=tri[:, :], in_=tri[:, :], compare_op=ALU.is_gt, fill=0.0,
                                    base=0, pattern=[[BN, WB]], channel_multiplier=-1).then_inc(s_const, 1)
            nc.gpsimd.affine_select(out=upper[:, :], in_=upper[:, :], compare_op=ALU.is_gt, fill=0.0,
                                    base=0, pattern=[[1, NW]], channel_multiplier=-1).then_inc(s_const, 1)
            nc.gpsimd.iota(wbase[:, :], pattern=[[P, NW]], base=0, **small).then_inc(s_const, 1)
            nc.gpsimd.iota(bbase[:, :], pattern=[[CB * BN, NCH]], base=0, channel_multiplier=BN,
                           allow_small_or_imprecise_dtypes=True).then_inc(s_const, 1)
            nc.gpsimd.iota(iota_f[:, :], pattern=[[1, P]], base=0, **small).then_inc(s_rep, 1)
            nc.gpsimd.iota(iota_b[:, :], pattern=[[1, BW]], base=0, **small).then_inc(s_rep, 1)
            pool.wait_ge(s_rowi, 1)
            pool.wait_ge(s_tab, 4 * 16)
            for c in range(NCH):
                for j in range(BR):
                    pool.indirect_dma_start(pack[:, c, j, :], None, edge_tab.rearrange("r a n -> r (a n)"),
                                            bass.IndirectOffsetOnAxis(ap=row_i[:, c, j:j + 1], axis=0)).then_inc(s_pack, 16)
            pool.wait_ge(s_histd, 2)
            pool.wait_ge(s_setup, REP_FREE)
            nc.gpsimd.iota(rep_a[:, :, :], pattern=[[1, P], [0, 8 * BT]], base=0, **small).then_inc(s_rep, 1)

            def store_rows(phase, target):
                def store_window(w, G):
                    last = w.unroll == 0
                    n = LAST if last and target is out else P
                    width = D if target is out else D2
                    dst_ap = target[w.v * P:w.v * P + n, :] if last else target[bass.ds(w.v * P, P), :]
                    pool.wait_ge(s_store, G.v + 1)
                    pool.sem_inc(s_spare, 1)
                    pool.dma_start(dst_ap, store[0:n, G.mod(2), 0:width]).then_inc(s_stored, 16)
                    pool.wait_ge(s_stored, (G.v + 1) * 16)
                    pool.sem_inc(s_free, 1)
                windows(pool, phase, store_window)
            store_rows(0, kv_tab)

            def gather_window(w, G):
                pool.wait_ge(s_idx, w.v + 1)
                pool.sem_inc(s_spare, 1)
                for k in range(K):
                    pool.indirect_dma_start(rows[:, w.mod(2), k * D2:(k + 1) * D2], None, kv_tab,
                                            bass.IndirectOffsetOnAxis(ap=idx_cur[:, w.mod(2), k:k + 1], axis=0)
                                            ).then_inc(s_gat[w.mod(2)], 16)
            windows(pool, 0, gather_window)
            store_rows(1, out)

        @block.scalar
        def _(act):
            copy = nc.scalar.copy
            act.wait_ge(s_wT, 1)
            copy(wT[:, 0:4, :].rearrange("p a d -> p (a d)"), acc[:, 0, :]).then_inc(s_wc, 1)
            copy(wT[:, 4, :], acc[:, 1, 0:D]).then_inc(s_wc, 1)
            act.wait_ge(s_tot, 1)
            copy(tot[:, :], psB[0:NW, 0:WB]).then_inc(s_totc, 1)
            for c in range(NCH):
                cols = slice(c * CB * BT, (c + 1) * CB * BT)
                act.wait_ge(s_ct, c + 1)
                for t, table in ((0, comb_t), (1, lo_t)):
                    copy(table[:, cols].rearrange("p (b t) -> p b t", t=BT),
                         pair[c % 2][:, t, 0:BT * CB].rearrange("p (t b) -> p b t", t=BT)).then_inc(s_ctc, 1)
            act.wait_ge(s_clip, 1)
            nc.scalar.activation(clip[:, :, :], clip[:, :, :], ACT.Sqrt).then_inc(s_sqrt, 1)
            act.wait_ge(s_fold, 1)
            copy(l3_m[:, :], psA[:, 0:D]).then_inc(s_foldc, 1)
            copy(l3_v[:, :], psA[:, D:2 * D]).then_inc(s_foldc, 1)

            def load_edges(w):
                act.wait_ge(s_edge, w.v + 1)
                first = act.value_load(first_i[0:1, bass.ds(w.v, 1)], min_val=0, max_val=E - CHUNK)
                act.dma_start(ea[:, w.mod(2), :, :].rearrange("p k d -> p (k d)"),
                              A["edge_attr_128"][bass.ds(first, CHUNK), :].rearrange("(p k) d -> p (k d)", p=P)
                              ).then_inc(s_ea[w.mod(2)], 16)

            def std_of(n):
                act.wait_ge(s_var, n)
                nc.scalar.activation(std[:, :], mv[:, 1:2], ACT.Sqrt, bias=eps_t[:, :]).then_inc(s_std, 1)

            def count_pair(w, q):
                act.wait_ge(s_blk, w.v * WB + 2 * q + 2 + RING)
                v = abuf[:, w.mod(2), :, 2 * q * BN:(2 * q + 2) * BN].rearrange("p w (b n) -> p b w n", b=2)
                copy(v, pair[q % 2][:, :, 0:BW].rearrange("p b (w n) -> p b w n", n=BN)).then_inc(s_evac, 1)

            def l0(w, e):
                if e is not None:
                    copy(xs[:, :], at_window(X, e)).then_inc(s_xs, 1)
                if w is not None:
                    load_edges(w)
                    act.wait_ge(s_abf, w.v + 1)
                for q in range(WB // 2):
                    if w is not None:
                        count_pair(w, q)
                    if e is None:
                        continue
                    if q == 0:
                        act.wait_ge(s_edge, e.v + 1 + CREDIT)
                        copy(sT[:, :], acc[:, e.mod(2), 0:P]).then_inc(s_tc, 1)
                        copy(at_window(ST, e), acc[:, e.mod(2), 0:P]).then_inc(s_tc, 1)
                        act.wait_ge(s_tp, e.v * 3 + 1)
                        copy(xT[:, :], psB[:, 0:P]).then_inc(s_tc, 1)
                    if q == 3:
                        std_of(e.v * 2 + 1)
                    if q == 5:
                        act.wait_ge(s_tp, e.v * 3 + 3)
                        copy(hT[:, :, :], psB[:, 0:2 * P].rearrange("p (a n) -> p a n", n=P)).then_inc(s_tc, 1)
                    if q == 6:
                        std_of(e.v * 2 + 2)
            act.wait_ge(s_first, 2)
            act.wait_ge(s_in, 16 * len(LOADS))
            skewed(act, l0, 2)

            def l1_last(w, G):
                act.wait_ge(s_tp, TP1 + w.v * 2 + 1)
                copy(xT[:, :], psB[:, 0:P]).then_inc(s_tc, 1)
                std_of(VAR1 + w.v + 1)
                act.wait_ge(s_tp, TP1 + w.v * 2 + 2)
                copy(xT[:, :], psB[:, 0:P]).then_inc(s_tc, 1)
            windows(act, 0, l1_last)

            def indices(w):
                act.wait_ge(s_agg, w.v + 1)
                copy(idx_cur[:, w.mod(2), :], at_window(src_all, w)).then_inc(s_idx, 1)

            def expand(w, prod=None):
                def queries(g):
                    a, b = GROUPS[g]
                    act.wait_ge(s_qe, w.v * NG + g + 1)
                    copy(qe[:, a:b, :].rearrange("p k n -> p (k n)"), pair[1][:, g % 2, 0:(b - a) * D]).then_inc(s_qec, 1)
                for g, (a, b) in enumerate(GROUPS):
                    act.wait_ge(s_qT, w.v * NG + g + 1)
                    if g >= 2:
                        queries(g - 2)
                    copy(ohT[:, g % 2, 0:b - a, :].rearrange("p k n -> p (k n)"),
                         pair[0][:, g % 2, 0:(b - a) * P]).then_inc(s_qTc, 1)
                queries(NG - 2)
                queries(NG - 1)

            w0 = W(0, 0, 0)
            act.wait_ge(s_mm, MM2)
            indices(w0)
            expand(w0)

            def l2(w, G):
                last = w.unroll == 0
                if not last:
                    indices(w.plus(1))
                act.wait_ge(s_sc, w.v + 1)
                s_at = rows[:, w.mod(2), :].rearrange("p (k n) -> p k n", n=D2)[:, :, D - H:D]
                nc.scalar.activation(s_at, sc[:, :, :], ACT.Exp, scale=1.0 / HD ** 0.5).then_inc(s_exp, 1)
                if not last:
                    expand(w.plus(1))
                std_of(VAR2 + w.v + 1)
                act.wait_ge(s_tp, TP2 + w.v + 1)
                copy(xT[:, :], psA[:, 0:P]).then_inc(s_tc, 1)
                copy(sT[:, :], at_window(ST, w)).then_inc(s_tc, 1)
            windows(act, 0, l2)

            def l3(w, G):
                act.wait_ge(s_tp, TP3 + w.v + 1)
                copy(xT[:, :], psB[:, 0:P]).then_inc(s_tc, 1)
                std_of(VAR3 + w.v + 1)
            windows(act, 0, l3)

        @block.vector
        def _(dve):
            V = nc.vector
            setup = Chain(dve, s_setup, 0)

            V.memset(eps_t[:, :], 1e-5).then_inc(s_spare, 1)
            setup(V.memset(ones[:, :], 1.0))
            dve.wait_ge(s_const, N_CONST)
            setup(V.tensor_copy(ident16[:, :], ident[:, :]))

            def histogram(i, flat):
                dve.wait_ge(s_edges, 16 * (i + 1))
                f = flat[0:EP, :]
                setup(V.tensor_scalar(flat_i[0:EP, :], f, 7, None, ALU.arith_shift_right))
                setup(V.tensor_copy(hi16[0:EP, i, :], flat_i[0:EP, :]))
                setup(V.tensor_scalar(flat_i[0:EP, :], f, P - 1, None, ALU.bitwise_and))
                setup(V.tensor_copy(lo16[0:EP, i, :], flat_i[0:EP, :]))

                def onehots(col, par):
                    V.tensor_tensor(hlo[0:EP, par, :, :], lo16[0:EP, i, col].unsqueeze(1).to_broadcast([EP, P, HJ]),
                                    rep[0:EP, :, :], ALU.is_equal).then_inc(s_hoh, 1)
                    V.tensor_tensor(hhi[0:EP, par, :, :], hi16[0:EP, i, col].unsqueeze(1).to_broadcast([EP, NW, HJ]),
                                    rep[0:EP, 0:NW, :], ALU.is_equal).then_inc(s_hoh, 1)
                h0 = i * HSTEPS
                if i == 0:
                    onehots(slice(0, HJ), 0)
                    onehots(slice(HJ, 2 * HJ), 1)
                else:
                    for t in range(2):
                        dve.wait_ge(s_hmm, h0 + t - 1)
                        onehots(slice(t * HJ, (t + 1) * HJ), (h0 + t) % 2)
                with dve.Fori(0, (HSTEPS - 3) // 2) as j:
                    for t in (2, 3):
                        dve.wait_ge(s_hmm, j * 2 + (h0 + t - 1))
                        onehots(bass.ds(j * (2 * HJ) + t * HJ, HJ), (h0 + t) % 2)
                t = HSTEPS - 1
                dve.wait_ge(s_hmm, h0 + t - 1)
                onehots(slice(t * HJ, (t + 1) * HJ), (h0 + t) % 2)
            histogram(0, flat_d)
            dve.wait_ge(s_hmm, HSTEPS)
            V.tensor_copy(indeg[:, :], psA[:, 0:NW]).then_inc(s_ind, 1)
            dve.wait_ge(s_off, 1)
            V.tensor_scalar(first_i[:, :], psB[0:1, 64:64 + NW], float(E - CHUNK), None, ALU.min).then_inc(s_first, 1)
            V.tensor_copy(off_i[:, :], psB[0:WB, 64:64 + NW]).then_inc(s_first, 1)
            histogram(1, flat_s)
            dve.wait_ge(s_offr, 16)
            setup(V.tensor_scalar(blk_row[:, :], blk_off[:, :], 5, None, ALU.arith_shift_right))
            for j in range(BR):
                ins = V.tensor_scalar(row_i[:, :, j], blk_row[:, :], float(j), None, ALU.add)
                setup(ins)
            V.tensor_scalar(row_i[:, :, BR - 1], blk_row[:, :], float(BR - 1), None, ALU.add).then_inc(s_rowi, 1)
            dve.wait_ge(s_hmm, 2 * HSTEPS)
            V.tensor_scalar(clip[:, 0, :], indeg[:, :], 1.0, None, ALU.max).then_inc(s_histd, 1)
            V.tensor_scalar(clip[:, 1, :], psA[:, 64:64 + NW], 1.0, None, ALU.max).then_inc(s_histd, 1)
            dve.wait_ge(s_histd, 2)
            setup(V.reciprocal(inv_cnt[:, :], clip[:, 0, :]))
            for c in range(NCH):
                dve.wait_ge(s_pack, (NCH * BR) * 16 if c == 0 else (NCH * BR) * 16)
                s_v = pack[:, c, :, 0:ROW]
                d_v = pack[:, c, :, ROW:2 * ROW]
                ti = t_int[:, :].rearrange("p (r n) -> p r n", n=ROW)
                ta = t_a[:, :].rearrange("p (r n) -> p r n", n=ROW)
                setup(V.tensor_scalar(ti, s_v, P - 1, None, ALU.bitwise_and))
                setup(V.tensor_copy(lo_f[:, c, :], t_int[:, :]))
                setup(V.tensor_scalar(ti, s_v, 7, None, ALU.arith_shift_right))
                setup(V.tensor_scalar(ta, d_v, bbase[:, c:c + 1], None, ALU.subtract))
                setup(V.scalar_tensor_tensor(comb_f[:, c, :], t_int[:, :], float(BN), t_a[:, :], ALU.mult, ALU.add))
                setup(V.tensor_scalar(t_b[:, :], t_a[:, :], 0.0, FAR, ALU.is_lt, ALU.mult))
                setup(V.tensor_tensor(comb_f[:, c, :], comb_f[:, c, :], t_b[:, :], ALU.add))
                setup(V.tensor_scalar(t_b[:, :], t_a[:, :], float(BN) - 0.5, FAR, ALU.is_gt, ALU.mult))
                V.tensor_tensor(comb_f[:, c, :], comb_f[:, c, :], t_b[:, :], ALU.add).then_inc(s_comb, 1)
                dve.wait_ge(s_comb, c + 1)
                if c < NCH - 1:
                    continue
            V.tensor_copy(clip[:, 0, 0:1], clip[:, 0, 0:1]).then_inc(s_clip, 1)
            dve.wait_ge(s_sqrt, 1)
            setup(V.reciprocal(clip[:, :, :], clip[:, :, :]))
            setup(V.tensor_scalar(nin[:, :], clip[:, 0, :], 0.5 / ZS, None, ALU.mult))
            setup(V.tensor_scalar(nout[:, :], clip[:, 1, :], ZS, None, ALU.mult))
            dve.wait_ge(s_in, 16 * len(LOADS))
            V.tensor_copy(be_bc[:, :], be_col[:, :].to_broadcast([P, P])).then_inc(s_be, 1)
            dve.wait_ge(s_win, 2 * 16 * NW)
            setup(V.tensor_tensor(dloc[:, :, :], dst_all[:, :, :], wbase[:, :].unsqueeze(2).to_broadcast([P, NW, K]), ALU.subtract))
            assert setup.j == REP_FREE, setup.j
            dve.wait_ge(s_rep, 3)
            dve.wait_ge(s_ctc, 2 * NCH)

            def onehot(w):
                return V.tensor_tensor(
                    oh[:, w.mod(2), :, :], at_window(dloc, w).unsqueeze(2).to_broadcast([P, K, P]),
                    iota_f[:, :].unsqueeze(1).to_broadcast([P, K, P]), ALU.is_equal)

            def normalised(link, dst_ap, src):
                return V.tensor_scalar(dst_ap, src, mv[:, 0:1], rstd[:, :], ALU.subtract, ALU.mult)

            def moments(link, src):
                link.held(V.bn_stats(stats[:, :], src))
                V.bn_aggr(mv[:, :], stats[:, :]).then_inc(s_var, 1)

            def split_z(link, w, b):
                link(V.tensor_copy(zp[b][:, bass.ds(w.v, 1), 0:D].rearrange("p a d -> p (a d)"), yc[:, :]))
                V.tensor_tensor(zp[b][:, bass.ds(w.v, 1), D:D2].rearrange("p a d -> p (a d)"), yc[:, :],
                                zp[b][:, bass.ds(w.v, 1), 0:D].rearrange("p a d -> p (a d)"), ALU.subtract).then_inc(s_z, 1)

            n0 = 15
            link = Chain(dve, s_dve, n0, s_spare)

            def l0_epilogue(e, b):
                if b == 6:
                    dve.wait_ge(s_mm, e.v * 2 + 1)
                    link(V.scalar_tensor_tensor(hneg, psA[:, 0:D2], column(inv_cnt, e), b1, ALU.mult, ALU.add))
                    link(V.tensor_tensor(hbuf, hneg, psA[:, D2:2 * D2], ALU.add))
                    moments(link, hbuf)
                if b == 9:
                    dve.wait_ge(s_std, e.v * 2 + 1)
                    link(V.reciprocal(rstd[:, :], std[:, :]))
                    link(normalised(link, hbuf, hbuf))
                    link(V.tensor_tensor(hbuf, hbuf, gamma, ALU.mult))
                    link(V.tensor_tensor(hbuf, hbuf, beta, ALU.add))
                    link(V.tensor_scalar(hneg, hbuf, 0.0, alpha[:, :], ALU.min, ALU.mult))
                    V.scalar_tensor_tensor(hbuf, hbuf, 0.0, hneg, ALU.max, ALU.add).then_inc(s_h, 1)
                if b == 13:
                    dve.wait_ge(s_mm, e.v * 2 + 2)
                    link(V.tensor_tensor(yb[:, :], psA[:, 0:D], b2, ALU.add))
                    link(V.tensor_tensor(yb[:, :], yb[:, :], xs[:, :], ALU.add))
                    moments(link, yb[:, :])
                if b == 15:
                    dve.wait_ge(s_std, e.v * 2 + 2)
                    link(V.reciprocal(rstd[:, :], std[:, :]))
                    link(normalised(link, at_window(X, e), yb[:, :]))
                    link(V.tensor_scalar(yc[:, :], at_window(X, e), column(nout, e), None, ALU.mult))
                    split_z(link, e, 0)

            def l0(w, e):
                if e is not None:
                    link.start(e.v)
                if w is not None:
                    dve.wait_ge(s_edge, w.v + 1)
                    onehot(w).then_inc(s_oh0, 1)
                    V.tensor_scalar(comb_cur[:, w.mod(2), :], comb_t[:, bass.ds(w.v * (WB * BT), WB * BT)], 0.0, None,
                                    ALU.add).then_inc(s_spare0, 1)
                    dve.wait_ge(s_spare0, w.v + 1)
                for b in range(WB):
                    if w is not None:
                        if b % 8 == 0:
                            V.tensor_tensor(loh[:, b // 8, :, :],
                                            lo_t[:, bass.ds(w.v * (WB * BT) + b * BT, 8 * BT)].unsqueeze(1).to_broadcast([P, P, 8 * BT]),
                                            rep_a[:, :, :], ALU.is_equal).then_inc(s_coh, 1)
                        dve.wait_ge(s_blk, w.v * WB + b + 1)
                        for t in range(BT):
                            ins = V.tensor_scalar(coh[:, b % RING, t, :], iota_b[:, :],
                                                  comb_cur[:, w.mod(2), b * BT + t:b * BT + t + 1], None, ALU.is_equal)
                        ins.then_inc(s_coh, 1)
                    if e is not None:
                        l0_epilogue(e, b)
                if e is not None:
                    link.end()
            skewed(dve, l0, 2)
            s0 = n0 * NW

            for step in range(L1_STEPS):
                last = step == L1_STEPS - 1
                n1 = 6 if last else 4
                link = Chain(dve, s_dve, n1, s_spare, s0)

                def l1(w, G, link=link, last=last, step=step):
                    link.start(w.v)
                    dve.wait_ge(s_fagg, G.v + 1 + 3)
                    p = acc[:, G.mod(2), :]
                    link(V.tensor_scalar(yb[:, :], p[:, 0:D], column(nin, w), None, ALU.mult))
                    V.scalar_tensor_tensor(yb[:, :], p[:, D:D2], column(nin, w), yb[:, :], ALU.mult, ALU.add).then_inc(s_facc, 1)
                    dve.wait_ge(s_facc, G.v + 1 + CREDIT)
                    if not last:
                        link(V.scalar_tensor_tensor(xs[:, :], at_window(X, w), 0.5, yb[:, :], ALU.mult, ALU.add))
                        link(V.tensor_scalar(yc[:, :], xs[:, :], column(nout, w), None, ALU.mult))
                        split_z(link, w, 1 - step % 2)
                        link.end()
                        return
                    V.scalar_tensor_tensor(xs[:, :], at_window(X, w), 0.5, yb[:, :], ALU.mult, ALU.add).then_inc(s_h, 1)
                    dve.wait_ge(s_mm, MM1 + w.v * 2 + 1)
                    link(V.tensor_tensor(yb[:, :], psA[:, 0:D], at_window(X, w), ALU.add))
                    moments(link, yb[:, :])
                    dve.wait_ge(s_std, VAR1 + w.v + 1)
                    link(V.reciprocal(rstd[:, :], std[:, :]))
                    normalised(link, xs[:, :], yb[:, :]).then_inc(s_h, 1)
                    link(normalised(link, at_window(X, w), yb[:, :]))
                    dve.wait_ge(s_mm, MM1 + w.v * 2 + 2)
                    link(V.tensor_tensor(at_window(Q, w), psA[:, 0:D], bqkv[:, 0:D], ALU.add))
                    dve.wait_ge(s_free, w.v + 1)
                    V.tensor_tensor(store[:, w.mod(2), :], psA[:, D:3 * D], bqkv[:, D:3 * D], ALU.add).then_inc(s_store, 1)
                    dve.wait_ge(s_store, w.v + 1)
                    link.end()
                windows(dve, step, l1, 6)
                s0 += n1 * NW

            n2 = 9
            link = Chain(dve, s_dve, n2, s_spare, s0)
            onehot(W(0, 0, 0)).then_inc(s_oh, 1)

            def l2(w, G):
                link.start(w.v)
                if w.unroll:
                    onehot(w.plus(1)).then_inc(s_oh, 1)
                kv = rows[:, w.mod(2), :].rearrange("p (k n) -> p k n", n=D2)
                dve.wait_ge(s_qec, (w.v + 1) * NG)
                dve.wait_ge(s_gat[w.mod(2)], (w.div(2) + 1) * 16 * K)
                V.tensor_tensor(kv[:, :, 0:D], kv[:, :, 0:D], qe[:, :, :], ALU.mult).then_inc(s_prod, 1)
                dve.wait_ge(s_prod, w.v + 1)
                link(V.tensor_reduce(sc[:, :, :], kv[:, :, 0:D].rearrange("p k (h d) -> p k h d", d=HD), AXX, ALU.add))
                lim = 5.0 * HD ** 0.5
                V.tensor_scalar(sc[:, :, :], sc[:, :, :], lim, -lim, ALU.min, ALU.max).then_inc(s_sc, 1)
                dve.wait_ge(s_exp, w.v + 1)
                for a, b in ((0, K // 2), (K // 2, K)):
                    v = kv[:, a:b, D:D2].rearrange("p k (h d) -> p k h d", d=HD)
                    s = kv[:, a:b, D - H:D].unsqueeze(3).to_broadcast([P, b - a, H, HD])
                    V.tensor_tensor(v, v, s, ALU.mult).then_inc(s_msg, 1)
                dve.wait_ge(s_agg, w.v + 1 + CREDIT)
                p = acc[:, w.mod(2), :]
                link(V.tensor_scalar(zr[:, :], p[:, 0:H], 1e-6, None, ALU.add))
                link(V.reciprocal(zr[:, :], zr[:, :]))
                link(V.tensor_tensor(yb[:, :].rearrange("p (h d) -> p h d", d=HD),
                                     p[:, H:H + D].rearrange("p (h d) -> p h d", d=HD),
                                     zr[:, :].unsqueeze(2).to_broadcast([P, H, HD]), ALU.mult))
                link(V.tensor_tensor(yb[:, :], yb[:, :], at_window(X, w), ALU.add))
                moments(link, yb[:, :])
                dve.wait_ge(s_std, VAR2 + w.v + 1)
                link(V.reciprocal(rstd[:, :], std[:, :]))
                normalised(link, xs[:, :], yb[:, :]).then_inc(s_h, 1)
                V.tensor_scalar(yc[:, :], l3_v[:, :], column(indeg, w), None, ALU.mult).then_inc(s_h2, 1)
                link(normalised(link, at_window(X, w), yb[:, :]))
                dve.wait_ge(s_mm, MM2 + w.v + 1)
                dve.wait_ge(s_h2, w.v + 1)
                link(V.tensor_tensor(yb[:, :], psB[:, 0:D], yc[:, :], ALU.add))
                parts = [yp[:, bass.ds(w.v, 1), i * D:(i + 1) * D].rearrange("p a d -> p (a d)") for i in range(3)]
                V.tensor_copy(parts[0], yb[:, :]).then_inc(s_yp, 1)
                dve.wait_ge(s_yp, w.v * 3 + 1)
                V.tensor_tensor(yc[:, :], yb[:, :], parts[0], ALU.subtract).then_inc(s_yp, 1)
                dve.wait_ge(s_yp, w.v * 3 + 2)
                V.tensor_copy(parts[1], yc[:, :]).then_inc(s_yp, 1)
                dve.wait_ge(s_yp, w.v * 3 + 3)
                V.tensor_tensor(parts[2], yc[:, :], parts[1], ALU.subtract).then_inc(s_z, 1)
                dve.wait_ge(s_z, 3 * NW + w.v + 1)
                link.end()
            windows(dve, 0, l2)
            s0 += n2 * NW

            n3 = 6
            link = Chain(dve, s_dve, n3, s_spare, s0)

            def l3(w, G):
                link.start(w.v)
                dve.wait_ge(s_fagg, G.v + 1 + 3)
                p = acc[:, G.mod(2), :]
                link(V.tensor_tensor(yb[:, :], p[:, 2 * D:3 * D], l3_b1[:, :], ALU.add))
                link(V.tensor_tensor(yb[:, :], p[:, D:2 * D], yb[:, :], ALU.add))
                V.tensor_tensor(yb[:, :], p[:, 0:D], yb[:, :], ALU.add).then_inc(s_facc, 1)
                dve.wait_ge(s_facc, G.v + 1 + CREDIT)
                V.tensor_scalar(xs[:, :], yb[:, :], 0.0, None, ALU.max).then_inc(s_h, 1)
                dve.wait_ge(s_mm, MM3 + w.v + 1)
                link(V.tensor_tensor(yb[:, :], psA[:, 0:D], l3_b2[:, :], ALU.add))
                link(V.tensor_tensor(yb[:, :], yb[:, :], at_window(X, w), ALU.add))
                moments(link, yb[:, :])
                dve.wait_ge(s_std, VAR3 + w.v + 1)
                link(V.reciprocal(rstd[:, :], std[:, :]))
                dve.wait_ge(s_free, NW + w.v + 1)
                normalised(link, store[:, (NW + w.rest) % 2, 0:D], yb[:, :]).then_inc(s_store, 1)
                dve.wait_ge(s_store, NW + w.v + 1)
                link.end()
            windows(dve, L1_STEPS, l3, 6)

        @block.tensor
        def _(pe):
            mm = nc.tensor.matmul
            turn = nc.tensor.transpose
            pe.sem_inc(s_edge, CREDIT)
            pe.sem_inc(s_blk, RING)
            pe.sem_inc(s_agg, CREDIT)
            pe.sem_inc(s_fagg, 3)

            def histogram(i):
                at = i * 64
                h0 = i * HSTEPS

                def step(t, n, first=False, last=False):
                    par = t % 2
                    pe.wait_ge(s_hoh, n)
                    for j in range(HJ):
                        m = mm(psA[:, at:at + NW], hlo[0:EP, par, :, j], hhi[0:EP, par, :, j],
                               start=(first and j == 0), stop=(last and j == HJ - 1), skip_group_check=True)
                    m.then_inc(s_hmm, 1)
                step(h0, 2 * h0 + 2, first=True)
                with pe.Fori(0, (HSTEPS - 3) // 2) as j:
                    for t in (1, 2):
                        step(h0 + t, j * 4 + 2 * (h0 + t) + 2)
                for t in (HSTEPS - 2, HSTEPS - 1):
                    step(h0 + t, 2 * (h0 + t) + 2, last=(t == HSTEPS - 1))
            pe.wait_ge(s_const, N_CONST)
            histogram(0)
            pe.wait_ge(s_ind, 1)
            mm(psB[0:NW, 0:WB], indeg[:, :], ones[:, :], start=True, stop=True).then_inc(s_tot, 1)
            pe.wait_ge(s_in, 16 * len(LOADS))
            for j in range(4):
                turn(acc[:, 0, j * P:(j + 1) * P], wraw[:, j, :], ident[:, :])
            turn(acc[:, 1, 0:P], wraw[:, 4, :], ident[:, :]).then_inc(s_wT, 1)
            pe.wait_ge(s_totc, 1)
            mm(psB[0:WB, 64:64 + NW], tri[:, :], indeg[:, :], start=True, stop=False)
            mm(psB[0:WB, 64:64 + NW], tot[:, :], upper[:, :], start=False, stop=True).then_inc(s_off, 1)
            histogram(1)
            for c in range(NCH):
                pe.wait_ge(s_comb, c + 1)
                if c >= 2:
                    pe.wait_ge(s_ctc, 2 * (c - 1))
                for t in range(BT):
                    turn(pair[c % 2][:, 0, t * CB:(t + 1) * CB], comb_f[:, c, t * P:(t + 1) * P], ident[0:CB, 0:CB])
                for t in range(BT):
                    m = turn(pair[c % 2][:, 1, t * CB:(t + 1) * CB], lo_f[:, c, t * P:(t + 1) * P], ident[0:CB, 0:CB])
                m.then_inc(s_ct, 1)
            pe.wait_ge(s_be, 1)
            pe.wait_ge(s_wc, 2)
            mm(psA[:, 0:D], wT[:, 4, :], l3_w1b[:, :], start=True, stop=True)
            mm(psA[:, D:2 * D], be_bc[:, :], l3_w1b[:, :], start=True, stop=True).then_inc(s_fold, 1)
            pe.wait_ge(s_foldc, 2)
            pe.wait_ge(s_ctc, 2 * NCH)

            pe.sem_inc(s_evac, CREDIT)

            def l0(w, e):
                for b in range(WB):
                    if w is not None:
                        if b % 2 == 0:
                            pe.wait_ge(s_evac, w.v * (WB // 2) + b // 2 + 1)
                        pe.wait_ge(s_coh, w.v * (WB + 2) + b + 1 + (b // 8 + 1))
                        for t in range(BT):
                            m = mm(pair[(b // 2) % 2][:, b % 2, 0:BW], loh[:, b // 8, :, (b % 8) * BT + t], coh[:, b % RING, t, :],
                                   start=(t == 0), stop=(t == BT - 1))
                        m.then_inc(s_blk, 1)
                    if e is None:
                        continue
                    if b == 0:
                        pe.wait_ge(s_xs, e.v + 1)
                        turn(psB[:, 0:P], xs[:, :], ident[:, :]).then_inc(s_tp, 1)
                    if b == 2:
                        pe.wait_ge(s_tc, e.v * 4 + 3)
                        mm(psA[:, D2:2 * D2], xT[:, :], w1a, start=True, stop=True)
                        mm(psA[:, 0:D2], sT[:, :], w1b, start=True, stop=True).then_inc(s_mm, 1)
                    if b == 9:
                        pe.wait_ge(s_h, e.v + 1)
                        turn(psB[:, 0:P], hbuf[:, 0:P], ident[:, :]).then_inc(s_tp, 1)
                        turn(psB[:, P:2 * P], hbuf[:, P:2 * P], ident[:, :]).then_inc(s_tp, 1)
                    if b == 12:
                        pe.wait_ge(s_tc, e.v * 4 + 4)
                        mm(psA[:, 0:D], hT[:, 0, :], w2a, start=True, stop=False)
                        mm(psA[:, 0:D], hT[:, 1, :], w2b, start=False, stop=True).then_inc(s_mm, 1)
                if w is not None:
                    pe.wait_ge(s_oh0, w.v + 1)
                    pe.wait_ge(s_ea[w.mod(2)], (w.div(2) + 1) * 16)
                    for k in range(K):
                        m = mm(acc[:, w.mod(2), 0:P], ea[:, w.mod(2), k, :], oh[:, w.mod(2), k, :], start=(k == 0), stop=(k == K - 1))
                    m.then_inc(s_edge, 1)
            skewed(pe, l0, 2)

            pe.sem_inc(s_facc, CREDIT)

            def propagate(phase, z, width, pieces):
                def step(w, e):
                    if w is not None:
                        G = w.plus(phase * NW)
                        pe.wait_ge(s_facc, G.v + 1)
                        pe.wait_ge(s_a[G.mod(3)], (G.div(3) + 1) * 16)
                        if phase == L1_STEPS:
                            mm(acc[:, G.mod(2), 0:width], ident16[:, :], z[:, bass.ds(w.v, 1), :].rearrange("p a d -> p (a d)"),
                               start=True, stop=False)
                    for s in range(NW):
                        if w is not None:
                            m = mm(acc[:, G.mod(2), 0:width], aslot[:, G.mod(3), s, :], z[:, s, :],
                                   start=(s == 0 and phase < L1_STEPS), stop=(s == NW - 1))
                        if e is not None and s in pieces:
                            pieces[s](e)
                    if w is not None:
                        m.then_inc(s_fagg, 1)
                pe.wait_ge(s_z, (phase + 1) * NW)
                skewed(pe, step, 6)

            def l1_turn(e):
                pe.wait_ge(s_h, H1 + e.v * 2 + 1)
                turn(psB[:, 0:P], xs[:, :], ident[:, :]).then_inc(s_tp, 1)

            def l1_out(e):
                pe.wait_ge(s_tc, TC1 + e.v * 2 + 1)
                mm(psA[:, 0:D], xT[:, :], wT[:, 0, :], start=True, stop=True).then_inc(s_mm, 1)

            def l1_turn_x(e):
                pe.wait_ge(s_h, H1 + e.v * 2 + 2)
                turn(psB[:, 0:P], xs[:, :], ident[:, :]).then_inc(s_tp, 1)

            def l1_qkv(e):
                pe.wait_ge(s_tc, TC1 + e.v * 2 + 2)
                mm(psA[:, 0:3 * D], xT[:, :], wT[:, 1:4, :].rearrange("p a d -> p (a d)"), start=True, stop=True).then_inc(s_mm, 1)

            propagate(0, zp[0], D2, {})
            propagate(1, zp[1], D2, {})
            propagate(2, zp[0], D2, {10: l1_turn, 16: l1_out, 38: l1_turn_x, 44: l1_qkv})


            def expand(w):
                q_w = at_window(Q, w)
                pe.wait_ge(s_oh, w.v + 1)

                def turn_group(g):
                    a, b = GROUPS[g]
                    for k in range(a, b):
                        m = turn(pair[0][:, g % 2, (k - a) * P:(k - a + 1) * P], oh[:, w.mod(2), k, :], ident[:, :])
                    m.then_inc(s_qT, 1)
                turn_group(0)
                for g, (a, b) in enumerate(GROUPS):
                    if g + 1 < NG:
                        turn_group(g + 1)
                    pe.wait_ge(s_qTc, w.v * NG + g + 1)
                    for k in range(a, b):
                        m = mm(pair[1][:, g % 2, (k - a) * D:(k - a + 1) * D], ohT[:, g % 2, k - a, :], q_w, start=True, stop=True)
                    m.then_inc(s_qe, 1)
            expand(W(0, 0, 0))

            def l2(w, G):
                if w.unroll:
                    pe.wait_ge(s_prod, w.v + 1)
                    expand(w.plus(1))
                pe.wait_ge(s_msg, (w.v + 1) * 2)
                for k in range(K):
                    r = rows[:, w.mod(2), k * D2 + D - H:(k + 1) * D2]
                    m = mm(acc[:, w.mod(2), 0:D + H], oh[:, w.mod(2), k, :], r, start=(k == 0), stop=(k == K - 1))
                m.then_inc(s_agg, 1)
                pe.wait_ge(s_h, H2 + w.v + 1)
                turn(psA[:, 0:P], xs[:, :], ident[:, :]).then_inc(s_tp, 1)
                pe.wait_ge(s_tc, TC2 + w.v * 2 + 2)
                mm(psB[:, 0:D], xT[:, :], l3_w1a[:, :], start=True, stop=False)
                mm(psB[:, 0:D], sT[:, :], l3_m[:, :], start=False, stop=True).then_inc(s_mm, 1)
            windows(pe, 0, l2)

            def l3_turn(e):
                pe.wait_ge(s_h, H3 + e.v + 1)
                turn(psB[:, 0:P], xs[:, :], ident[:, :]).then_inc(s_tp, 1)

            def l3_out(e):
                pe.wait_ge(s_tc, TC3 + e.v + 1)
                mm(psA[:, 0:D], xT[:, :], l3_w2[:, :], start=True, stop=True).then_inc(s_mm, 1)
            propagate(L1_STEPS, yp, 3 * D, {14: l3_turn, 24: l3_out})


_INS = ['x', 'src', 'dst', 'edge_attr_128', 'L0_gnn_W1', 'L0_gnn_b1', 'L0_gnn_gamma', 'L0_gnn_beta', 'L0_gnn_prelu_a',
        'L0_gnn_W2', 'L0_gnn_b2', 'L1_gnn_W', 'L2_gnn_Wq', 'L2_gnn_bq', 'L2_gnn_Wk', 'L2_gnn_bk', 'L2_gnn_Wv', 'L2_gnn_bv',
        'L3_gnn_We', 'L3_gnn_be', 'L3_gnn_W1', 'L3_gnn_b1', 'L3_gnn_W2', 'L3_gnn_b2']


def kernel(**inputs):
    import numpy as _np
    import concourse.bacc as _bacc
    from concourse import mybir as _mybir
    from concourse.bass_utils import run_bass_kernel_spmd as _run

    nc = _bacc.Bacc("TRN2", target_bir_lowering=False, num_devices=1)
    arrays, args = {}, {}
    for name in _INS:
        a = _np.ascontiguousarray(inputs[name])
        arrays[f"in_{name}"] = a
        args[name] = nc.dram_tensor(f"in_{name}", a.shape, _mybir.dt.from_np(a.dtype), kind="ExternalInput").ap()
    out = nc.dram_tensor("out_0", (N, D), _mybir.dt.float32, kind="ExternalOutput").ap()
    build(nc, args, out)
    return _run(nc, [arrays], core_ids=[0]).results[0]["out_0"]
```

```python
import concourse.bass as bass
from concourse import mybir
from contextlib import ExitStack

N, E, D = 6250, 106250, 128
P = 128
NW = -(-N // P)
NPAD = NW * P
LAST = N - (NW - 1) * P
K = 19
CHUNK = K * P
H = 8
HD = D // H
D2 = 2 * D
EP, EJ = 125, 850
HJ = 34
HSTEPS = EJ // HJ
KM = K // 2 + 2
GROUPS = [(a, min(a + 4, K)) for a in range(0, K, 4)]
NG = len(GROUPS)
CREDIT = 2
L1_STEPS = 3

BN, BT = 8, 2
WB = P // BN
NB = NW * WB
BW = NW * BN
ROW = 32
BR = BT * P // ROW
ER = -(-E // ROW) + BR
CW = 7
NCH = NW // CW
CB = CW * WB
RING = 4
ZS = 64.0
FAR = 1024.0
RW = -(-E // CHUNK)
R = NW + RW

F32, I32 = mybir.dt.float32, mybir.dt.int32
F16, BF16 = mybir.dt.float16, mybir.dt.bfloat16
ALU = mybir.AluOpType
ACT = mybir.ActivationFunctionType
AXX = mybir.AxisListType.X


class Chain:

    def __init__(self, eng, sem, n, spare=None, base=0):
        self.eng, self.sem, self.n, self.spare, self.first, self.base, self.j = eng, sem, n, spare, base, base, 0

    def start(self, window, j=0):
        self.base, self.j = window * self.n + self.first, j

    def __call__(self, ins):
        self.j += 1
        ins.then_inc(self.sem, 1)
        self.eng.wait_ge(self.sem, self.base + self.j)

    def later(self, ins):
        self.j += 1
        ins.then_inc(self.sem, 1)

    def due(self):
        self.eng.wait_ge(self.sem, self.base + self.j)

    def due_held(self):
        self.due()
        self.eng.sem_inc(self.spare, 1)

    def held(self, ins):
        self(ins)
        self.eng.sem_inc(self.spare, 1)

    def end(self):
        assert self.j == self.n, (self.j, self.n)


class W:

    def __init__(self, i, rest, unroll):
        self.i, self.rest, self.unroll = i, rest, unroll
        self.v = i * unroll + rest if unroll else rest

    def mod(self, m):
        assert self.unroll % m == 0
        return self.rest % m

    def div(self, m):
        return self.i * (self.unroll // m) + self.rest // m if self.unroll else self.rest // m

    def plus(self, c):
        return W(self.i, self.rest + c, self.unroll)


def windows(eng, phase, body, unroll=2):
    with eng.Fori(0, (NW - 1) // unroll) as i:
        for h in range(unroll):
            body(W(i, h, unroll), W(i, phase * NW + h, unroll))
    last = W(0, NW - 1, 0)
    body(last, last.plus(phase * NW))


def rounds(eng, body):
    with eng.Fori(0, R) as r:
        body(r)


def skewed(eng, body, unroll):
    body(W(0, 0, 0), None)
    with eng.Fori(0, (NW - 1) // unroll) as i:
        for h in range(unroll):
            body(W(i, h + 1, unroll), W(i, h, unroll))
    body(None, W(0, NW - 1, 0))


def skewed_twice(eng, body):
    body(W(0, 0, 0), None, None)
    body(W(0, 1, 0), W(0, 0, 0), None)
    with eng.Fori(0, (NW - 3) // 2) as i:
        for h in range(2):
            body(W(i, h + 2, 2), W(i, h + 1, 2), W(i, h, 2))
    body(W(0, NW - 1, 0), W(0, NW - 2, 0), W(0, NW - 3, 0))
    body(None, W(0, NW - 1, 0), W(0, NW - 2, 0))
    body(None, None, W(0, NW - 1, 0))


def skewed_ahead(eng, body):
    body(W(0, 0, 0), None, 2)
    with eng.Fori(0, (NW - 3) // 2) as i:
        for h in range(2):
            body(W(i, h + 1, 2), W(i, h, 2), 2)
    body(W(0, NW - 2, 0), W(0, NW - 3, 0), 1)
    body(W(0, NW - 1, 0), W(0, NW - 2, 0), 0)
    body(None, W(0, NW - 1, 0), 0)


REP_FREE = 8 + 3 + 8 + 4 + 1 + NCH * 8 + 3 + 1


def build(nc, A, out):
    ctx = ExitStack()
    with ctx:
        def sb(name, shape, dt=F32):
            return ctx.enter_context(nc.sbuf_tensor(name, shape, dt))

        def sem(name):
            return ctx.enter_context(nc.semaphore(name))

        def dram(name, shape, dt=F32):
            return nc.dram_tensor(name, shape, dt).ap()

        ctx.enter_context(nc.allow_non_contiguous_dma(reason="small columns and tables, once"))

        kv_tab = dram("kv_tab", (NPAD, D2))
        edge_tab = dram("edge_tab", (ER, 2, ROW), I32)
        off_tab = dram("off_tab", (NB + 1,), I32)
        adj = dram("adj", (NW, P, NW, P), BF16)

        def carve(region, at, shape, dt=F32, parts=P):
            n = 1
            for x in shape:
                n *= x
            words = n * (2 if dt in (F16, BF16) else 4) // 4
            v = region[0:parts, at:at + words]
            if dt != F32:
                v = v.bitcast(dt)
            if len(shape) > 1:
                names = " ".join(f"d{i}" for i in range(len(shape)))
                v = v.rearrange(f"p ({names}) -> p {names}", **{f"d{i}": x for i, x in enumerate(shape)})
            return v, at + words

        X = sb("X", [P, NW, D])
        r_st = sb("r_st", [P, NW * P])
        r_zq = sb("r_zq", [P, 2 * NW * D])
        r_rows = sb("r_rows", [P, 2 * K * D2])
        r_oh = sb("r_oh", [P, 2 * K * P])
        r_tab = sb("r_tab", [P, NB * BT * 3 // 2])
        r_l0 = sb("r_l0", [P, K * P + D])
        rep, at = carve(r_st, 0, (P, HJ), BF16)
        pack, at = carve(r_st, at, (NCH, BR, 2 * ROW), I32, CB)
        lo_f, at = carve(r_zq, 0, (NCH, BT * P), F32, CB)
        comb_f, at = carve(r_zq, at, (NCH, BT * P), F32, CB)
        t_int, at = carve(r_zq, at, (BT * P,), I32, CB)
        t_a, at = carve(r_zq, at, (BT * P,), F32, CB)
        t_b, at = carve(r_zq, at, (BT * P,), F32, CB)
        hlo, at = carve(r_rows, 0, (2, P, HJ), BF16)
        hhi, at = carve(r_rows, at, (2, NW, HJ), BF16)
        flat_d, at = carve(r_oh, 0, (EJ,), I32)
        flat_s, at = carve(r_oh, at, (EJ,), I32)
        flat_i, at = carve(r_oh, at, (EJ,), I32)
        lo16, at = carve(r_oh, at, (2, EJ), BF16)
        hi16, at = carve(r_oh, at, (2, EJ), BF16)
        ST = r_st[:, :].rearrange("p (w n) -> p w n", n=P)
        ea, at = carve(r_rows, 0, (2, K, D))
        loh, at = carve(r_rows, at, (2, P, 8 * BT), BF16)
        rep_a, at = carve(r_rows, at, (P, 8 * BT), BF16)
        coh, at = carve(r_rows, at, (RING, BT, BW), BF16)
        assert at <= 2 * K * D2
        abuf, _ = carve(r_zq, NW * D, (2, NW, P), BF16)
        comb_t, at = carve(r_tab, 0, (NB * BT,))
        lo_t, at = carve(r_tab, at, (NB * BT,), BF16)
        zp = [carve(r_zq, b * NW * D, (NW, D2), F16)[0] for b in range(2)]
        Q, _ = carve(r_zq, NW * D, (NW, D))
        yp, _ = carve(r_zq, 0, (NW, 3 * D), BF16)
        aslot, at = carve(r_rows, 0, (3, NW, P), BF16)
        assert at <= 2 * K * D2
        rows = r_rows[:, :].rearrange("p (b n) -> p b n", b=2)
        oh = r_oh[:, :].rearrange("p (b k n) -> p b k n", b=2, n=P)
        ohT, _ = carve(r_tab, 0, (2, 4, P))
        qe = r_l0[:, 0:K * P].rearrange("p (k n) -> p k n", n=D)
        src_g, at = carve(r_rows, 0, (R, K), I32)
        dloc_g, at = carve(r_rows, at, (R, K))
        dst_g, _ = carve(r_rows, at, (R, K), I32)
        rows_g, at = carve(r_rows, at, (K * D2,))
        assert at <= 2 * K * D2
        oh_g, _ = carve(r_oh, 0, (K, P))
        sum_g, _ = carve(r_zq, 0, (NW, D))
        _, at = carve(r_tab, 0, (4, P))
        z_g, at = carve(r_tab, at, (NW, H))
        base_i, at = carve(r_tab, at, (R,), I32)
        win_i, at = carve(r_tab, at, (R,), I32)
        q_g, at = carve(r_tab, at, (D,))
        assert at <= NB * BT * 3 // 2
        prior, at = carve(r_zq, 0, (R, NW))
        at_round, at = carve(r_zq, at, (R, K))
        late, at = carve(r_zq, at, (R, K))
        first_g, at = carve(r_zq, at, (NW,))
        used_g, at = carve(r_zq, at, (NW,))
        step_g, at = carve(r_zq, at, (NW,))
        start_g, at = carve(r_zq, at, (R,))
        base_g, at = carve(r_zq, at, (R,))
        win_g, at = carve(r_zq, at, (R,))
        order, at = carve(r_zq, at, (R,))
        place, at = carve(r_zq, at, (K,))
        spread, at = carve(r_zq, at, (2, P))
        need, at = carve(r_zq, at, (RW + 1,))
        at = 0
        w1a, w1b, b1, gamma, beta, hbuf, hneg = (r_l0[:, D2 * i:D2 * i + D2] for i in range(7))
        w2a, w2b, b2 = (r_l0[:, 7 * D2 + D * i:7 * D2 + D * i + D] for i in range(3))
        hT = r_l0[:, 7 * D2 + 3 * D:7 * D2 + 5 * D].rearrange("p (a n) -> p a n", n=P)

        src_all = sb("src_all", [P, NW, K], I32)
        r_dst = sb("r_dst", [P, NW * K])
        dst_all, _ = carve(r_dst, 0, (NW, K), I32)
        dloc, _ = carve(r_dst, 0, (NW, K))
        idx_cur = sb("idx_cur", [P, 2, K], I32)
        comb_cur = sb("comb_cur", [P, 2, WB * BT])
        store = sb("store", [P, 2, D2])
        iota_f = sb("iota_f", [P, P])
        iota_b = sb("iota_b", [P, BW], F16)
        ident = sb("ident", [P, P])
        ident16 = sb("ident16", [P, P], BF16)
        wbase = sb("wbase", [P, NW])
        bbase = sb("bbase", [CB, NCH])
        ones = sb("ones", [P, WB])
        ones_row = sb("ones_row", [1, P])
        tri = sb("tri", [P, WB])
        upper = sb("upper", [NW, NW])
        indeg = sb("indeg", [P, NW])
        nin = sb("nin", [P, NW])
        inv_cnt = sb("inv_cnt", [P, NW])
        nout = sb("nout", [P, NW])
        clip = sb("clip", [P, 2, NW])
        tot = sb("tot", [NW, WB])
        off_i = sb("off_i", [WB, NW + 1], I32)
        first_i = sb("first_i", [1, NW], I32)
        blk_off = sb("blk_off", [CB, NCH], I32)
        blk_row = sb("blk_row", [CB, NCH], I32)
        blk_end = sb("blk_end", [CB, NCH], I32)
        over = sb("over", [P, NCH + 2])
        n_over = sb("n_over", [1, 1], I32)
        row_i = sb("row_i", [CB, NCH, BR], I32)
        eps_t = sb("eps_t", [P, 1])
        alpha = sb("alpha", [P, 1])
        wraw = sb("wraw", [P, 5, D])
        wT = sb("wT", [P, 5, D])
        bqkv = sb("bqkv", [P, 3 * D])
        l3_w1a = sb("l3_w1a", [P, D])
        l3_w1b = sb("l3_w1b", [P, D])
        l3_w2 = sb("l3_w2", [P, D])
        be_col = sb("be_col", [P, 1])
        be_bc = sb("be_bc", [P, P])
        l3_b1 = sb("l3_b1", [P, D])
        l3_b2 = sb("l3_b2", [P, D])
        l3_m = sb("l3_m", [P, D])
        l3_v = sb("l3_v", [P, D])
        xs = sb("xs", [P, D])
        xT = sb("xT", [P, P])
        sT = sb("sT", [P, P])
        stats = sb("stats", [P, 6])
        mv = sb("mv", [P, 2])
        std = sb("std", [P, 1])
        rstd = sb("rstd", [P, 1])
        yb = sb("yb", [P, D])
        yc = sb("yc", [P, D])
        zr = sb("zr", [P, H])
        sc = sb("sc", [P, K, H])
        empty = sb("empty", [BR + 1, 2 * ROW], I32)

        def pb(name, banks):
            return ctx.enter_context(nc.psum_tensor(name, [P, banks, 512], F32))
        acc = pb("acc", 2)
        pair = [pb("pair0", 2), pb("pair1", 2)]
        psA = pb("psA", 1)[:, 0, :]
        psB = pb("psB", 1)[:, 0, :]

        s_const = sem("constants_ready"); s_in = sem("weights_loaded"); s_edges = sem("edges_loaded")
        s_tab = sem("edge_table_written"); s_empty = sem("empty_rows_written")
        s_wT = sem("weights_transposed"); s_wc = sem("weights_copied")
        s_be = sem("be_spread"); s_fold = sem("l3_folded"); s_foldc = sem("l3_fold_copied")
        s_hoh = sem("hist_onehots"); s_hmm = sem("hist_products"); s_ind = sem("indegree_copied")
        s_tot = sem("window_totals"); s_totc = sem("window_totals_copied"); s_off = sem("offsets_summed")
        s_first = sem("first_edges_ready"); s_offw = sem("offsets_written"); s_offr = sem("block_offsets_loaded")
        s_rowi = sem("block_rows_ready"); s_pack = sem("block_edges_gathered")
        s_comb = sem("block_tables_ready"); s_ct = sem("block_tables_transposed"); s_ctc = sem("block_tables_copied")
        s_over = sem("lengths_compared"); s_nover = sem("too_long_counted"); s_case = sem("case_known")
        s_rep = sem("repeated_iota_ready"); s_win = sem("window_indices_loaded"); s_histd = sem("histograms_read")
        s_clip = sem("degrees_clipped"); s_sqrt = sem("degree_roots_ready"); s_setup = sem("dve_setup_step")
        s_ea = [sem(f"edge_rows_loaded{i}") for i in range(2)]
        s_oh0 = sem("l0_onehot_ready"); s_edge = sem("edge_features_summed"); s_coh = sem("block_onehots_ready")
        s_blk = sem("blocks_counted"); s_evac = sem("block_pairs_copied"); s_ab = sem("adjacency_stored")
        s_abf = sem("adjacency_buffer_free"); s_spare = sem("carries_a_wait"); s_dve = sem("dve_step")
        s_xs = sem("l0_x_copied"); s_xw = sem("l0_x_product_copied"); s_tp = sem("pe_transposed"); s_tc = sem("transposes_copied")
        s_mm = sem("pe_product_ready"); s_var = sem("variance_ready"); s_std = sem("std_ready")
        s_h = sem("hidden_ready"); s_h2 = sem("be_term_ready"); s_yp = sem("y_part_step"); s_cols = sem("block_columns_ready"); s_z = sem("propagated_row_ready")
        s_a = [sem(f"adjacency_loaded{i}") for i in range(3)]
        s_fagg = sem("propagated"); s_facc = sem("propagated_read")
        s_idx = sem("gather_indices_ready"); s_gat = [sem(f"rows_gathered{i}") for i in range(2)]
        s_oh = sem("l2_onehot_ready"); s_agg = sem("l2_aggregated"); s_qT = sem("onehots_transposed")
        s_qTc = sem("onehotT_copied"); s_qe = sem("queries_expanded"); s_qec = sem("queries_copied")
        s_prod = sem("qk_products_ready"); s_raw = sem("scores_summed"); s_sc = sem("scores_ready"); s_exp = sem("exp_ready"); s_msg = sem("messages_ready")
        s_store = sem("rows_to_store"); s_stored = sem("rows_stored"); s_free = sem("store_buffer_free")

        g_dve = sem("g_dve_step"); g_ready = sem("g_counts_spread"); g_sum = sem("g_counts_summed"); g_const = sem("g_constants")
        g_tab = sem("g_rounds_known"); g_win = sem("g_round_indices_loaded"); g_ea = sem("g_edge_rows_loaded")
        g_oh = sem("g_onehot_ready"); g_gat = [sem(f"g_rows_gathered{i}") for i in range(L1_STEPS + 2)]
        g_agg = sem("g_round_summed"); g_used = sem("g_round_added"); g_qT = sem("g_onehots_transposed")
        g_qTc = sem("g_onehotT_copied"); g_qe = sem("g_queries_expanded"); g_qec = sem("g_queries_copied")
        g_sc = sem("g_scores_ready"); g_exp = sem("g_exp_ready"); g_msg = sem("g_messages_ready")

        def bc_row(v, n):
            return v.rearrange("(a n) -> a n", a=1).to_broadcast([P, n])

        LOADS = [(w1a, A["L0_gnn_W1"][0:P, :]), (w1b, A["L0_gnn_W1"][P:2 * P, :]),
                 (w2a, A["L0_gnn_W2"][0:P, :]), (w2b, A["L0_gnn_W2"][P:2 * P, :]),
                 (b1, bc_row(A["L0_gnn_b1"], D2)), (gamma, bc_row(A["L0_gnn_gamma"], D2)),
                 (beta, bc_row(A["L0_gnn_beta"], D2)), (alpha[:, :], bc_row(A["L0_gnn_prelu_a"], 1)),
                 (b2, bc_row(A["L0_gnn_b2"], D)),
                 (wraw[:, 0, :], A["L1_gnn_W"]), (wraw[:, 1, :], A["L2_gnn_Wq"]), (wraw[:, 2, :], A["L2_gnn_Wk"]),
                 (wraw[:, 3, :], A["L2_gnn_Wv"]), (wraw[:, 4, :], A["L3_gnn_We"]),
                 (bqkv[:, 0:D], bc_row(A["L2_gnn_bq"], D)), (bqkv[:, D:2 * D], bc_row(A["L2_gnn_bk"], D)),
                 (bqkv[:, 2 * D:3 * D], bc_row(A["L2_gnn_bv"], D)),
                 (l3_w1a[:, :], A["L3_gnn_W1"][0:P, :]), (l3_w1b[:, :], A["L3_gnn_W1"][P:2 * P, :]),
                 (l3_w2[:, :], A["L3_gnn_W2"]), (be_col[:, :], A["L3_gnn_be"].rearrange("(p a) -> p a", a=1)),
                 (l3_b1[:, :], bc_row(A["L3_gnn_b1"], D)), (l3_b2[:, :], bc_row(A["L3_gnn_b2"], D)),
                 *[(X[:, w:w + 6, :], A["x"][w * P:(w + 6) * P, :].rearrange("(w p) d -> p w d", p=P))
                   for w in range(0, NW - 1, 6)],
                 (X[0:LAST, NW - 1, :], A["x"][(NW - 1) * P:N, :])]
        N_CONST = 11
        TP1, TC1, MM1, VAR1, H1 = 3 * NW, 4 * NW, 2 * NW, 2 * NW, NW
        TP2, TC2, MM2, VAR2, H2 = 5 * NW, 6 * NW, 4 * NW, 3 * NW, 3 * NW
        TP3, TC3, MM3, VAR3, H3 = 6 * NW, 8 * NW, 5 * NW, 4 * NW, 4 * NW

        def at_window(t, w):
            return t[:, bass.ds(w.v, 1), :].rearrange("p a d -> p (a d)")

        def column(t, w):
            return t[:, bass.ds(w.v, 1)]

        def too_long(eng):
            eng.wait_ge(s_case, 1)
            return eng.value_load(n_over[0:1, 0:1], min_val=0, max_val=NB + NW)

        def of_round(t, r):
            return t[:, bass.ds(r, 1), :].rearrange("p a k -> p (a k)")

        block = ctx.enter_context(nc.Block())

        @block.sync
        def _(sp):
            sp.sem_inc(s_abf, CREDIT)
            sp.dma_start(flat_d[0:EP, :], A["dst"].rearrange("(p j) -> p j", p=EP)).then_inc(s_edges, 16)
            sp.wait_ge(s_edges, 16)
            sp.sem_inc(s_spare, 1)
            sp.dma_start(flat_s[0:EP, :], A["src"].rearrange("(p j) -> p j", p=EP)).then_inc(s_edges, 16)
            full = E // ROW
            sp.wait_ge(s_const, N_CONST)
            sp.dma_start(edge_tab[full:ER, :, :].rearrange("r a n -> r (a n)"), empty[0:ER - full, :]).then_inc(s_empty, 16)
            for i, name in enumerate(("src", "dst")):
                sp.dma_start(edge_tab[0:full, i, :], A[name][0:full * ROW].rearrange("(r n) -> r n", n=ROW)).then_inc(s_tab, 16)
            sp.wait_ge(s_empty, 16)
            for i, name in enumerate(("src", "dst")):
                sp.dma_start(edge_tab[full:full + 1, i, 0:E - full * ROW],
                             A[name][full * ROW:E].rearrange("(r n) -> r n", r=1)).then_inc(s_tab, 16)
            for dst_ap, src_ap in LOADS:
                sp.dma_start(dst_ap, src_ap).then_inc(s_in, 16)
            sp.wait_ge(s_first, 3)
            sp.dma_start(off_tab[0:NB].rearrange("(w m) -> m w", m=WB), off_i[:, 0:NW]).then_inc(s_offw, 16)
            sp.dma_start(off_tab[NB:NB + 1].rearrange("(a n) -> a n", a=1), off_i[0:1, NW:NW + 1]).then_inc(s_offw, 16)
            sp.wait_ge(s_offw, 2 * 16)
            sp.dma_start(blk_off[:, :], off_tab[0:NB].rearrange("(c p) -> p c", p=CB)).then_inc(s_offr, 16)
            sp.dma_start(blk_end[:, :], off_tab[1:NB + 1].rearrange("(c p) -> p c", p=CB)).then_inc(s_offr, 16)

            def load_window(w, G):
                first = sp.value_load(first_i[0:1, bass.ds(w.v, 1)], min_val=0, max_val=E - CHUNK)
                for dst_ap, name in ((src_all, "src"), (dst_all, "dst")):
                    sp.dma_start(at_window(dst_ap, w),
                                 A[name][bass.ds(first, CHUNK)].rearrange("(p k) -> p k", p=P)).then_inc(s_win, 16)
            windows(sp, 0, load_window)

            def usual_case():
                def store_adjacency(w, G):
                    sp.wait_ge(s_evac, (w.v + 1) * (WB // 2) + CREDIT)
                    sp.dma_start(adj[bass.ds(w.v, 1), :, :, :].rearrange("a p w n -> p (a w n)"),
                                 abuf[:, w.mod(2), :, :].rearrange("p w n -> p (w n)")).then_inc(s_ab, 16)
                    sp.wait_ge(s_ab, (w.v + 1) * 16)
                    sp.sem_inc(s_abf, 1)
                windows(sp, 0, store_adjacency)

                def load_adjacency(w, G):
                    sp.wait_ge(s_fagg, G.v + 1)
                    sp.dma_start(aslot[:, G.mod(3), :, :].rearrange("p w n -> p (w n)"),
                                 adj[bass.ds(w.v, 1), :, :, :].rearrange("a p w n -> p (a w n)")).then_inc(s_a[G.mod(3)], 16)
                sp.wait_ge(s_edge, NW + CREDIT)
                for phase in range(L1_STEPS):
                    windows(sp, phase, load_adjacency, 6)
                sp.wait_ge(s_agg, NW + CREDIT)
                windows(sp, L1_STEPS, load_adjacency, 6)

            def any_case():
                def load_round(r):
                    first = sp.value_load(base_i[0:1, bass.ds(r, 1)], min_val=0, max_val=E - CHUNK)
                    for dst_ap, name in ((src_g, "src"), (dst_g, "dst")):
                        sp.dma_start(of_round(dst_ap, r),
                                     A[name][bass.ds(first, CHUNK)].rearrange("(p k) -> p k", p=P)).then_inc(g_win, 16)
                sp.wait_ge(g_tab, 1)
                rounds(sp, load_round)

                def load_features(r):
                    sp.wait_ge(g_used, r + 1)
                    first = sp.value_load(base_i[0:1, bass.ds(r, 1)], min_val=0, max_val=E - CHUNK)
                    sp.dma_start(rows_g[:, 0:K * D],
                                 A["edge_attr_128"][bass.ds(first, CHUNK), :].rearrange("(p k) d -> p (k d)", p=P)
                                 ).then_inc(g_ea, 16)
                rounds(sp, load_features)
            n = too_long(sp)
            with sp.If(n == 0):
                usual_case()
            with sp.Else():
                any_case()
            sp.sem_inc(s_spare, 1)

        @block.gpsimd
        def _(pool):
            pool.sem_inc(s_free, CREDIT)
            small = dict(channel_multiplier=0, allow_small_or_imprecise_dtypes=True)
            nc.gpsimd.iota(rep[:, :, :], pattern=[[1, P], [0, HJ]], base=0, **small).then_inc(s_const, 1)
            nc.gpsimd.memset(X[:, NW - 1, :], 0.0).then_inc(s_const, 1)
            nc.gpsimd.memset(ident[:, :], 0.0).then_inc(s_const, 1)
            nc.gpsimd.memset(tri[:, :], 1.0).then_inc(s_const, 1)
            nc.gpsimd.memset(upper[:, :], 1.0).then_inc(s_const, 1)
            nc.gpsimd.memset(empty[:, :], -1).then_inc(s_const, 1)
            pool.wait_ge(s_const, 6)
            nc.gpsimd.affine_select(out=ident[:, :], in_=ident[:, :], compare_op=ALU.not_equal, fill=1.0,
                                    base=0, pattern=[[-1, P]], channel_multiplier=1).then_inc(s_const, 1)
            nc.gpsimd.affine_select(out=tri[:, :], in_=tri[:, :], compare_op=ALU.is_gt, fill=0.0,
                                    base=0, pattern=[[BN, WB]], channel_multiplier=-1).then_inc(s_const, 1)
            nc.gpsimd.affine_select(out=upper[:, :], in_=upper[:, :], compare_op=ALU.is_gt, fill=0.0,
                                    base=0, pattern=[[1, NW]], channel_multiplier=-1).then_inc(s_const, 1)
            nc.gpsimd.iota(wbase[:, :], pattern=[[P, NW]], base=0, **small).then_inc(s_const, 1)
            nc.gpsimd.iota(bbase[:, :], pattern=[[CB * BN, NCH]], base=0, channel_multiplier=BN,
                           allow_small_or_imprecise_dtypes=True).then_inc(s_const, 1)
            nc.gpsimd.iota(iota_f[:, :], pattern=[[1, P]], base=0, **small).then_inc(s_rep, 1)
            nc.gpsimd.iota(iota_b[:, :], pattern=[[1, BW]], base=0, **small).then_inc(s_rep, 1)
            pool.wait_ge(s_rowi, 1)
            pool.wait_ge(s_tab, 4 * 16)
            for c in range(NCH):
                for j in range(BR):
                    pool.indirect_dma_start(pack[:, c, j, :], None, edge_tab.rearrange("r a n -> r (a n)"),
                                            bass.IndirectOffsetOnAxis(ap=row_i[:, c, j:j + 1], axis=0)).then_inc(s_pack, 16)
            def store_rows(phase, target):
                def store_window(w, G):
                    last = w.unroll == 0
                    n = LAST if last and target is out else P
                    width = D if target is out else D2
                    dst_ap = target[w.v * P:w.v * P + n, :] if last else target[bass.ds(w.v * P, P), :]
                    pool.wait_ge(s_store, G.v + 1)
                    pool.sem_inc(s_spare, 1)
                    pool.dma_start(dst_ap, store[0:n, G.mod(2), 0:width]).then_inc(s_stored, 16)
                    pool.wait_ge(s_stored, (G.v + 1) * 16)
                    pool.sem_inc(s_free, 1)
                windows(pool, phase, store_window)

            def usual_case():
                pool.wait_ge(s_histd, 2)
                pool.wait_ge(s_setup, REP_FREE)
                nc.gpsimd.iota(rep_a[:, :, :], pattern=[[1, P], [0, 8 * BT]], base=0, **small).then_inc(s_rep, 1)

                store_rows(0, kv_tab)

                def gather_window(w, G):
                    pool.wait_ge(s_idx, w.v + 1)
                    pool.wait_ge(s_agg, w.v + 1)
                    pool.sem_inc(s_spare, 1)
                    for k in range(K):
                        pool.indirect_dma_start(rows[:, w.mod(2), k * D2:(k + 1) * D2], None, kv_tab,
                                                bass.IndirectOffsetOnAxis(ap=idx_cur[:, w.mod(2), k:k + 1], axis=0)
                                                ).then_inc(s_gat[w.mod(2)], 16)
                windows(pool, 0, gather_window)
                store_rows(1, out)

            def any_case():
                pool.wait_ge(s_ctc, 2 * NCH)
                nc.gpsimd.iota(order[:, :], pattern=[[1, R]], base=0, **small).then_inc(g_const, 1)
                nc.gpsimd.iota(need[:, 0:RW], pattern=[[CHUNK, RW]], base=0, **small).then_inc(g_const, 1)
                nc.gpsimd.iota(place[:, :], pattern=[[1, K]], base=0, channel_multiplier=K,
                               allow_small_or_imprecise_dtypes=True).then_inc(g_const, 1)

                def gather_rounds(phase):
                    pool.wait_ge(s_free, (phase + 1) * NW + CREDIT)

                    def gather_round(r):
                        pool.wait_ge(g_oh, (phase + 1) * (R + 1) + 2 + r)
                        pool.sem_inc(s_spare, 1)
                        for k in range(K):
                            pool.indirect_dma_start(rows_g[:, k * D2:(k + 1) * D2], None, kv_tab,
                                                    bass.IndirectOffsetOnAxis(ap=idx_cur[:, 0, k:k + 1], axis=0)
                                                    ).then_inc(g_gat[phase], 16)
                    rounds(pool, gather_round)
                for phase in range(L1_STEPS + 2):
                    store_rows(phase, kv_tab)
                    gather_rounds(phase)
                store_rows(L1_STEPS + 2, out)
            n = too_long(pool)
            with pool.If(n == 0):
                usual_case()
            with pool.Else():
                any_case()
            pool.sem_inc(s_spare, 1)

        @block.scalar
        def _(act):
            copy = nc.scalar.copy
            act.wait_ge(s_wT, 1)
            copy(wT[:, 0:4, :].rearrange("p a d -> p (a d)"), acc[:, 0, :]).then_inc(s_wc, 1)
            copy(wT[:, 4, :], acc[:, 1, 0:D]).then_inc(s_wc, 1)
            act.wait_ge(s_tot, 1)
            copy(tot[:, :], psB[0:NW, 0:WB]).then_inc(s_totc, 1)
            for c in range(NCH):
                cols = slice(c * CB * BT, (c + 1) * CB * BT)
                act.wait_ge(s_ct, c + 1)
                for t, table in ((0, comb_t), (1, lo_t)):
                    copy(table[:, cols].rearrange("p (b t) -> p b t", t=BT),
                         pair[c % 2][:, t, 0:BT * CB].rearrange("p (t b) -> p b t", t=BT)).then_inc(s_ctc, 1)
            act.wait_ge(s_clip, 1)
            nc.scalar.activation(clip[:, :, :], clip[:, :, :], ACT.Sqrt).then_inc(s_sqrt, 1)
            act.wait_ge(s_fold, 1)
            copy(l3_m[:, :], psA[:, 0:D]).then_inc(s_foldc, 1)
            copy(l3_v[:, :], psA[:, D:2 * D]).then_inc(s_foldc, 1)

            def load_edges(w):
                act.wait_ge(s_edge, w.v + 1)
                first = act.value_load(first_i[0:1, bass.ds(w.v, 1)], min_val=0, max_val=E - CHUNK)
                act.dma_start(ea[:, w.mod(2), :, :].rearrange("p k d -> p (k d)"),
                              A["edge_attr_128"][bass.ds(first, CHUNK), :].rearrange("(p k) d -> p (k d)", p=P)
                              ).then_inc(s_ea[w.mod(2)], 16)

            def std_of(n):
                act.wait_ge(s_var, n)
                nc.scalar.activation(std[:, :], mv[:, 1:2], ACT.Sqrt, bias=eps_t[:, :]).then_inc(s_std, 1)

            def count_pair(w, q):
                act.wait_ge(s_blk, w.v * WB + 2 * q + 2 + RING)
                v = abuf[:, w.mod(2), :, 2 * q * BN:(2 * q + 2) * BN].rearrange("p w (b n) -> p b w n", b=2)
                copy(v, pair[q % 2][:, :, 0:BW].rearrange("p b (w n) -> p b w n", n=BN)).then_inc(s_evac, 1)

            def l0(w, e, f, summed=True):
                if f is not None:
                    act.wait_ge(s_tp, f.v * 3 + 3 if e is None else e.v * 3 + 1)
                    copy(hT[:, :, :], psB[:, 0:2 * P].rearrange("p (a n) -> p a n", n=P)).then_inc(s_tc, 1)
                if e is not None:
                    act.wait_ge(s_tp, e.v * 3 + 1)
                    copy(xT[:, :], psB[:, D2 + D:2 * D2]).then_inc(s_tc, 1)
                    if summed:
                        act.wait_ge(s_edge, e.v + 1 + CREDIT)
                        copy(sT[:, :], acc[:, e.mod(2), 0:P]).then_inc(s_tc, 1)
                        copy(at_window(ST, e), acc[:, e.mod(2), 0:P]).then_inc(s_tc, 1)
                    else:
                        copy(sT[:, :], at_window(ST, e)).then_inc(s_tc, 1)
                        act.sem_inc(s_tc, 1)
                if w is not None:
                    act.wait_ge(s_abf, w.v + 1)
                for q in range(WB // 2):
                    if e is not None and q == 2:
                        act.wait_ge(s_mm, e.v * 2 + 1)
                        copy(hneg, psA[:, D2:2 * D2]).then_inc(s_xw, 1)
                    if w is not None and q == 1 and (w.unroll or w.rest < NW - 1):
                        load_edges(w.plus(1))
                    if f is not None and q == 1:
                        std_of(f.v * 2 + 2)
                    if e is not None and q == 4:
                        std_of(e.v * 2 + 1)
                    if w is not None:
                        if q == 6:
                            copy(xs[:, :], at_window(X, w)).then_inc(s_xs, 1)
                        count_pair(w, q)
            act.wait_ge(s_first, 3)
            act.wait_ge(s_in, 16 * len(LOADS))

            def l1_last(w, G):
                act.wait_ge(s_tp, TP1 + w.v * 2 + 1)
                copy(xT[:, :], psB[:, 0:P]).then_inc(s_tc, 1)
                std_of(VAR1 + w.v + 1)
                act.wait_ge(s_tp, TP1 + w.v * 2 + 2)
                copy(xT[:, :], psB[:, 0:P]).then_inc(s_tc, 1)
            def indices(w):
                copy(idx_cur[:, w.mod(2), :], at_window(src_all, w)).then_inc(s_idx, 1)

            def expand(w, first, last):
                def queries(g):
                    a, b = GROUPS[g]
                    act.wait_ge(s_qe, w.v * NG + g + 1)
                    copy(qe[:, a:b, :].rearrange("p k n -> p (k n)"), pair[1][:, g % 2, 0:(b - a) * D]).then_inc(s_qec, 1)
                for g in range(first, last):
                    if g >= 2:
                        queries(g - 2)
                    if g < NG:
                        a, b = GROUPS[g]
                        act.wait_ge(s_qT, w.v * NG + g + 1)
                        copy(ohT[:, g % 2, 0:b - a, :].rearrange("p k n -> p (k n)"),
                             pair[0][:, g % 2, 0:(b - a) * P]).then_inc(s_qTc, 1)

            def l2_end(w, G, root=True):
                if root:
                    std_of(VAR2 + w.v + 1)
                act.wait_ge(s_tp, TP2 + w.v + 1)
                copy(xT[:, :], psA[:, 0:P]).then_inc(s_tc, 1)
                copy(sT[:, :], at_window(ST, w)).then_inc(s_tc, 1)

            def l2(w, e, ahead):
                if ahead:
                    expand(w.plus(1), 0, 2)
                    act.wait_ge(s_prod, w.v + 1)
                    expand(w.plus(1), 2, 4)
                if w is not None:
                    act.wait_ge(s_sc, w.v + 1)
                    s_at = rows[:, w.mod(2), :].rearrange("p (k n) -> p k n", n=D2)[:, :, D - H:D]
                    nc.scalar.activation(s_at, sc[:, :, :], ACT.Exp, scale=1.0 / HD ** 0.5).then_inc(s_exp, 1)
                if ahead == 2:
                    indices(w.plus(2))
                if e is not None:
                    std_of(VAR2 + e.v + 1)
                if ahead:
                    expand(w.plus(1), 4, NG + 2)
                if e is not None:
                    l2_end(e, e, root=False)

            def l3(w, G):
                act.wait_ge(s_tp, TP3 + w.v + 1)
                copy(xT[:, :], psB[:, 0:P]).then_inc(s_tc, 1)
                std_of(VAR3 + w.v + 1)

            def usual_case():
                load_edges(W(0, 0, 0))
                skewed_twice(act, l0)
                windows(act, 0, l1_last)
                w0 = W(0, 0, 0)
                act.wait_ge(s_mm, MM2)
                indices(w0)
                indices(w0.plus(1))
                expand(w0, 0, NG + 2)
                skewed_ahead(act, l2)
                windows(act, 0, l3)

            def any_case():
                act.wait_ge(g_used, R + 1)

                def l0_window(w, G):
                    copy(xs[:, :], at_window(X, w)).then_inc(s_xs, 1)
                    l0(None, w, None, summed=False)
                    l0(None, None, w)
                windows(act, 0, l0_window)
                windows(act, 0, l1_last)

                def attend_round(r):
                    for g, (a, b) in enumerate(GROUPS):
                        act.wait_ge(g_qT, r * NG + g + 1)
                        copy(ohT[:, 0, 0:b - a, :].rearrange("p k n -> p (k n)"), pair[0][:, 0, 0:(b - a) * P]).then_inc(g_qTc, 1)
                        act.wait_ge(g_qe, r * NG + g + 1)
                        copy(qe[:, a:b, :].rearrange("p k n -> p (k n)"), pair[1][:, 0, 0:(b - a) * D]).then_inc(g_qec, 1)
                    act.wait_ge(g_sc, r + 1)
                    s_at = rows_g[:, :].rearrange("p (k n) -> p k n", n=D2)[:, :, D - H:D]
                    nc.scalar.activation(s_at, sc[:, :, :], ACT.Exp, scale=1.0 / HD ** 0.5).then_inc(g_exp, 1)
                rounds(act, attend_round)
                windows(act, 0, l2_end)
                windows(act, 0, l3)
            n = too_long(act)
            with act.If(n == 0):
                usual_case()
            with act.Else():
                any_case()
            act.sem_inc(s_spare, 1)

        @block.vector
        def _(dve):
            V = nc.vector
            setup = Chain(dve, s_setup, 0)

            V.memset(eps_t[:, :], 1e-5).then_inc(s_spare, 1)
            setup(V.memset(ones[:, :], 1.0))
            setup(V.memset(ones_row[:, :], 1.0))
            dve.wait_ge(s_const, N_CONST)
            setup(V.tensor_copy(ident16[:, :], ident[:, :]))

            def split_nodes(i, flat):
                dve.wait_ge(s_edges, 16 * (i + 1))
                f = flat[0:EP, :]
                setup(V.tensor_scalar(flat_i[0:EP, :], f, 7, None, ALU.arith_shift_right))
                setup(V.tensor_copy(hi16[0:EP, i, :], flat_i[0:EP, :]))
                setup(V.tensor_scalar(flat_i[0:EP, :], f, P - 1, None, ALU.bitwise_and))
                setup(V.tensor_copy(lo16[0:EP, i, :], flat_i[0:EP, :]))

            def histogram(i):
                def onehots(col, par):
                    V.tensor_tensor(hlo[0:EP, par, :, :], lo16[0:EP, i, col].unsqueeze(1).to_broadcast([EP, P, HJ]),
                                    rep[0:EP, :, :], ALU.is_equal).then_inc(s_hoh, 1)
                    V.tensor_tensor(hhi[0:EP, par, :, :], hi16[0:EP, i, col].unsqueeze(1).to_broadcast([EP, NW, HJ]),
                                    rep[0:EP, 0:NW, :], ALU.is_equal).then_inc(s_hoh, 1)
                h0 = i * HSTEPS
                if i == 0:
                    onehots(slice(0, HJ), 0)
                    onehots(slice(HJ, 2 * HJ), 1)
                else:
                    for t in range(2):
                        dve.wait_ge(s_hmm, h0 + t - 1)
                        onehots(slice(t * HJ, (t + 1) * HJ), (h0 + t) % 2)
                with dve.Fori(0, (HSTEPS - 3) // 2) as j:
                    for t in (2, 3):
                        dve.wait_ge(s_hmm, j * 2 + (h0 + t - 1))
                        onehots(bass.ds(j * (2 * HJ) + t * HJ, HJ), (h0 + t) % 2)
                t = HSTEPS - 1
                dve.wait_ge(s_hmm, h0 + t - 1)
                onehots(slice(t * HJ, (t + 1) * HJ), (h0 + t) % 2)
            split_nodes(0, flat_d)
            histogram(0)
            dve.wait_ge(s_hmm, HSTEPS)
            V.tensor_copy(indeg[:, :], psA[:, 0:NW]).then_inc(s_ind, 1)
            dve.wait_ge(s_off, 1)
            V.tensor_scalar(first_i[:, :], psB[0:1, 64:64 + NW], float(E - CHUNK), None, ALU.min).then_inc(s_first, 1)
            V.tensor_copy(off_i[:, 0:NW], psB[0:WB, 64:64 + NW]).then_inc(s_first, 1)
            V.memset(off_i[:, NW:NW + 1], E).then_inc(s_first, 1)
            split_nodes(1, flat_s)
            dve.wait_ge(s_offr, 2 * 16)
            setup(V.tensor_scalar(blk_row[:, :], blk_off[:, :], 5, None, ALU.arith_shift_right))
            for j in range(BR - 1):
                setup(V.tensor_scalar(row_i[:, :, j], blk_row[:, :], float(j), None, ALU.add))
            V.tensor_scalar(row_i[:, :, BR - 1], blk_row[:, :], float(BR - 1), None, ALU.add).then_inc(s_rowi, 1)
            setup(V.memset(over[:, :], 0.0))
            setup(V.scalar_tensor_tensor(over[0:CB, 0:NCH], blk_row[:, :], -float(ROW), blk_end[:, :], ALU.mult, ALU.add))
            setup(V.tensor_scalar(over[0:CB, 0:NCH], over[0:CB, 0:NCH], float(BT * P), None, ALU.is_gt))
            setup(V.tensor_reduce(over[0:CB, NCH:NCH + 1], over[0:CB, 0:NCH], AXX, ALU.add))
            V.tensor_scalar(over[0:NW, NCH + 1:NCH + 2], tot[:, 0:1], float(CHUNK), None, ALU.is_gt).then_inc(s_over, 1)
            histogram(1)
            dve.wait_ge(s_nover, 1)
            V.tensor_copy(n_over[:, :], psB[0:1, 160:161]).then_inc(s_case, 1)
            dve.wait_ge(s_hmm, 2 * HSTEPS)
            V.tensor_scalar(clip[:, 0, :], indeg[:, :], 1.0, None, ALU.max).then_inc(s_histd, 1)
            V.tensor_scalar(clip[:, 1, :], psA[:, 64:64 + NW], 1.0, None, ALU.max).then_inc(s_histd, 1)
            dve.wait_ge(s_histd, 2)
            setup(V.reciprocal(inv_cnt[:, :], clip[:, 0, :]))
            for c in range(NCH):
                dve.wait_ge(s_pack, NCH * BR * 16)
                s_v = pack[:, c, :, 0:ROW]
                d_v = pack[:, c, :, ROW:2 * ROW]
                ti = t_int[:, :].rearrange("p (r n) -> p r n", n=ROW)
                ta = t_a[:, :].rearrange("p (r n) -> p r n", n=ROW)
                setup(V.tensor_scalar(ti, s_v, P - 1, None, ALU.bitwise_and))
                setup(V.tensor_copy(lo_f[:, c, :], t_int[:, :]))
                setup(V.tensor_scalar(ti, s_v, 7, None, ALU.arith_shift_right))
                setup(V.tensor_scalar(ta, d_v, bbase[:, c:c + 1], None, ALU.subtract))
                setup(V.scalar_tensor_tensor(comb_f[:, c, :], t_int[:, :], float(BN), t_a[:, :], ALU.mult, ALU.add))
                setup(V.tensor_scalar(t_b[:, :], t_a[:, :], 0.0, FAR, ALU.is_lt, ALU.mult))
                setup(V.tensor_tensor(comb_f[:, c, :], comb_f[:, c, :], t_b[:, :], ALU.add))
                setup(V.tensor_scalar(t_b[:, :], t_a[:, :], float(BN) - 0.5, FAR, ALU.is_gt, ALU.mult))
                V.tensor_tensor(comb_f[:, c, :], comb_f[:, c, :], t_b[:, :], ALU.add).then_inc(s_comb, 1)
                dve.wait_ge(s_comb, c + 1)
            V.tensor_copy(clip[:, 0, 0:1], clip[:, 0, 0:1]).then_inc(s_clip, 1)
            dve.wait_ge(s_sqrt, 1)
            setup(V.reciprocal(clip[:, :, :], clip[:, :, :]))
            setup(V.tensor_scalar(nin[:, :], clip[:, 0, :], 0.5 / ZS, None, ALU.mult))
            setup(V.tensor_scalar(nout[:, :], clip[:, 1, :], ZS, None, ALU.mult))
            dve.wait_ge(s_in, 16 * len(LOADS))
            V.tensor_copy(be_bc[:, :], be_col[:, :].to_broadcast([P, P])).then_inc(s_be, 1)
            dve.wait_ge(s_ctc, 2 * NCH)

            def onehot(w):
                return V.tensor_tensor(
                    oh[:, w.mod(2), :, :], at_window(dloc, w).unsqueeze(2).to_broadcast([P, K, P]),
                    iota_f[:, :].unsqueeze(1).to_broadcast([P, K, P]), ALU.is_equal)

            def normalised(link, dst_ap, src):
                return V.tensor_scalar(dst_ap, src, mv[:, 0:1], rstd[:, :], ALU.subtract, ALU.mult)

            def moments(link, src):
                link.held(V.bn_stats(stats[:, :], src))
                V.bn_aggr(mv[:, :], stats[:, :]).then_inc(s_var, 1)

            def z_high(w, b, x):
                return V.tensor_scalar(zp[b][:, bass.ds(w.v, 1), 0:D].rearrange("p a d -> p (a d)"), x, column(nout, w), None, ALU.mult)

            def z_low(w, b, x):
                V.scalar_tensor_tensor(zp[b][:, bass.ds(w.v, 1), D:D2].rearrange("p a d -> p (a d)"), x, column(nout, w),
                                       zp[b][:, bass.ds(w.v, 1), 0:D].rearrange("p a d -> p (a d)"), ALU.mult, ALU.subtract).then_inc(s_z, 1)

            L0_HEAD = 7

            def l0_end(f, at, link, rows_only=False):
                if at == 2:
                    dve.wait_ge(s_mm, f.v * 2 + 2)
                    link.later(V.tensor_tensor(yb[:, :], psB[:, D2:D2 + D], at_window(X, f), ALU.add))
                if at == 4:
                    link.due()
                    link.later(V.bn_stats(stats[:, :], yb[:, :]))
                if at == 5:
                    link.due_held()
                    V.bn_aggr(mv[:, :], stats[:, :]).then_inc(s_var, 1)
                if at == 10:
                    dve.wait_ge(s_std, f.v * 2 + 2)
                    link.later(V.reciprocal(rstd[:, :], std[:, :]))
                if at == 11:
                    link.due()
                    link.later(normalised(link, at_window(X, f), yb[:, :]))
                if at == 12:
                    link.due()
                    if rows_only:
                        dve.wait_ge(s_free, f.v + 1)
                        V.tensor_scalar(store[:, f.mod(2), 0:D], at_window(X, f), column(nout, f), None, ALU.mult).then_inc(s_store, 1)
                    else:
                        link.later(z_high(f, 0, at_window(X, f)))
                if at == 13 and not rows_only:
                    link.due()
                    z_low(f, 0, at_window(X, f))

            def l0_hidden(e, at, link):
                if at == 15:
                    dve.wait_ge(s_xw, e.v + 1)
                    link.later(V.scalar_tensor_tensor(hbuf, psA[:, 0:D2], column(inv_cnt, e), hneg, ALU.mult, ALU.add))
                if at == 17:
                    link.due()
                    link.later(V.bn_stats(stats[:, :], hbuf))
                if at == 18:
                    link.due_held()
                    V.bn_aggr(mv[:, :], stats[:, :]).then_inc(s_var, 1)
                if at == 22:
                    dve.wait_ge(s_std, e.v * 2 + 1)
                    link.later(V.reciprocal(rstd[:, :], std[:, :]))
                if at == 23:
                    link.due()
                    link.later(normalised(link, hbuf, hbuf))
                if at == 24:
                    link.due()
                    link.later(V.tensor_tensor(hbuf, hbuf, gamma, ALU.mult))
                if at == 25:
                    link.due()
                    link.later(V.tensor_tensor(hbuf, hbuf, beta, ALU.add))
                if at == 26:
                    link.due()
                    link.later(V.tensor_scalar(hneg, hbuf, 0.0, alpha[:, :], ALU.min, ALU.mult))
                if at == 27:
                    link.due()
                    V.scalar_tensor_tensor(hbuf, hbuf, 0.0, hneg, ALU.max, ALU.add).then_inc(s_h, 1)

            def l0(w, e, f, link):
                if w is not None:
                    dve.wait_ge(s_edge, w.v + 1)
                    onehot(w).then_inc(s_oh0, 1)
                    V.tensor_scalar(comb_cur[:, w.mod(2), :], comb_t[:, bass.ds(w.v * (WB * BT), WB * BT)], 0.0, None,
                                    ALU.add).then_inc(s_cols, 1)
                if f is not None:
                    link.start(f.v, L0_HEAD)
                for b in range(WB):
                    if w is not None and b % 8 == 0:
                        V.tensor_tensor(loh[:, b // 8, :, :],
                                        lo_t[:, bass.ds(w.v * (WB * BT) + b * BT, 8 * BT)].unsqueeze(1).to_broadcast([P, P, 8 * BT]),
                                        rep_a[:, :, :], ALU.is_equal).then_inc(s_coh, 1)
                        if b == 0:
                            dve.wait_ge(s_cols, w.v + 1)
                    if w is not None:
                        dve.wait_ge(s_blk, w.v * WB + b + 1)
                    for t in range(BT):
                        at = b * BT + t
                        if w is not None:
                            ins = V.tensor_scalar(coh[:, b % RING, t, :], iota_b[:, :],
                                                  comb_cur[:, w.mod(2), b * BT + t:b * BT + t + 1], None, ALU.is_equal)
                            if t == BT - 1:
                                ins.then_inc(s_coh, 1)
                        if f is not None:
                            l0_end(f, at, link)
                            if at == 13:
                                link.end()
                        if e is not None:
                            if at == 15:
                                link.start(e.v)
                            l0_hidden(e, at, link)

            def l1_end(w, link, stores):
                V.scalar_tensor_tensor(xs[:, :], at_window(X, w), 0.5, yb[:, :], ALU.mult, ALU.add).then_inc(s_h, 1)
                dve.wait_ge(s_mm, MM1 + w.v * 2 + 1)
                link(V.tensor_tensor(yb[:, :], psA[:, 0:D], at_window(X, w), ALU.add))
                moments(link, yb[:, :])
                dve.wait_ge(s_std, VAR1 + w.v + 1)
                link(V.reciprocal(rstd[:, :], std[:, :]))
                normalised(link, xs[:, :], yb[:, :]).then_inc(s_h, 1)
                link(normalised(link, at_window(X, w), yb[:, :]))
                dve.wait_ge(s_mm, MM1 + w.v * 2 + 2)
                link(V.tensor_tensor(at_window(Q, w), psA[:, 0:D], bqkv[:, 0:D], ALU.add))
                dve.wait_ge(s_free, w.v + stores * NW + 1)
                V.tensor_tensor(store[:, (stores * NW + w.rest) % 2, :], psA[:, D:3 * D], bqkv[:, D:3 * D], ALU.add).then_inc(s_store, 1)
                dve.wait_ge(s_store, w.v + stores * NW + 1)

            def l1_steps(s0):
                for step in range(L1_STEPS):
                    last = step == L1_STEPS - 1
                    n1 = 6 if last else 3
                    link = Chain(dve, s_dve, n1, s_spare, s0)

                    def l1(w, G, link=link, last=last, step=step):
                        link.start(w.v)
                        dve.wait_ge(s_fagg, G.v + 1 + 3)
                        p = acc[:, G.mod(2), :]
                        link(V.tensor_scalar(yb[:, :], p[:, 0:D], column(nin, w), None, ALU.mult))
                        V.scalar_tensor_tensor(yb[:, :], p[:, D:D2], column(nin, w), yb[:, :], ALU.mult, ALU.add).then_inc(s_facc, 1)
                        dve.wait_ge(s_facc, G.v + 1 + CREDIT)
                        if not last:
                            link(V.scalar_tensor_tensor(xs[:, :], at_window(X, w), 0.5, yb[:, :], ALU.mult, ALU.add))
                            link(z_high(w, 1 - step % 2, xs[:, :]))
                            z_low(w, 1 - step % 2, xs[:, :])
                            link.end()
                            return
                        l1_end(w, link, 0)
                        link.end()
                    windows(dve, step, l1, 6)
                    s0 += n1 * NW
                return s0

            def l2(w, e, link, ahead):
                if e is not None:
                    link.start(e.v)
                p = acc[:, e.mod(2), :] if e is not None else None
                if w is not None:
                    kv = rows[:, w.mod(2), :].rearrange("p (k n) -> p k n", n=D2)
                    dve.wait_ge(s_qec, (w.v + 1) * NG)
                    dve.wait_ge(s_gat[w.mod(2)], (w.div(2) + 1) * 16 * K)
                    V.tensor_tensor(kv[:, :, 0:D], kv[:, :, 0:D], qe[:, :, :], ALU.mult).then_inc(s_prod, 1)
                    dve.wait_ge(s_prod, w.v + 1)
                    V.tensor_reduce(sc[:, :, :], kv[:, :, 0:D].rearrange("p k (h d) -> p k h d", d=HD), AXX, ALU.add).then_inc(s_raw, 1)
                    dve.wait_ge(s_raw, w.v + 1)
                    lim = 5.0 * HD ** 0.5
                    V.tensor_scalar(sc[:, :, :], sc[:, :, :], lim, -lim, ALU.min, ALU.max).then_inc(s_sc, 1)
                if e is not None:
                    dve.wait_ge(s_agg, e.v + 1 + CREDIT)
                    l2_norm(e, link, p[:, 0:H], p[:, H:H + D])
                if w is not None:
                    dve.wait_ge(s_exp, w.v + 1)
                    for a, b in ((0, K // 2), (K // 2, K)):
                        v = kv[:, a:b, D:D2].rearrange("p k (h d) -> p k h d", d=HD)
                        s = kv[:, a:b, D - H:D].unsqueeze(3).to_broadcast([P, b - a, H, HD])
                        V.tensor_tensor(v, v, s, ALU.mult).then_inc(s_msg, 1)
                if e is not None:
                    l2_rows(e, link)
                if ahead:
                    dve.wait_ge(s_agg, w.v + 1 + CREDIT)
                    onehot(w.plus(2)).then_inc(s_oh, 1)
                if e is not None:
                    l2_y(e, link)
                    parts = [yp[:, bass.ds(e.v, 1), i * D:(i + 1) * D].rearrange("p a d -> p (a d)") for i in range(3)]
                    V.tensor_copy(parts[0], yb[:, :]).then_inc(s_yp, 1)
                    dve.wait_ge(s_yp, e.v * 3 + 1)
                    V.tensor_tensor(yc[:, :], yb[:, :], parts[0], ALU.subtract).then_inc(s_yp, 1)
                    dve.wait_ge(s_yp, e.v * 3 + 2)
                    V.tensor_copy(parts[1], yc[:, :]).then_inc(s_yp, 1)
                    dve.wait_ge(s_yp, e.v * 3 + 3)
                    V.tensor_tensor(parts[2], yc[:, :], parts[1], ALU.subtract).then_inc(s_z, 1)
                    dve.wait_ge(s_z, 3 * NW + e.v + 1)
                    link.end()

            def l2_norm(w, link, z_sum, v_sum):
                link(V.tensor_scalar(zr[:, :], z_sum, 1e-6, None, ALU.add))
                link(V.reciprocal(zr[:, :], zr[:, :]))
                link(V.tensor_tensor(yb[:, :].rearrange("p (h d) -> p h d", d=HD),
                                     v_sum.rearrange("p (h d) -> p h d", d=HD),
                                     zr[:, :].unsqueeze(2).to_broadcast([P, H, HD]), ALU.mult))
                link(V.tensor_tensor(yb[:, :], yb[:, :], at_window(X, w), ALU.add))
                moments(link, yb[:, :])

            def l2_rows(w, link):
                dve.wait_ge(s_std, VAR2 + w.v + 1)
                link(V.reciprocal(rstd[:, :], std[:, :]))
                normalised(link, xs[:, :], yb[:, :]).then_inc(s_h, 1)
                V.tensor_scalar(yc[:, :], l3_v[:, :], column(indeg, w), None, ALU.mult).then_inc(s_h2, 1)
                link(normalised(link, at_window(X, w), yb[:, :]))

            def l2_y(w, link):
                dve.wait_ge(s_mm, MM2 + w.v + 1)
                dve.wait_ge(s_h2, w.v + 1)
                link(V.tensor_tensor(yb[:, :], psB[:, 0:D], yc[:, :], ALU.add))

            def l3_norm(w, link, stores):
                V.tensor_scalar(xs[:, :], yb[:, :], 0.0, None, ALU.max).then_inc(s_h, 1)
                dve.wait_ge(s_mm, MM3 + w.v + 1)
                link(V.tensor_tensor(yb[:, :], psA[:, 0:D], l3_b2[:, :], ALU.add))
                link(V.tensor_tensor(yb[:, :], yb[:, :], at_window(X, w), ALU.add))
                moments(link, yb[:, :])
                dve.wait_ge(s_std, VAR3 + w.v + 1)
                link(V.reciprocal(rstd[:, :], std[:, :]))
                dve.wait_ge(s_free, stores * NW + w.v + 1)
                normalised(link, store[:, (stores * NW + w.rest) % 2, 0:D], yb[:, :]).then_inc(s_store, 1)
                dve.wait_ge(s_store, stores * NW + w.v + 1)

            def l3(w, G, link):
                link.start(w.v)
                dve.wait_ge(s_fagg, G.v + 1 + 3)
                p = acc[:, G.mod(2), :]
                link(V.tensor_tensor(yb[:, :], p[:, 2 * D:3 * D], l3_b1[:, :], ALU.add))
                link(V.tensor_tensor(yb[:, :], p[:, D:2 * D], yb[:, :], ALU.add))
                V.tensor_tensor(yb[:, :], p[:, 0:D], yb[:, :], ALU.add).then_inc(s_facc, 1)
                dve.wait_ge(s_facc, G.v + 1 + CREDIT)
                l3_norm(w, link, 1)
                link.end()

            def usual_case():
                dve.wait_ge(s_win, 2 * 16 * NW)
                setup(V.tensor_tensor(dloc[:, :, :], dst_all[:, :, :], wbase[:, :].unsqueeze(2).to_broadcast([P, NW, K]), ALU.subtract))
                assert setup.j == REP_FREE, setup.j
                dve.wait_ge(s_rep, 3)
                n0, n2, n3 = 12, 8, 6
                link0 = Chain(dve, s_dve, n0, s_spare)
                skewed_twice(dve, lambda w, e, f: l0(w, e, f, link0))
                s0 = l1_steps(n0 * NW)
                for w in (0, 1):
                    onehot(W(0, w, 0)).then_inc(s_oh, 1)
                link2 = Chain(dve, s_dve, n2, s_spare, s0)
                skewed_ahead(dve, lambda w, e, ahead: l2(w, e, link2, ahead >= 2))
                link3 = Chain(dve, s_dve, n3, s_spare, s0 + n2 * NW)
                windows(dve, L1_STEPS, lambda w, G: l3(w, G, link3), 6)

            def round_table(link):
                dve.wait_ge(g_const, 3)
                link(V.tensor_scalar(need[0:NW, 0:RW], need[0:NW, 0:RW], tot[:, 0:1], None, ALU.is_lt))
                link(V.tensor_reduce(need[0:NW, RW:RW + 1], need[0:NW, 0:RW], AXX, ALU.add))
                link(V.tensor_copy(spread[0:NW, 0, :], tot[:, 0:1].to_broadcast([NW, P])))
                V.tensor_copy(spread[0:NW, 1, :], need[0:NW, RW:RW + 1].to_broadcast([NW, P])).then_inc(g_ready, 1)
                dve.wait_ge(g_sum, 1)
                link(V.tensor_copy(used_g[:, :], psB[:, 64:64 + NW]))
                link(V.scalar_tensor_tensor(first_g[:, :], used_g[:, :], -float(CHUNK), psB[:, 0:NW], ALU.mult, ALU.add))
                link(V.tensor_copy(step_g[:, 0:1], first_g[:, 0:1]))
                link(V.tensor_tensor(step_g[:, 1:NW], first_g[:, 1:NW], first_g[:, 0:NW - 1], ALU.subtract))
                link(V.tensor_tensor(prior[:, :, :], used_g[:, :].unsqueeze(1).to_broadcast([P, R, NW]),
                                     order[:, :].unsqueeze(2).to_broadcast([P, R, NW]), ALU.is_le))
                link(V.tensor_reduce(win_g[:, :], prior[:, :, :], AXX, ALU.add))
                link(V.tensor_scalar(win_g[:, :], win_g[:, :], -1.0, None, ALU.add))
                link(V.tensor_tensor(prior[:, :, :], prior[:, :, :], step_g[:, :].unsqueeze(1).to_broadcast([P, R, NW]), ALU.mult))
                link(V.tensor_reduce(start_g[:, :], prior[:, :, :], AXX, ALU.add))
                link(V.scalar_tensor_tensor(start_g[:, :], order[:, :], float(CHUNK), start_g[:, :], ALU.mult, ALU.add))
                link(V.tensor_scalar(base_g[:, :], start_g[:, :], float(E - CHUNK), None, ALU.min))
                link(V.tensor_copy(base_i[:, :], base_g[:, :]))
                V.tensor_copy(win_i[:, :], win_g[:, :]).then_inc(g_tab, 1)
                dve.wait_ge(g_tab, 1)
                dve.wait_ge(g_win, 2 * 16 * R)
                link(V.tensor_scalar(win_g[:, :], win_g[:, :], float(P), None, ALU.mult))
                link(V.tensor_tensor(dloc_g[:, :, :], dst_g[:, :, :], win_g[:, :].unsqueeze(2).to_broadcast([P, R, K]), ALU.subtract))
                link(V.tensor_tensor(start_g[:, :], start_g[:, :], base_g[:, :], ALU.subtract))
                link(V.tensor_copy(at_round[:, :, :], place[:, :].unsqueeze(1).to_broadcast([P, R, K])))
                link(V.tensor_tensor(late[:, :, :], at_round[:, :, :], start_g[:, :].unsqueeze(2).to_broadcast([P, R, K]), ALU.is_lt))
                link(V.tensor_scalar(late[:, :, :], late[:, :, :], FAR * P, None, ALU.mult))
                link(V.tensor_tensor(dloc_g[:, :, :], dloc_g[:, :, :], late[:, :, :], ALU.add))

            def window_of(r):
                return dve.value_load(win_i[0:1, bass.ds(r, 1)], min_val=0, max_val=NW - 1)

            def sum_rounds(phase, sums, s0):
                link = Chain(dve, g_dve, 1, s_spare, s0)
                V.memset(sums[:, :, :], 0.0).then_inc(g_oh, 1)
                dve.wait_ge(g_oh, phase * (R + 1) + 1)

                def one(r):
                    link.start(r)
                    dve.wait_ge(g_used, phase * R + 1 + r)
                    link(V.tensor_scalar(idx_cur[:, 0, :], of_round(src_g, r), 0.0, None, ALU.add))
                    V.tensor_tensor(oh_g[:, :, :], of_round(dloc_g, r).unsqueeze(2).to_broadcast([P, K, P]),
                                    iota_f[:, :].unsqueeze(1).to_broadcast([P, K, P]), ALU.is_equal).then_inc(g_oh, 1)
                    dve.wait_ge(g_agg, phase * R + 1 + r)
                    v = window_of(r)
                    t = sums[:, bass.ds(v, 1), :].rearrange("p a d -> p (a d)")
                    V.tensor_tensor(t, acc[:, 0, 0:D], t, ALU.add).then_inc(g_used, 1)
                    link.end()
                rounds(dve, one)
                return s0 + R

            def attend_rounds(phase, s0):
                link = Chain(dve, g_dve, 4, s_spare, s0)
                V.memset(sum_g[:, :, :], 0.0).then_inc(s_spare, 1)
                V.memset(z_g[:, :, :], 0.0).then_inc(g_oh, 1)
                dve.wait_ge(g_oh, phase * (R + 1) + 1)
                kv = rows_g[:, :].rearrange("p (k n) -> p k n", n=D2)

                def one(r):
                    link.start(r)
                    dve.wait_ge(g_used, phase * R + 1 + r)
                    v = window_of(r)
                    link(V.tensor_scalar(idx_cur[:, 0, :], of_round(src_g, r), 0.0, None, ALU.add))
                    link(V.tensor_scalar(q_g, Q[:, bass.ds(v, 1), :].rearrange("p a d -> p (a d)"), 0.0, None, ALU.add))
                    V.tensor_tensor(oh_g[:, :, :], of_round(dloc_g, r).unsqueeze(2).to_broadcast([P, K, P]),
                                    iota_f[:, :].unsqueeze(1).to_broadcast([P, K, P]), ALU.is_equal).then_inc(g_oh, 1)
                    dve.wait_ge(g_qec, (r + 1) * NG)
                    dve.wait_ge(g_gat[phase - 1], (r + 1) * 16 * K)
                    link(V.tensor_tensor(kv[:, :, 0:D], kv[:, :, 0:D], qe[:, :, :], ALU.mult))
                    link(V.tensor_reduce(sc[:, :, :], kv[:, :, 0:D].rearrange("p k (h d) -> p k h d", d=HD), AXX, ALU.add))
                    lim = 5.0 * HD ** 0.5
                    V.tensor_scalar(sc[:, :, :], sc[:, :, :], lim, -lim, ALU.min, ALU.max).then_inc(g_sc, 1)
                    dve.wait_ge(g_exp, r + 1)
                    m = kv[:, :, D:D2].rearrange("p k (h d) -> p k h d", d=HD)
                    V.tensor_tensor(m, m, kv[:, :, D - H:D].unsqueeze(3).to_broadcast([P, K, H, HD]), ALU.mult).then_inc(g_msg, 1)
                    dve.wait_ge(g_agg, phase * R + 1 + r)
                    tz = z_g[:, bass.ds(v, 1), :].rearrange("p a d -> p (a d)")
                    tv = sum_g[:, bass.ds(v, 1), :].rearrange("p a d -> p (a d)")
                    V.tensor_tensor(tz, acc[:, 0, 0:H], tz, ALU.add).then_inc(s_spare, 1)
                    V.tensor_tensor(tv, acc[:, 0, H:H + D], tv, ALU.add).then_inc(g_used, 1)
                    link.end()
                rounds(dve, one)
                return s0 + 4 * R

            def any_case():
                table = Chain(dve, g_dve, 23)
                table.start(0)
                table(V.memset(store[:, :, :], 0.0))
                round_table(table)
                table.end()
                dve.sem_inc(g_used, 1)
                g0 = sum_rounds(0, ST, 23)
                dve.wait_ge(g_used, R + 1)
                n0 = 11
                link0 = Chain(dve, s_dve, n0, s_spare)

                def l0_window(w, G):
                    link0.start(w.v)
                    for at in range(WB * BT):
                        l0_hidden(w, at, link0)
                    for at in range(WB * BT):
                        l0_end(w, at, link0, rows_only=True)
                    dve.wait_ge(s_store, w.v + 1)
                    link0.end()
                windows(dve, 0, l0_window)
                s0 = n0 * NW
                for step in range(L1_STEPS):
                    g0 = sum_rounds(step + 1, sum_g, g0)
                    dve.wait_ge(g_used, (step + 2) * R + 1)
                    n1 = 7 if step == L1_STEPS - 1 else 2
                    link1 = Chain(dve, s_dve, n1, s_spare, s0)

                    def l1(w, G, step=step, link=link1):
                        link.start(w.v)
                        link(V.tensor_scalar(yb[:, :], at_window(sum_g, w), column(nin, w), None, ALU.mult))
                        if step == L1_STEPS - 1:
                            link(V.tensor_copy(zr[:, 0:1], rstd[:, :]))
                            l1_end(w, link, L1_STEPS)
                        else:
                            link(V.scalar_tensor_tensor(xs[:, :], at_window(X, w), 0.5, yb[:, :], ALU.mult, ALU.add))
                            stores = (step + 1) * NW
                            dve.wait_ge(s_free, stores + w.v + 1)
                            V.tensor_scalar(store[:, (stores + w.rest) % 2, 0:D], xs[:, :], column(nout, w), None, ALU.mult).then_inc(s_store, 1)
                            dve.wait_ge(s_store, stores + w.v + 1)
                        link.end()
                    windows(dve, 0, l1)
                    s0 += n1 * NW
                g0 = attend_rounds(L1_STEPS + 1, g0)
                dve.wait_ge(g_used, (L1_STEPS + 2) * R + 1)
                n2 = 8
                link2 = Chain(dve, s_dve, n2, s_spare, s0)

                def l2_end(w, G):
                    stores = (L1_STEPS + 1) * NW
                    link2.start(w.v)
                    l2_norm(w, link2, at_window(z_g, w), at_window(sum_g, w))
                    l2_rows(w, link2)
                    l2_y(w, link2)
                    V.tensor_scalar(at_window(Q, w), yb[:, :], 0.0, None, ALU.add).then_inc(s_yp, 1)
                    dve.wait_ge(s_free, stores + w.v + 1)
                    V.tensor_scalar(store[:, (stores + w.rest) % 2, 0:D], yb[:, :], 0.0, None, ALU.add).then_inc(s_store, 1)
                    dve.wait_ge(s_yp, w.v + 1)
                    dve.wait_ge(s_store, stores + w.v + 1)
                    link2.end()
                windows(dve, 0, l2_end)
                s0 += n2 * NW
                g0 = sum_rounds(L1_STEPS + 2, sum_g, g0)
                dve.wait_ge(g_used, (L1_STEPS + 3) * R + 1)
                n3 = 6
                link3 = Chain(dve, s_dve, n3, s_spare, s0)

                def l3_end(w, G):
                    link3.start(w.v)
                    link3(V.tensor_tensor(yb[:, :], at_window(sum_g, w), l3_b1[:, :], ALU.add))
                    link3(V.tensor_tensor(yb[:, :], at_window(Q, w), yb[:, :], ALU.add))
                    l3_norm(w, link3, L1_STEPS + 2)
                    link3.end()
                windows(dve, 0, l3_end)
            n = too_long(dve)
            with dve.If(n == 0):
                usual_case()
            with dve.Else():
                any_case()
            dve.sem_inc(s_spare, 1)

        @block.tensor
        def _(pe):
            mm = nc.tensor.matmul
            turn = nc.tensor.transpose
            pe.sem_inc(s_edge, CREDIT)
            pe.sem_inc(s_blk, RING)
            pe.sem_inc(s_agg, CREDIT)
            pe.sem_inc(s_fagg, 3)

            def histogram(i):
                at = i * 64
                h0 = i * HSTEPS

                def step(t, n, first=False, last=False):
                    par = t % 2
                    pe.wait_ge(s_hoh, n)
                    for j in range(HJ):
                        m = mm(psA[:, at:at + NW], hlo[0:EP, par, :, j], hhi[0:EP, par, :, j],
                               start=(first and j == 0), stop=(last and j == HJ - 1), skip_group_check=True)
                    m.then_inc(s_hmm, 1)
                step(h0, 2 * h0 + 2, first=True)
                with pe.Fori(0, (HSTEPS - 3) // 2) as j:
                    for t in (1, 2):
                        step(h0 + t, j * 4 + 2 * (h0 + t) + 2)
                for t in (HSTEPS - 2, HSTEPS - 1):
                    step(h0 + t, 2 * (h0 + t) + 2, last=(t == HSTEPS - 1))
            pe.wait_ge(s_const, N_CONST)
            histogram(0)
            pe.wait_ge(s_ind, 1)
            mm(psB[0:NW, 0:WB], indeg[:, :], ones[:, :], start=True, stop=True).then_inc(s_tot, 1)
            pe.wait_ge(s_in, 16 * len(LOADS))
            for j in range(4):
                turn(acc[:, 0, j * P:(j + 1) * P], wraw[:, j, :], ident[:, :])
            turn(acc[:, 1, 0:P], wraw[:, 4, :], ident[:, :]).then_inc(s_wT, 1)
            pe.wait_ge(s_totc, 1)
            mm(psB[0:WB, 64:64 + NW], tri[:, :], indeg[:, :], start=True, stop=False)
            mm(psB[0:WB, 64:64 + NW], tot[:, :], upper[:, :], start=False, stop=True).then_inc(s_off, 1)
            pe.wait_ge(s_over, 1)
            mm(psB[0:1, 160:161], over[:, NCH:NCH + 1], ones[:, 0:1], start=True, stop=False)
            mm(psB[0:1, 160:161], over[:, NCH + 1:NCH + 2], ones[:, 0:1], start=False, stop=True).then_inc(s_nover, 1)
            histogram(1)
            for c in range(NCH):
                pe.wait_ge(s_comb, c + 1)
                if c >= 2:
                    pe.wait_ge(s_ctc, 2 * (c - 1))
                for t in range(BT):
                    turn(pair[c % 2][:, 0, t * CB:(t + 1) * CB], comb_f[:, c, t * P:(t + 1) * P], ident[0:CB, 0:CB])
                for t in range(BT):
                    m = turn(pair[c % 2][:, 1, t * CB:(t + 1) * CB], lo_f[:, c, t * P:(t + 1) * P], ident[0:CB, 0:CB])
                m.then_inc(s_ct, 1)
            pe.wait_ge(s_be, 1)
            pe.wait_ge(s_wc, 2)
            mm(psA[:, 0:D], wT[:, 4, :], l3_w1b[:, :], start=True, stop=True)
            mm(psA[:, D:2 * D], be_bc[:, :], l3_w1b[:, :], start=True, stop=True).then_inc(s_fold, 1)
            pe.wait_ge(s_foldc, 2)
            pe.wait_ge(s_ctc, 2 * NCH)

            def l0_turn(h, x):
                if h is not None:
                    pe.wait_ge(s_h, h.v + 1)
                    turn(psB[:, 0:P], hbuf[:, 0:P], ident[:, :]).then_inc(s_tp, 1)
                    turn(psB[:, P:2 * P], hbuf[:, P:2 * P], ident[:, :]).then_inc(s_tp, 1)
                if x is not None:
                    pe.wait_ge(s_xs, x.v + 1)
                    turn(psB[:, D2 + D:2 * D2], xs[:, :], ident[:, :]).then_inc(s_tp, 1)

            def l0_out(h, copies):
                pe.wait_ge(s_tc, h.v * 4 + copies)
                mm(psB[:, D2:D2 + D], hT[:, 0, :], w2a, start=True, stop=False)
                mm(psB[:, D2:D2 + D], hT[:, 1, :], w2b, start=False, stop=False)
                mm(psB[:, D2:D2 + D], ones_row[:, :], b2[0:1, :], start=False, stop=True).then_inc(s_mm, 1)

            def l0_features(w, a, b):
                for k in range(a, b):
                    m = mm(acc[:, w.mod(2), 0:P], ea[:, w.mod(2), k, :], oh[:, w.mod(2), k, :], start=(k == 0), stop=(k == K - 1))
                if b == K:
                    m.then_inc(s_edge, 1)

            def l0(w, e):
                for b in range(WB):
                    if w is not None and b == WB // 2:
                        pe.wait_ge(s_oh0, w.v + 1)
                        pe.wait_ge(s_ea[w.mod(2)], (w.div(2) + 1) * 16)
                        l0_features(w, 0, KM)
                    if w is not None:
                        if b % 2 == 0:
                            pe.wait_ge(s_evac, w.v * (WB // 2) + b // 2 + 1)
                        pe.wait_ge(s_coh, w.v * (WB + 2) + b + 1 + (b // 8 + 1))
                        for t in range(BT):
                            m = mm(pair[(b // 2) % 2][:, b % 2, 0:BW], loh[:, b // 8, :, (b % 8) * BT + t], coh[:, b % RING, t, :],
                                   start=(t == 0), stop=(t == BT - 1))
                        m.then_inc(s_blk, 1)
                    if e is not None and b == 1:
                        pe.wait_ge(s_tc, e.v * 4 + 3)
                        mm(psA[:, D2:2 * D2], xT[:, :], w1a, start=True, stop=False)
                        mm(psA[:, D2:2 * D2], ones_row[:, :], b1[0:1, :], start=False, stop=True)
                        mm(psA[:, 0:D2], sT[:, :], w1b, start=True, stop=True).then_inc(s_mm, 1)
                l0_turn(e, w)
                if w is None:
                    l0_out(e, 4)
                    return
                l0_features(w, KM, K - 4)
                if e is not None:
                    l0_out(e, 5)
                l0_features(w, K - 4, K)

            def propagate(phase, z, width, pieces):
                def step(w, e):
                    if w is not None:
                        G = w.plus(phase * NW)
                        pe.wait_ge(s_facc, G.v + 1)
                        pe.wait_ge(s_a[G.mod(3)], (G.div(3) + 1) * 16)
                        if phase == L1_STEPS:
                            mm(acc[:, G.mod(2), 0:width], ident16[:, :], z[:, bass.ds(w.v, 1), :].rearrange("p a d -> p (a d)"),
                               start=True, stop=False)
                    for s in range(NW):
                        if w is not None:
                            m = mm(acc[:, G.mod(2), 0:width], aslot[:, G.mod(3), s, :], z[:, s, :],
                                   start=(s == 0 and phase < L1_STEPS), stop=(s == NW - 1))
                        if e is not None and s in pieces:
                            pieces[s](e)
                    if w is not None:
                        m.then_inc(s_fagg, 1)
                pe.wait_ge(s_z, (phase + 1) * NW)
                skewed(pe, step, 6)

            def l1_turn(e):
                pe.wait_ge(s_h, H1 + e.v * 2 + 1)
                turn(psB[:, 0:P], xs[:, :], ident[:, :]).then_inc(s_tp, 1)

            def l1_out(e):
                pe.wait_ge(s_tc, TC1 + e.v * 2 + 1)
                mm(psA[:, 0:D], xT[:, :], wT[:, 0, :], start=True, stop=True).then_inc(s_mm, 1)

            def l1_turn_x(e):
                pe.wait_ge(s_h, H1 + e.v * 2 + 2)
                turn(psB[:, 0:P], xs[:, :], ident[:, :]).then_inc(s_tp, 1)

            def l1_qkv(e):
                pe.wait_ge(s_tc, TC1 + e.v * 2 + 2)
                mm(psA[:, 0:3 * D], xT[:, :], wT[:, 1:4, :].rearrange("p a d -> p (a d)"), start=True, stop=True).then_inc(s_mm, 1)


            def expand(w):
                q_w = at_window(Q, w)
                pe.wait_ge(s_oh, w.v + 1)

                def turn_group(g):
                    a, b = GROUPS[g]
                    for k in range(a, b):
                        m = turn(pair[0][:, g % 2, (k - a) * P:(k - a + 1) * P], oh[:, w.mod(2), k, :], ident[:, :])
                    m.then_inc(s_qT, 1)
                turn_group(0)
                for g, (a, b) in enumerate(GROUPS):
                    if g + 1 < NG:
                        turn_group(g + 1)
                    pe.wait_ge(s_qTc, w.v * NG + g + 1)
                    for k in range(a, b):
                        m = mm(pair[1][:, g % 2, (k - a) * D:(k - a + 1) * D], ohT[:, g % 2, k - a, :], q_w, start=True, stop=True)
                    m.then_inc(s_qe, 1)
            def l2(w, e, ahead):
                if w is not None:
                    if ahead:
                        expand(w.plus(1))
                    pe.wait_ge(s_msg, w.v * 2 + 1)
                    for k in range(K):
                        if k == K // 2:
                            pe.wait_ge(s_msg, w.v * 2 + 2)
                        r = rows[:, w.mod(2), k * D2 + D - H:(k + 1) * D2]
                        m = mm(acc[:, w.mod(2), 0:D + H], oh[:, w.mod(2), k, :], r, start=(k == 0), stop=(k == K - 1))
                    m.then_inc(s_agg, 1)
                if e is not None:
                    l2_end(e, e)

            def l2_end(w, G):
                pe.wait_ge(s_h, H2 + w.v + 1)
                turn(psA[:, 0:P], xs[:, :], ident[:, :]).then_inc(s_tp, 1)
                pe.wait_ge(s_tc, TC2 + w.v * 2 + 2)
                mm(psB[:, 0:D], xT[:, :], l3_w1a[:, :], start=True, stop=False)
                mm(psB[:, 0:D], sT[:, :], l3_m[:, :], start=False, stop=True).then_inc(s_mm, 1)
            def l3_turn(e):
                pe.wait_ge(s_h, H3 + e.v + 1)
                turn(psB[:, 0:P], xs[:, :], ident[:, :]).then_inc(s_tp, 1)

            def l3_out(e):
                pe.wait_ge(s_tc, TC3 + e.v + 1)
                mm(psA[:, 0:D], xT[:, :], l3_w2[:, :], start=True, stop=True).then_inc(s_mm, 1)

            def usual_case():
                pe.sem_inc(s_evac, CREDIT)
                pe.sem_inc(s_facc, CREDIT)
                skewed(pe, l0, 2)
                propagate(0, zp[0], D2, {})
                propagate(1, zp[1], D2, {})
                propagate(2, zp[0], D2, {14: l1_turn, 18: l1_out, 37: l1_turn_x, 41: l1_qkv})
                expand(W(0, 0, 0))
                skewed_ahead(pe, l2)
                propagate(L1_STEPS, yp, 3 * D, {14: l3_turn, 24: l3_out})

            def sum_rounds(phase):
                def one(r):
                    pe.wait_ge(g_oh, phase * (R + 1) + 2 + r)
                    if phase == 0:
                        pe.wait_ge(g_ea, (r + 1) * 16)
                    else:
                        pe.wait_ge(g_gat[phase - 1], (r + 1) * 16 * K)
                    for k in range(K):
                        if phase == 0:
                            m = mm(acc[:, 0, 0:P], rows_g[:, k * D:(k + 1) * D], oh_g[:, k, :], start=(k == 0), stop=(k == K - 1))
                        else:
                            m = mm(acc[:, 0, 0:D], oh_g[:, k, :], rows_g[:, k * D2:k * D2 + D], start=(k == 0), stop=(k == K - 1))
                    m.then_inc(g_agg, 1)
                rounds(pe, one)

            def attend_rounds(phase):
                def one(r):
                    pe.wait_ge(g_oh, phase * (R + 1) + 2 + r)
                    for g, (a, b) in enumerate(GROUPS):
                        for k in range(a, b):
                            m = turn(pair[0][:, 0, (k - a) * P:(k - a + 1) * P], oh_g[:, k, :], ident[:, :])
                        m.then_inc(g_qT, 1)
                        pe.wait_ge(g_qTc, r * NG + g + 1)
                        for k in range(a, b):
                            m = mm(pair[1][:, 0, (k - a) * D:(k - a + 1) * D], ohT[:, 0, k - a, :], q_g, start=True, stop=True)
                        m.then_inc(g_qe, 1)
                        pe.wait_ge(g_qec, r * NG + g + 1)
                    pe.wait_ge(g_msg, r + 1)
                    for k in range(K):
                        m = mm(acc[:, 0, 0:D + H], oh_g[:, k, :], rows_g[:, k * D2 + D - H:(k + 1) * D2], start=(k == 0), stop=(k == K - 1))
                    m.then_inc(g_agg, 1)
                rounds(pe, one)

            def any_case():
                pe.wait_ge(g_ready, 1)
                mm(psB[:, 0:NW], spread[0:NW, 0, :], upper[:, :], start=True, stop=True)
                mm(psB[:, 64:64 + NW], spread[0:NW, 1, :], upper[:, :], start=True, stop=True).then_inc(g_sum, 1)
                sum_rounds(0)

                def l0_window(w, G):
                    l0_turn(None, w)
                    l0(None, w)
                windows(pe, 0, l0_window)
                for phase in range(1, L1_STEPS + 1):
                    sum_rounds(phase)

                def l1_end(w, G):
                    for piece in (l1_turn, l1_out, l1_turn_x, l1_qkv):
                        piece(w)

                def l3_end(w, G):
                    l3_turn(w)
                    l3_out(w)
                windows(pe, 0, l1_end)
                attend_rounds(L1_STEPS + 1)
                windows(pe, 0, l2_end)
                sum_rounds(L1_STEPS + 2)
                windows(pe, 0, l3_end)
            n = too_long(pe)
            with pe.If(n == 0):
                usual_case()
            with pe.Else():
                any_case()
            pe.sem_inc(s_spare, 1)


_INS = ['x', 'src', 'dst', 'edge_attr_128', 'L0_gnn_W1', 'L0_gnn_b1', 'L0_gnn_gamma', 'L0_gnn_beta', 'L0_gnn_prelu_a',
        'L0_gnn_W2', 'L0_gnn_b2', 'L1_gnn_W', 'L2_gnn_Wq', 'L2_gnn_bq', 'L2_gnn_Wk', 'L2_gnn_bk', 'L2_gnn_Wv', 'L2_gnn_bv',
        'L3_gnn_We', 'L3_gnn_be', 'L3_gnn_W1', 'L3_gnn_b1', 'L3_gnn_W2', 'L3_gnn_b2']


def kernel(**inputs):
    import numpy as _np
    import concourse.bacc as _bacc
    from concourse import mybir as _mybir
    from concourse.bass_utils import run_bass_kernel_spmd as _run

    nc = _bacc.Bacc("TRN2", target_bir_lowering=False, num_devices=1)
    arrays, args = {}, {}
    for name in _INS:
        a = _np.ascontiguousarray(inputs[name])
        arrays[f"in_{name}"] = a
        args[name] = nc.dram_tensor(f"in_{name}", a.shape, _mybir.dt.from_np(a.dtype), kind="ExternalInput").ap()
    out = nc.dram_tensor("out_0", (N, D), _mybir.dt.float32, kind="ExternalOutput").ap()
    build(nc, args, out)
    return _run(nc, [arrays], core_ids=[0]).results[0]["out_0"]
```
